# Optimizing a Trainium2 kernel written in Bass

```python
import numpy as np
import jax
import jax.numpy as jnp

def _softmax(x, axis=-1):
    return jax.nn.softmax(x, axis=axis)

def _gelu(x):
    return jax.nn.gelu(x, approximate=True)

def _silu(x):
    return jax.nn.silu(x)

def _sigmoid(x):
    return jax.nn.sigmoid(x)

def _layernorm(x, axis=-1, eps=1e-05):
    m = jnp.mean(x, axis=axis, keepdims=True)
    v = jnp.var(x, axis=axis, keepdims=True)
    return (x - m) / jnp.sqrt(v + eps)

def _scatter_add(tgt, idx, src, axis=0):
    return tgt.at[idx].add(src)

def _segment_sum(src, seg, n):
    return jax.ops.segment_sum(src, seg, n)
kernel_name = 'mk_perceiver_d2_seqx_r2_defa21'

def setup_inputs(seed: int=0):
    np.random.seed(seed)
    _w = jnp.asarray

    def _rec_inputs():
        import jax
        import jax.numpy as jnp
        _rk = jax.random.key(seed)
        x = -0.0002928 + 1 * jax.random.normal(jax.random.fold_in(_rk, 1), (8, 64, 512), jnp.float32)
        _lenS = 64 - jax.random.randint(jax.random.fold_in(_rk, 7), (8,), 0, max(1, 64 // 4) + 1, jnp.int32)
        _lenS2 = 1601 - jax.random.randint(jax.random.fold_in(_rk, 8), (8,), 0, max(1, 1601 // 4) + 1, jnp.int32)
        _ctx_1024P = jax.random.normal(jax.random.fold_in(_rk, 11), (8, 16, 512), jnp.float32)
        _ctx_1024c = jax.random.dirichlet(jax.random.fold_in(_rk, 511), 0.3 * jnp.ones((16,), jnp.float32), (8, 1601))
        _ctx_1024t = jnp.einsum('bsk,bkd->bsd', _ctx_1024c, _ctx_1024P)
        _ctx_1024t = _ctx_1024t * jax.lax.rsqrt(jnp.mean(jnp.square(_ctx_1024t)) + 1e-12) * 0.953939
        ctx_1024 = 4.13588e-05 + 0.999923 * (_ctx_1024t + 0.3 * jax.random.normal(jax.random.fold_in(_rk, 611), (8, 1601, 512), jnp.float32))
        itok_BxS_8_8191 = jax.random.randint(jax.random.fold_in(_rk, 12), (8, 64), 8, 4096, jnp.int32)
        itok_BxS2_1_8191 = jax.random.randint(jax.random.fold_in(_rk, 13), (8, 1601), 1, 4096, jnp.int32)
        _validS = jnp.arange(64)[None, :] < _lenS[:, None]
        _validS2 = jnp.arange(1601)[None, :] < _lenS2[:, None]
        _causal = jnp.tril(jnp.ones((64, 64), dtype=bool))
        mask_BxSxS2_if1 = jnp.where(jnp.ones((8, 64, 1601), dtype=bool), 1, 0).astype(jnp.int32)
        return (x, ctx_1024, itok_BxS_8_8191, itok_BxS2_1_8191, mask_BxSxS2_if1)
    x, ctx_1024, itok_BxS_8_8191, itok_BxS2_1_8191, mask_BxSxS2_if1 = _rec_inputs()

    def _L0_xattn_setup():
        import jax, jax.numpy as jnp
        import numpy as np
        DIM = 512
        NUM_HEADS = 16
        HEAD_DIM = DIM // NUM_HEADS

        def _slopes(num_heads):
            ratio = 2.0 ** (-8.0 / num_heads)
            return jnp.asarray([ratio ** i for i in range(1, num_heads + 1)], dtype=jnp.float32)
        key = jax.random.key(seed)
        ks = jax.random.split(key, 10)
        b, q_len, k_len = (2, 1024, 2048)
        query = jax.random.normal(ks[0], (b, q_len, DIM), dtype=jnp.float32)
        keys = jax.random.normal(ks[1], (b, k_len, DIM), dtype=jnp.float32)
        values = jax.random.normal(ks[2], (b, k_len, DIM), dtype=jnp.float32)
        query_pos = jnp.sort(jax.random.randint(ks[3], (b, q_len), 0, 4096), axis=-1)
        key_pos = jnp.sort(jax.random.randint(ks[4], (b, k_len), 0, 4096), axis=-1)
        mask = jnp.ones((b, q_len, k_len), dtype=jnp.int32)
        lim = float(np.sqrt(6.0 / (DIM + DIM)))
        W_q = jax.random.uniform(ks[5], (DIM, DIM), minval=-lim, maxval=lim, dtype=jnp.float32)
        W_k = jax.random.uniform(ks[6], (DIM, DIM), minval=-lim, maxval=lim, dtype=jnp.float32)
        W_v = jax.random.uniform(ks[7], (DIM, DIM), minval=-lim, maxval=lim, dtype=jnp.float32)
        W_o = jax.random.uniform(ks[8], (DIM, DIM), minval=-lim, maxval=lim, dtype=jnp.float32)
        return {'query': query, 'keys': keys, 'values': values, 'W_q': W_q, 'W_k': W_k, 'W_v': W_v, 'W_o': W_o, 'query_pos': query_pos, 'key_pos': key_pos, 'mask': mask}
    _L0_xattn_all = _L0_xattn_setup()
    _L0_xattn_in = {k: v for k, v in _L0_xattn_all.items() if k in ('W_q', 'W_k', 'W_v', 'W_o')}
    del _L0_xattn_all

    def _L0_attn_setup():
        import jax, jax.numpy as jnp
        import numpy as np
        T, B, C = (512, 16, 512)
        FF = 4 * C

        def _ln(x, g, b):
            m = x.mean(-1, keepdims=True)
            v = jnp.var(x, axis=-1, keepdims=True)
            return (x - m) * jax.lax.rsqrt(v + 1e-05) * g + b

        def _wkv(w, u, k, v):
            b_, c_ = (k.shape[1], k.shape[2])
            init = (jnp.zeros((b_, c_), k.dtype), jnp.zeros((b_, c_), k.dtype), jnp.full((b_, c_), -1e+38, k.dtype))

            def step(carry, kv):
                aa, bb, pp = carry
                kt, vt = kv
                ww = u + kt
                qq = jnp.maximum(pp, ww)
                e1 = jnp.exp(pp - qq)
                e2 = jnp.exp(ww - qq)
                out = (e1 * aa + e2 * vt) / (e1 * bb + e2)
                ww2 = pp + w
                qq2 = jnp.maximum(ww2, kt)
                e1 = jnp.exp(ww2 - qq2)
                e2 = jnp.exp(kt - qq2)
                return ((e1 * aa + e2 * vt, e1 * bb + e2, qq2), out)
            _, out = jax.lax.scan(step, init, (k, v))
            return out

        def _shift(x):
            return jnp.concatenate([jnp.zeros_like(x[:1]), x[:-1]], axis=0)
        key = jax.random.key(seed)
        ks = jax.random.split(key, 16)
        sc = 1.0 / np.sqrt(C)
        return {'x': jax.random.normal(ks[0], (T, B, C), dtype=jnp.float32), 'ln1_g': jnp.ones((C,), jnp.float32), 'ln1_b': jnp.zeros((C,), jnp.float32), 'ln2_g': jnp.ones((C,), jnp.float32), 'ln2_b': jnp.zeros((C,), jnp.float32), 'time_mix_k': jax.random.uniform(ks[1], (C,), jnp.float32), 'time_mix_v': jax.random.uniform(ks[2], (C,), jnp.float32), 'time_mix_r': jax.random.uniform(ks[3], (C,), jnp.float32), 'time_decay': jax.random.normal(ks[4], (C,), jnp.float32) * 0.1, 'time_first': jax.random.normal(ks[5], (C,), jnp.float32) * 0.1, 'Wk': jax.random.normal(ks[6], (C, C), jnp.float32) * sc, 'Wv': jax.random.normal(ks[7], (C, C), jnp.float32) * sc, 'Wr': jax.random.normal(ks[8], (C, C), jnp.float32) * sc, 'Wo': jax.random.normal(ks[9], (C, C), jnp.float32) * sc, 'cmix_k': jax.random.uniform(ks[10], (C,), jnp.float32), 'cmix_r': jax.random.uniform(ks[11], (C,), jnp.float32), 'Wck': jax.random.normal(ks[12], (FF, C), jnp.float32) * sc, 'Wcv': jax.random.normal(ks[13], (C, FF), jnp.float32) * (1.0 / np.sqrt(FF)), 'Wcr': jax.random.normal(ks[14], (C, C), jnp.float32) * sc}
    _L0_attn_all = _L0_attn_setup()
    _L0_attn_in = {k: v for k, v in _L0_attn_all.items() if k in ('ln1_g', 'ln1_b', 'ln2_g', 'ln2_b', 'time_mix_k', 'time_mix_v', 'time_mix_r', 'time_decay', 'time_first', 'Wk', 'Wv', 'Wr', 'Wo', 'cmix_k', 'cmix_r', 'Wck', 'Wcv', 'Wcr')}
    del _L0_attn_all

    def _L0_ffn_setup():
        import jax, jax.numpy as jnp
        import numpy as np
        D = 512
        E = 8
        H = 1024
        TOP_K = 2
        ALPHA = 0.5
        LN_EPS = 1e-05

        def _experts_all(x, W1, b1, W2, b2):
            h = jax.nn.relu(jnp.einsum('bld,edh->eblh', x, W1) + b1[:, None, None, :])
            return jnp.einsum('eblh,ehd->ebld', h, W2) + b2[:, None, None, :]

        def _selected_expert(x, expert_idx, W1, b1, W2, b2):
            oh = jax.nn.one_hot(expert_idx, E, dtype=x.dtype)
            return jnp.einsum('ebld,ble->bld', _experts_all(x, W1, b1, W2, b2), oh)

        def _layer_norm(x, gamma, beta):
            mu = jnp.mean(x, axis=-1, keepdims=True)
            var = jnp.mean(jnp.square(x - mu), axis=-1, keepdims=True)
            return (x - mu) * jax.lax.rsqrt(var + LN_EPS) * gamma + beta
        key = jax.random.key(seed)
        ks = jax.random.split(key, 8)
        x = jax.random.normal(ks[0], (2, 1024, D), dtype=jnp.float32)
        gate_W = jax.random.normal(ks[1], (D, E), dtype=jnp.float32) * 0.02
        gate_b = jnp.zeros((E,), dtype=jnp.float32)
        W1 = jax.random.normal(ks[2], (E, D, H), dtype=jnp.float32) * 0.02
        b1 = jnp.zeros((E, H), dtype=jnp.float32)
        W2 = jax.random.normal(ks[3], (E, H, D), dtype=jnp.float32) * 0.02
        b2 = jnp.zeros((E, D), dtype=jnp.float32)
        ln_gamma = jnp.ones((D,), dtype=jnp.float32)
        ln_beta = jnp.zeros((D,), dtype=jnp.float32)
        return {'x': x, 'gate_W': gate_W, 'gate_b': gate_b, 'W1': W1, 'b1': b1, 'W2': W2, 'b2': b2, 'ln_gamma': ln_gamma, 'ln_beta': ln_beta}
    _L0_ffn_all = _L0_ffn_setup()
    _L0_ffn_in = {k: v for k, v in _L0_ffn_all.items() if k in ('gate_W', 'gate_b', 'W1', 'b1', 'W2', 'b2', 'ln_gamma', 'ln_beta')}
    del _L0_ffn_all

    def _L1_xattn_setup():
        import jax, jax.numpy as jnp
        import numpy as np
        H = 512
        B = 8
        L_CHAR = 1024
        L_SUB = 512

        def _linear(x, W, b):
            return jnp.einsum('blh,oh->blo', x, W) + b

        def _interp_linear(x, out_len):
            L_in = x.shape[1]
            pos = (jnp.arange(out_len, dtype=x.dtype) + 0.5) * (L_in / out_len) - 0.5
            pos = jnp.clip(pos, 0.0, L_in - 1)
            lo = jnp.floor(pos).astype(jnp.int32)
            hi = jnp.minimum(lo + 1, L_in - 1)
            w = (pos - lo.astype(x.dtype))[None, :, None]
            return x[:, lo] * (1 - w) + x[:, hi] * w
        key = jax.random.key(seed)
        ks = jax.random.split(key, 18)
        s = 0.02
        inp = {'char_emb': jax.random.normal(ks[0], (B, L_CHAR, H), jnp.float32), 'subword_emb': jax.random.normal(ks[1], (B, L_SUB, H), jnp.float32)}
        names = ['Wq_c', 'Wk_s', 'Wv_s', 'Wq_s', 'Wk_c', 'Wv_c']
        for i, n in enumerate(names):
            inp[n] = jax.random.normal(ks[2 + 2 * i], (H, H), jnp.float32) * s
            inp['b' + n[1:]] = jax.random.normal(ks[3 + 2 * i], (H,), jnp.float32) * s
        inp['Wg'] = jax.random.normal(ks[14], (H, 2 * H), jnp.float32) * s
        inp['bg'] = jax.random.normal(ks[15], (H,), jnp.float32) * s
        return inp
    _L1_xattn_all = _L1_xattn_setup()
    _L1_xattn_in = {k: v for k, v in _L1_xattn_all.items() if k in ('Wq_c', 'bq_c', 'Wk_s', 'bk_s', 'Wv_s', 'bv_s', 'Wq_s', 'bq_s', 'Wk_c', 'bk_c', 'Wv_c', 'bv_c', 'Wg', 'bg')}
    del _L1_xattn_all

    def _L1_attn_setup():
        import jax, jax.numpy as jnp
        import numpy as np
        BATCH, L, D_MODEL = (2, 512, 512)
        D_STATE, D_CONV, EXPAND = (16, 4, 2)
        D_INNER = EXPAND * D_MODEL
        DT_RANK = max(1, -(-D_MODEL // 16))

        def _forward(x, W_in, conv_w, conv_b, W_x, W_dt, b_dt, A_log, D, W_out):
            xv = x @ W_in
            xc = jnp.transpose(xv, (0, 2, 1))
            xc = jax.lax.conv_general_dilated(xc, conv_w, window_strides=(1,), padding=[(D_CONV - 1, 0)], dimension_numbers=('NCH', 'OIH', 'NCH'), feature_group_count=D_INNER)
            xv = jnp.transpose(xc, (0, 2, 1)) + conv_b
            xv = jax.nn.silu(xv)
            ssm = xv @ W_x
            dt_raw = ssm[..., :DT_RANK]
            Bp = ssm[..., DT_RANK:DT_RANK + D_STATE]
            Cp = ssm[..., DT_RANK + D_STATE:]
            delta = jax.nn.softplus(dt_raw @ W_dt + b_dt)
            A = -jnp.exp(A_log)
            dA = jnp.exp(delta[..., None] * A)
            dBx = delta[..., None] * Bp[:, :, None, :] * xv[..., None]

            def comb(c1, c2):
                a1, b1 = c1
                a2, b2 = c2
                return (a1 * a2, a2 * b1 + b2)
            _, h = jax.lax.associative_scan(comb, (dA, dBx), axis=1)
            y = jnp.einsum('bldn,bln->bld', h, Cp)
            y = y + xv * D
            return y @ W_out
        key = jax.random.key(seed)
        ks = jax.random.split(key, 10)
        s = 0.02
        x = jax.random.normal(ks[0], (BATCH, L, D_MODEL), jnp.float32)
        W_in = jax.random.normal(ks[1], (D_MODEL, D_INNER), jnp.float32) * s
        conv_w = jax.random.normal(ks[2], (D_INNER, 1, D_CONV), jnp.float32) * s
        conv_b = jax.random.normal(ks[3], (D_INNER,), jnp.float32) * s
        W_x = jax.random.normal(ks[4], (D_INNER, DT_RANK + 2 * D_STATE), jnp.float32) * s
        W_dt = jax.random.normal(ks[5], (DT_RANK, D_INNER), jnp.float32) * s
        b_dt = jax.random.normal(ks[6], (D_INNER,), jnp.float32) * s
        A_log = jnp.log(jnp.broadcast_to(jnp.arange(1, D_STATE + 1, dtype=jnp.float32), (D_INNER, D_STATE)))
        D = jnp.ones((D_INNER,), jnp.float32)
        W_out = jax.random.normal(ks[7], (D_INNER, D_MODEL), jnp.float32) * s
        return {'x': x, 'W_in': W_in, 'conv_w': conv_w, 'conv_b': conv_b, 'W_x': W_x, 'W_dt': W_dt, 'b_dt': b_dt, 'A_log': A_log, 'D': D, 'W_out': W_out}
    _L1_attn_all = _L1_attn_setup()
    _L1_attn_in = {k: v for k, v in _L1_attn_all.items() if k in ('W_in', 'conv_w', 'conv_b', 'W_x', 'W_dt', 'b_dt', 'A_log', 'D', 'W_out')}
    del _L1_attn_all

    def _L1_ffn_setup():
        import jax, jax.numpy as jnp
        import numpy as np
        E = 8
        H = 512
        D = 512
        TOP_K = 2
        key = jax.random.key(seed)
        k0, k1, k2, k3 = jax.random.split(key, 4)
        x = jax.random.normal(k0, (1, 1024, H), dtype=jnp.float32)
        router_w = jax.random.normal(k1, (E, H), dtype=jnp.float32) * (1.0 / np.sqrt(H))
        up_proj = jax.random.normal(k2, (E, H, 2 * D), dtype=jnp.float32) * (1.0 / np.sqrt(H))
        down_proj = jax.random.normal(k3, (E, D, H), dtype=jnp.float32) * (1.0 / np.sqrt(D))
        return {'x': x, 'router_w': router_w, 'up_proj': up_proj, 'down_proj': down_proj}
    _L1_ffn_all = _L1_ffn_setup()
    _L1_ffn_in = {k: v for k, v in _L1_ffn_all.items() if k in ('router_w', 'up_proj', 'down_proj')}
    del _L1_ffn_all
    return {'x': x, 'ctx_1024': ctx_1024, 'itok_BxS_8_8191': itok_BxS_8_8191, 'itok_BxS2_1_8191': itok_BxS2_1_8191, 'mask_BxSxS2_if1': mask_BxSxS2_if1, 'L0_xattn_W_q': _L0_xattn_in['W_q'], 'L0_xattn_W_k': _L0_xattn_in['W_k'], 'L0_xattn_W_v': _L0_xattn_in['W_v'], 'L0_xattn_W_o': _L0_xattn_in['W_o'], 'L0_attn_ln1_g': _L0_attn_in['ln1_g'], 'L0_attn_ln1_b': _L0_attn_in['ln1_b'], 'L0_attn_ln2_g': _L0_attn_in['ln2_g'], 'L0_attn_ln2_b': _L0_attn_in['ln2_b'], 'L0_attn_time_mix_k': _L0_attn_in['time_mix_k'], 'L0_attn_time_mix_v': _L0_attn_in['time_mix_v'], 'L0_attn_time_mix_r': _L0_attn_in['time_mix_r'], 'L0_attn_time_decay': _L0_attn_in['time_decay'], 'L0_attn_time_first': _L0_attn_in['time_first'], 'L0_attn_Wk': _L0_attn_in['Wk'], 'L0_attn_Wv': _L0_attn_in['Wv'], 'L0_attn_Wr': _L0_attn_in['Wr'], 'L0_attn_Wo': _L0_attn_in['Wo'], 'L0_attn_cmix_k': _L0_attn_in['cmix_k'], 'L0_attn_cmix_r': _L0_attn_in['cmix_r'], 'L0_attn_Wck': _L0_attn_in['Wck'], 'L0_attn_Wcv': _L0_attn_in['Wcv'], 'L0_attn_Wcr': _L0_attn_in['Wcr'], 'L0_ffn_gate_W': _L0_ffn_in['gate_W'], 'L0_ffn_gate_b': _L0_ffn_in['gate_b'], 'L0_ffn_W1': _L0_ffn_in['W1'], 'L0_ffn_b1': _L0_ffn_in['b1'], 'L0_ffn_W2': _L0_ffn_in['W2'], 'L0_ffn_b2': _L0_ffn_in['b2'], 'L0_ffn_ln_gamma': _L0_ffn_in['ln_gamma'], 'L0_ffn_ln_beta': _L0_ffn_in['ln_beta'], 'L1_xattn_Wq_c': _L1_xattn_in['Wq_c'], 'L1_xattn_bq_c': _L1_xattn_in['bq_c'], 'L1_xattn_Wk_s': _L1_xattn_in['Wk_s'], 'L1_xattn_bk_s': _L1_xattn_in['bk_s'], 'L1_xattn_Wv_s': _L1_xattn_in['Wv_s'], 'L1_xattn_bv_s': _L1_xattn_in['bv_s'], 'L1_xattn_Wq_s': _L1_xattn_in['Wq_s'], 'L1_xattn_bq_s': _L1_xattn_in['bq_s'], 'L1_xattn_Wk_c': _L1_xattn_in['Wk_c'], 'L1_xattn_bk_c': _L1_xattn_in['bk_c'], 'L1_xattn_Wv_c': _L1_xattn_in['Wv_c'], 'L1_xattn_bv_c': _L1_xattn_in['bv_c'], 'L1_xattn_Wg': _L1_xattn_in['Wg'], 'L1_xattn_bg': _L1_xattn_in['bg'], 'L1_attn_W_in': _L1_attn_in['W_in'], 'L1_attn_conv_w': _L1_attn_in['conv_w'], 'L1_attn_conv_b': _L1_attn_in['conv_b'], 'L1_attn_W_x': _L1_attn_in['W_x'], 'L1_attn_W_dt': _L1_attn_in['W_dt'], 'L1_attn_b_dt': _L1_attn_in['b_dt'], 'L1_attn_A_log': _L1_attn_in['A_log'], 'L1_attn_D': _L1_attn_in['D'], 'L1_attn_W_out': _L1_attn_in['W_out'], 'L1_ffn_router_w': _L1_ffn_in['router_w'], 'L1_ffn_up_proj': _L1_ffn_in['up_proj'], 'L1_ffn_down_proj': _L1_ffn_in['down_proj']}

def reference(x, ctx_1024, itok_BxS_8_8191, itok_BxS2_1_8191, mask_BxSxS2_if1, L0_xattn_W_q, L0_xattn_W_k, L0_xattn_W_v, L0_xattn_W_o, L0_attn_ln1_g, L0_attn_ln1_b, L0_attn_ln2_g, L0_attn_ln2_b, L0_attn_time_mix_k, L0_attn_time_mix_v, L0_attn_time_mix_r, L0_attn_time_decay, L0_attn_time_first, L0_attn_Wk, L0_attn_Wv, L0_attn_Wr, L0_attn_Wo, L0_attn_cmix_k, L0_attn_cmix_r, L0_attn_Wck, L0_attn_Wcv, L0_attn_Wcr, L0_ffn_gate_W, L0_ffn_gate_b, L0_ffn_W1, L0_ffn_b1, L0_ffn_W2, L0_ffn_b2, L0_ffn_ln_gamma, L0_ffn_ln_beta, L1_xattn_Wq_c, L1_xattn_bq_c, L1_xattn_Wk_s, L1_xattn_bk_s, L1_xattn_Wv_s, L1_xattn_bv_s, L1_xattn_Wq_s, L1_xattn_bq_s, L1_xattn_Wk_c, L1_xattn_bk_c, L1_xattn_Wv_c, L1_xattn_bv_c, L1_xattn_Wg, L1_xattn_bg, L1_attn_W_in, L1_attn_conv_w, L1_attn_conv_b, L1_attn_W_x, L1_attn_W_dt, L1_attn_b_dt, L1_attn_A_log, L1_attn_D, L1_attn_W_out, L1_ffn_router_w, L1_ffn_up_proj, L1_ffn_down_proj):
    import jax
    import jax.numpy as jnp

    def _L0_xattn_ref(query, keys, values, W_q, W_k, W_v, W_o, query_pos, key_pos, mask):
        import jax, jax.numpy as jnp
        import numpy as np
        DIM = 512
        NUM_HEADS = 16
        HEAD_DIM = DIM // NUM_HEADS

        def _slopes(num_heads):
            ratio = 2.0 ** (-8.0 / num_heads)
            return jnp.asarray([ratio ** i for i in range(1, num_heads + 1)], dtype=jnp.float32)
        b, q_len, _ = query.shape
        k_len = keys.shape[1]
        scale = 1.0 / np.sqrt(HEAD_DIM)
        Q = (query @ W_q.T).reshape(b, q_len, NUM_HEADS, HEAD_DIM).transpose(0, 2, 1, 3)
        K = (keys @ W_k.T).reshape(b, k_len, NUM_HEADS, HEAD_DIM).transpose(0, 2, 1, 3)
        V = (values @ W_v.T).reshape(b, k_len, NUM_HEADS, HEAD_DIM).transpose(0, 2, 1, 3)
        scores = jnp.einsum('bhqd,bhkd->bhqk', Q, K) * scale
        dist = (query_pos[:, :, None] - key_pos[:, None, :]).astype(scores.dtype)
        bias = -_slopes(NUM_HEADS)[None, :, None, None] * dist[:, None, :, :]
        scores = scores + bias
        scores = jnp.where(mask[:, None, :, :] == 0, -jnp.inf, scores)
        m = jnp.max(scores, axis=-1, keepdims=True)
        e = jnp.exp(scores - m)
        attn = e / (1.0 + jnp.sum(e, axis=-1, keepdims=True))
        out = jnp.einsum('bhqk,bhkd->bhqd', attn, V)
        out = out.transpose(0, 2, 1, 3).reshape(b, q_len, DIM)
        return out @ W_o.T

    def _L0_attn_ref(x, ln1_g, ln1_b, ln2_g, ln2_b, time_mix_k, time_mix_v, time_mix_r, time_decay, time_first, Wk, Wv, Wr, Wo, cmix_k, cmix_r, Wck, Wcv, Wcr):
        import jax, jax.numpy as jnp
        import numpy as np
        T, B, C = (512, 16, 512)
        FF = 4 * C

        def _ln(x, g, b):
            m = x.mean(-1, keepdims=True)
            v = jnp.var(x, axis=-1, keepdims=True)
            return (x - m) * jax.lax.rsqrt(v + 1e-05) * g + b

        def _wkv(w, u, k, v):
            b_, c_ = (k.shape[1], k.shape[2])
            init = (jnp.zeros((b_, c_), k.dtype), jnp.zeros((b_, c_), k.dtype), jnp.full((b_, c_), -1e+38, k.dtype))

            def step(carry, kv):
                aa, bb, pp = carry
                kt, vt = kv
                ww = u + kt
                qq = jnp.maximum(pp, ww)
                e1 = jnp.exp(pp - qq)
                e2 = jnp.exp(ww - qq)
                out = (e1 * aa + e2 * vt) / (e1 * bb + e2)
                ww2 = pp + w
                qq2 = jnp.maximum(ww2, kt)
                e1 = jnp.exp(ww2 - qq2)
                e2 = jnp.exp(kt - qq2)
                return ((e1 * aa + e2 * vt, e1 * bb + e2, qq2), out)
            _, out = jax.lax.scan(step, init, (k, v))
            return out

        def _shift(x):
            return jnp.concatenate([jnp.zeros_like(x[:1]), x[:-1]], axis=0)
        xx = _ln(x, ln1_g, ln1_b)
        xs = _shift(xx)
        k = jnp.einsum('tbc,oc->tbo', xx * time_mix_k + xs * (1 - time_mix_k), Wk)
        v = jnp.einsum('tbc,oc->tbo', xx * time_mix_v + xs * (1 - time_mix_v), Wv)
        r = jax.nn.sigmoid(jnp.einsum('tbc,oc->tbo', xx * time_mix_r + xs * (1 - time_mix_r), Wr))
        wkv = _wkv(-jnp.exp(time_decay), time_first, k, v)
        x = x + jnp.einsum('tbc,oc->tbo', r * wkv, Wo)
        yy = _ln(x, ln2_g, ln2_b)
        ys = _shift(yy)
        kk = jnp.einsum('tbc,fc->tbf', yy * cmix_k + ys * (1 - cmix_k), Wck)
        vv = jnp.einsum('tbf,of->tbo', jnp.square(jax.nn.relu(kk)), Wcv)
        rr = jax.nn.sigmoid(jnp.einsum('tbc,oc->tbo', yy * cmix_r + ys * (1 - cmix_r), Wcr))
        return x + rr * vv

    def _L0_ffn_ref(x, gate_W, gate_b, W1, b1, W2, b2, ln_gamma, ln_beta):
        import jax, jax.numpy as jnp
        import numpy as np
        D = 512
        E = 8
        H = 1024
        TOP_K = 2
        ALPHA = 0.5
        LN_EPS = 1e-05

        def _experts_all(x, W1, b1, W2, b2):
            h = jax.nn.relu(jnp.einsum('bld,edh->eblh', x, W1) + b1[:, None, None, :])
            return jnp.einsum('eblh,ehd->ebld', h, W2) + b2[:, None, None, :]

        def _selected_expert(x, expert_idx, W1, b1, W2, b2):
            oh = jax.nn.one_hot(expert_idx, E, dtype=x.dtype)
            return jnp.einsum('ebld,ble->bld', _experts_all(x, W1, b1, W2, b2), oh)

        def _layer_norm(x, gamma, beta):
            mu = jnp.mean(x, axis=-1, keepdims=True)
            var = jnp.mean(jnp.square(x - mu), axis=-1, keepdims=True)
            return (x - mu) * jax.lax.rsqrt(var + LN_EPS) * gamma + beta
        residual = x
        gate_logits = jnp.einsum('bld,de->ble', x, gate_W) + gate_b
        gate_weights = jax.nn.softmax(gate_logits, axis=-1)
        topk_vals, topk_idx = jax.lax.top_k(gate_weights, TOP_K)
        boost = jax.lax.stop_gradient(x)
        outs = []
        for i in range(TOP_K):
            eo = _selected_expert(boost, topk_idx[:, :, i], W1, b1, W2, b2)
            outs.append(eo)
            if i < TOP_K - 1:
                boost = boost + ALPHA * jax.lax.stop_gradient(eo)
        fused = sum((topk_vals[:, :, i:i + 1] * outs[i] for i in range(TOP_K)))
        return _layer_norm(residual + fused, ln_gamma, ln_beta)

    def _L1_xattn_ref(char_emb, subword_emb, Wq_c, bq_c, Wk_s, bk_s, Wv_s, bv_s, Wq_s, bq_s, Wk_c, bk_c, Wv_c, bv_c, Wg, bg):
        import jax, jax.numpy as jnp
        import numpy as np
        H = 512
        B = 8
        L_CHAR = 1024
        L_SUB = 512

        def _linear(x, W, b):
            return jnp.einsum('blh,oh->blo', x, W) + b

        def _interp_linear(x, out_len):
            L_in = x.shape[1]
            pos = (jnp.arange(out_len, dtype=x.dtype) + 0.5) * (L_in / out_len) - 0.5
            pos = jnp.clip(pos, 0.0, L_in - 1)
            lo = jnp.floor(pos).astype(jnp.int32)
            hi = jnp.minimum(lo + 1, L_in - 1)
            w = (pos - lo.astype(x.dtype))[None, :, None]
            return x[:, lo] * (1 - w) + x[:, hi] * w
        h = char_emb.shape[-1]
        scale = 1.0 / jnp.sqrt(jnp.asarray(h, char_emb.dtype))
        Q_char = _linear(char_emb, Wq_c, bq_c)
        K_sub = _linear(subword_emb, Wk_s, bk_s)
        V_sub = _linear(subword_emb, Wv_s, bv_s)
        scores = jnp.einsum('bqh,bkh->bqk', Q_char, K_sub) * scale
        char2sub = jnp.einsum('bqk,bkh->bqh', jax.nn.softmax(scores, axis=-1), V_sub)
        Q_sub = _linear(subword_emb, Wq_s, bq_s)
        K_char = _linear(char_emb, Wk_c, bk_c)
        V_char = _linear(char_emb, Wv_c, bv_c)
        scores2 = jnp.einsum('bqh,bkh->bqk', Q_sub, K_char) * scale
        sub2char = jnp.einsum('bqk,bkh->bqh', jax.nn.softmax(scores2, axis=-1), V_char)
        L_char = char_emb.shape[1]
        if sub2char.shape[1] != L_char:
            sub2char = _interp_linear(sub2char, L_char)
        gate_in = jnp.concatenate([char2sub, sub2char], axis=-1)
        gate = jax.nn.sigmoid(jnp.einsum('blh,oh->blo', gate_in, Wg) + bg)
        return gate * char2sub + (1 - gate) * sub2char

    def _L1_attn_ref(x, W_in, conv_w, conv_b, W_x, W_dt, b_dt, A_log, D, W_out):
        import jax, jax.numpy as jnp
        import numpy as np
        BATCH, L, D_MODEL = (2, 512, 512)
        D_STATE, D_CONV, EXPAND = (16, 4, 2)
        D_INNER = EXPAND * D_MODEL
        DT_RANK = max(1, -(-D_MODEL // 16))

        def _forward(x, W_in, conv_w, conv_b, W_x, W_dt, b_dt, A_log, D, W_out):
            xv = x @ W_in
            xc = jnp.transpose(xv, (0, 2, 1))
            xc = jax.lax.conv_general_dilated(xc, conv_w, window_strides=(1,), padding=[(D_CONV - 1, 0)], dimension_numbers=('NCH', 'OIH', 'NCH'), feature_group_count=D_INNER)
            xv = jnp.transpose(xc, (0, 2, 1)) + conv_b
            xv = jax.nn.silu(xv)
            ssm = xv @ W_x
            dt_raw = ssm[..., :DT_RANK]
            Bp = ssm[..., DT_RANK:DT_RANK + D_STATE]
            Cp = ssm[..., DT_RANK + D_STATE:]
            delta = jax.nn.softplus(dt_raw @ W_dt + b_dt)
            A = -jnp.exp(A_log)
            dA = jnp.exp(delta[..., None] * A)
            dBx = delta[..., None] * Bp[:, :, None, :] * xv[..., None]

            def comb(c1, c2):
                a1, b1 = c1
                a2, b2 = c2
                return (a1 * a2, a2 * b1 + b2)
            _, h = jax.lax.associative_scan(comb, (dA, dBx), axis=1)
            y = jnp.einsum('bldn,bln->bld', h, Cp)
            y = y + xv * D
            return y @ W_out
        return _forward(x, W_in, conv_w, conv_b, W_x, W_dt, b_dt, A_log, D, W_out)

    def _L1_ffn_ref(x, router_w, up_proj, down_proj):
        import jax, jax.numpy as jnp
        import numpy as np
        E = 8
        H = 512
        D = 512
        TOP_K = 2
        B, T, _ = x.shape
        xt = x.reshape(-1, H)
        N = xt.shape[0]
        logits = jnp.einsum('nh,eh->ne', xt, router_w)
        probs = jax.nn.softmax(logits, axis=-1)
        scores, expert_idx = jax.lax.top_k(probs, TOP_K)
        scores = scores / jnp.sum(scores, axis=-1, keepdims=True)
        gate = jnp.zeros((N, E), dtype=xt.dtype).at[jnp.arange(N)[:, None], expert_idx].add(scores)
        h = jnp.einsum('nh,ehd->end', xt, up_proj)
        hidden = jax.nn.silu(h[..., :D]) * h[..., D:]
        out_e = jnp.einsum('end,edh->enh', hidden, down_proj)
        out = jnp.einsum('ne,enh->nh', gate, out_e)
        return out.reshape(B, T, H)
    x = x + _L0_xattn_ref(_layernorm(x, axis=-1), ctx_1024, ctx_1024, L0_xattn_W_q, L0_xattn_W_k, L0_xattn_W_v, L0_xattn_W_o, itok_BxS_8_8191, itok_BxS2_1_8191, mask_BxSxS2_if1)
    x = x + _L0_attn_ref(_layernorm(x, axis=-1), L0_attn_ln1_g, L0_attn_ln1_b, L0_attn_ln2_g, L0_attn_ln2_b, L0_attn_time_mix_k, L0_attn_time_mix_v, L0_attn_time_mix_r, L0_attn_time_decay, L0_attn_time_first, L0_attn_Wk, L0_attn_Wv, L0_attn_Wr, L0_attn_Wo, L0_attn_cmix_k, L0_attn_cmix_r, L0_attn_Wck, L0_attn_Wcv, L0_attn_Wcr)
    x = x + _L0_ffn_ref(_layernorm(x, axis=-1), L0_ffn_gate_W, L0_ffn_gate_b, L0_ffn_W1, L0_ffn_b1, L0_ffn_W2, L0_ffn_b2, L0_ffn_ln_gamma, L0_ffn_ln_beta)
    x = x + _L1_xattn_ref(_layernorm(x, axis=-1), ctx_1024, L1_xattn_Wq_c, L1_xattn_bq_c, L1_xattn_Wk_s, L1_xattn_bk_s, L1_xattn_Wv_s, L1_xattn_bv_s, L1_xattn_Wq_s, L1_xattn_bq_s, L1_xattn_Wk_c, L1_xattn_bk_c, L1_xattn_Wv_c, L1_xattn_bv_c, L1_xattn_Wg, L1_xattn_bg)
    x = x + _L1_attn_ref(_layernorm(x, axis=-1), L1_attn_W_in, L1_attn_conv_w, L1_attn_conv_b, L1_attn_W_x, L1_attn_W_dt, L1_attn_b_dt, L1_attn_A_log, L1_attn_D, L1_attn_W_out)
    x = x + _L1_ffn_ref(_layernorm(x, axis=-1), L1_ffn_router_w, L1_ffn_up_proj, L1_ffn_down_proj)
    return x

_drawn_inputs = setup_inputs


def setup_inputs(seed=0):
    import zlib

    import numpy as np

    out = dict(_drawn_inputs(seed))
    spreads = {'L0_attn_ln1_g': (1.0, 0.2),
     'L0_attn_ln1_b': (0.0, 0.267),
     'L0_attn_ln2_g': (1.0, 0.2),
     'L0_attn_ln2_b': (0.0, 0.1),
     'L0_ffn_gate_b': (0.0, 0.642),
     'L0_ffn_b1': (0.0, 0.8),
     'L0_ffn_b2': (0.0, 0.534),
     'L0_ffn_ln_gamma': (1.0, 0.2),
     'L0_ffn_ln_beta': (0.0, 0.1),
     'L1_attn_D': (1.0, 0.6)}
    factors = {'L0_attn_time_decay': 7.945,
     'L0_attn_time_first': 6.867,
     'L0_ffn_W1': 2.861,
     'L1_xattn_Wq_c': 8.0,
     'L1_xattn_bq_c': 8.0,
     'L1_xattn_Wk_s': 8.0,
     'L1_xattn_bk_s': 64.0,
     'L1_xattn_bv_s': 8.0,
     'L1_xattn_Wq_s': 8.0,
     'L1_xattn_bq_s': 25.653,
     'L1_xattn_Wk_c': 8.0,
     'L1_xattn_bk_c': 64.0,
     'L1_xattn_bv_c': 8.0,
     'L1_xattn_Wg': 6.839,
     'L1_xattn_bg': 40.577,
     'L1_attn_W_in': 8.0,
     'L1_attn_conv_w': 8.0,
     'L1_attn_conv_b': 8.0,
     'L1_attn_W_x': 8.0,
     'L1_attn_W_dt': 8.0,
     'L1_attn_b_dt': 8.0,
     'L1_attn_A_log': 8.0,
     'L1_attn_W_out': 8.0,
     'L1_ffn_router_w': 8.0,
     'L1_ffn_up_proj': 8.0,
     'L1_ffn_down_proj': 8.0}
    for name, (base, spread) in spreads.items():
        noise = np.random.default_rng([zlib.crc32(name.encode()), seed]).standard_normal(out[name].shape)
        drawn = base * np.exp(spread * noise) if base else spread * noise
        out[name] = jnp.asarray(drawn.astype(out[name].dtype))
    for name, factor in factors.items():
        out[name] = (out[name] * factor).astype(out[name].dtype)
    return out
```

```python
from contextlib import ExitStack, contextmanager

import numpy as np

import concourse.bass as bass
from concourse import mybir

F32 = mybir.dt.float32
I32 = mybir.dt.int32
U32 = mybir.dt.uint32
ALU = mybir.AluOpType
ACT = mybir.ActivationFunctionType
AX_X = mybir.AxisListType.X

P = 128
B, S, D = 8, 64, 512
S2 = 1601
N = B * S
C = D // P
NT = N // P
HEADS, HD = 16, 32
PAIRS = HEADS // 2
KT_TILES = (S2 + P - 1) // P
LAST = S2 - (KT_TILES - 1) * P
CHUNKS = [(0, 401), (401, 801), (801, 1201), (1201, 1601)]
EXPERTS = 8
FF = 4 * D
HID = 1024
DI, NS, TAPS, RANK = 1024, 16, 4, 32
SLOT = 8200
BIG = 1e38
STRIDE, PICK = 25, 12

COLS = {}
_at = 0
for _name, _n in [("ln1_g", 4), ("ln1_b", 4), ("ln2_g", 4), ("ln2_b", 4), ("mix_k", 4), ("mix_v", 4), ("mix_r", 4),
                  ("decay", 4), ("first", 4), ("cmix_k", 4), ("cmix_r", 4), ("bq_c", 4), ("bk_s", 4), ("bv_s", 4),
                  ("bq_s", 4), ("bk_c", 4), ("bg", 4), ("conv_w", 32), ("conv_b", 8), ("b_dt", 8), ("A_log", 128),
                  ("D", 8), ("ident", 128), ("slopes", 8), ("interp", 64), ("iota", 8), ("gate_W", 32), ("router", 32)]:
    COLS[_name] = (_at, _n)
    _at += _n
NCOLS = _at
ROWS = {"gamma": 0, "beta": 512, "bv_c": 1024, "gate_b": 1536}
NROWS = 1544


class Side:

    def __init__(self):
        self.n, self.off = 0, 0

    @contextmanager
    def loop(self, i, first, trips, per, step=1):
        was = self.n
        if per:
            self.off = (i - first) * (per // step)
        yield
        assert self.n - was == per, (self.n - was, per)
        self.off = 0
        self.n = was + per * (trips // step)


class Chain(Side):

    def __init__(self, eng, sem):
        super().__init__()
        self.eng, self.sem = eng, sem

    def done(self, ins):
        ins.then_inc(self.sem, 1)
        self.n += 1

    def wait(self):
        self.eng.wait_ge(self.sem, self.off + self.n)

    def link(self, ins):
        self.done(ins)
        self.wait()


class Ring:

    def __init__(self, banks, filled, emptied):
        self.banks, self.filled, self.emptied = banks, filled, emptied
        self.fills, self.takes = Side(), Side()

    def claim(self, pe):
        k, r = self.fills.n, len(self.banks)
        if k >= r:
            pe.wait_ge(self.emptied, self.fills.off + (k - r + 1))
        return self.banks[k % r]

    def fill(self, ins):
        ins.then_inc(self.filled, 1)
        self.fills.n += 1

    def take(self, eng):
        eng.wait_ge(self.filled, self.takes.off + (self.takes.n + 1))
        return self.banks[self.takes.n % len(self.banks)]

    def empty(self, ins):
        ins.then_inc(self.emptied, 1)
        self.takes.n += 1


def perceiver_kernel(nc, t, stages="ABCDEF"):
    with ExitStack() as ctx:
        def sb(name, shape, dt=F32):
            return ctx.enter_context(nc.sbuf_tensor(name, shape, dt))

        def sem(name):
            return ctx.enter_context(nc.semaphore(name))

        ps = ctx.enter_context(nc.psum_tensor("ps", [P, 8, 512], F32))

        cols = sb("cols", [P, NCOLS])
        rows = sb("rows", [P, NROWS])
        x = sb("x", [P, NT, D])
        hn = sb("hn", [P, 2 * NT * D])
        wbuf = sb("wbuf", [P, 2, SLOT])
        small = sb("small", [P, 512])
        arena = sb("arena", [P, 27800])

        def col(name):
            a, n = COLS[name]
            return cols[:, a:a + n]

        def row(name, n=512):
            return rows[:, ROWS[name]:ROWS[name] + n]

        ident = col("ident")
        h_tok = hn[:, 0:NT * D].rearrange("p (t d) -> p t d", t=NT)
        hT = hn[:, NT * D:].rearrange("p (c n) -> p c n", c=C)

        def slot(n, a, b, **kw):
            v = wbuf[:, n % 2, a:b]
            return v.rearrange("p (c n) -> p c n", **kw) if kw else v

        class Carve:
            def __init__(self):
                self.at = 0

            def take(self, n, c=None):
                v = arena[:, self.at:self.at + n]
                self.at += n
                assert self.at <= 27800, self.at
                return v if c is None else v.rearrange("p (c n) -> p c n", c=c)

        sm = [0]

        def stat(n):
            v = small[:, sm[0]:sm[0] + n]
            sm[0] += n
            assert sm[0] <= 512
            return v

        ar = Carve()
        a_ctxT = ar.take(C * S2, C)
        a_V = ar.take(KT_TILES * D, KT_TILES)
        a_S = ar.take(2 * S2, 2)
        a_PT = ar.take(KT_TILES * P, KT_TILES)
        a_dist = ar.take(S2)
        a_mask = ar.take(S2)
        a_bias = ar.take(2 * S2, 2)
        a_Qbd = ar.take(PAIRS * P, PAIRS)
        a_QT = ar.take(C * N, C)
        a_KT = wbuf[:, 1, 0:C * S2].rearrange("p (c n) -> p c n", c=C)
        a_attn = hn[0:S, 0:B * D].rearrange("p (b d) -> p b d", b=B)
        a_attnT = a_QT
        a_qpos = stat(1)
        a_mx, a_nm, a_rs, a_rd = stat(4), stat(8), stat(8), stat(8)

        ar = Carve()
        b_xxT, b_mk, b_mv, b_mr = (ar.take(C * N, C) for _ in range(4))
        b_k, b_v, b_r = (ar.take(C * N, C) for _ in range(3))
        b_h1 = ar.take(NT * D, NT)
        b_wcr = ar.take(C * D, C)
        b_t = [b_xxT, b_mk, b_mv, b_mr] + [ar.take(C * N, C) for _ in range(4)]
        b_kk = arena[:, 3 * C * N:3 * C * N + 16 * N].rearrange("p (c n) -> p c n", c=16)
        b_w, b_omk = stat(4), stat(20)

        ar = Carve()
        c_acc, c_res = ar.take(NT * D, NT), ar.take(NT * D, NT)
        c_hid = ar.take(8 * N, 8)
        c_h1, c_e = ar.take(4 * N, 4), ar.take(4 * N, 4)
        c_oh = ar.take(3 * NT * 8).rearrange("p (k t e) -> p k t e", k=3, t=NT)
        c_lg, c_m8, c_e8, c_ixf = (ar.take(NT * 8, NT) for _ in range(4))
        c_ix = ar.take(NT * 8, NT)
        c_ohT = ar.take(N)
        c_b2 = ar.take(D)
        c_gate_e = ar.take(8).rearrange("p (k t) -> p k t", k=2)
        c_sum, c_w, c_nmx = stat(4), stat(8), stat(4)

        ar = Carve()
        d_ctxT = ar.take(C * S2, C)
        d_qkT, d_g2T = ar.take(C * N, C), ar.take(C * N, C)
        d_qcT, d_kcT = ar.take(C * N, C), ar.take(C * N, C)
        d_Vc = ar.take(B * D, B)[0:S]
        d_S = ar.take(S2)[0:S]
        d_PT = ar.take(KT_TILES * S, KT_TILES)
        d_qk_b = ar.take(C * S, C)
        d_sel = ar.take(C * P, C)
        d_P2 = ar.take(S)
        d_P2T = ar.take(B * S, B)[0:S]
        d_bqk = ar.take(N)[0:1]
        d_ones = ar.take(P)[0:1]
        d_ctx = wbuf[:, 0, 0:KT_TILES * D].rearrange("p (c n) -> p c n", c=KT_TILES)
        d_pc = hn[0:S, 0:B * D].rearrange("p (b d) -> p b d", b=B)
        d_pcT, d_c2s, d_s2c, d_gate = d_qkT, d_qcT, d_kcT, d_g2T
        d_qbk, d_qb1, d_nm, d_rs, d_rd = stat(8), stat(1), stat(2), stat(2), stat(2)

        ar = Carve()
        e_xv, e_dx, e_de = (ar.take(8 * N, 8) for _ in range(3))
        G = 4
        e_dA, e_h, e_hC = (ar.take(2 * G * N, 2) for _ in range(3))
        e_wx = ar.take(512, 8)
        e_wdt = ar.take(DI)
        e_ssm = ar.take(N)
        e_B = wbuf[:, 1, 0:NS * N]
        e_C = [hn[:, 0:8 * N], wbuf[:, 0, 0:8 * N]]
        e_negA = stat(128)

        ln_eps, ln_sd, ln_rstd, ln_st, d_nbg = stat(1), stat(4), stat(4), stat(24), stat(4)
        ln_mv = stat(8).rearrange("p (t k) -> p t k", k=2)

        def flat(v):
            return v.rearrange("p c n -> p (c n)")

        def timed(v):
            return v.rearrange("p c (s t) -> p (c s) t", t=B)

        NORMS = [n for n in ("A", "B0", "B1", "B2", "C", "C2", "D", "E", "F") if n[0] in stages]
        TURNS = [n for n in ("A", "B", "B2", "C", "C2", "D", "E", "F") if n[0] in stages]

        in_consts, in_x = sem("in_consts"), sem("in_x")
        slot_in = [sem("slot0_in"), sem("slot1_in")]
        slot_free, kt_free, brows_free = sem("slot_free"), sem("kt_free"), sem("brows_free")
        ringV = Ring([0, 1, 2, 3], sem("vector_bank_filled"), sem("vector_bank_emptied"))
        ringS = Ring([4, 5, 6, 7], sem("scalar_bank_filled"), sem("scalar_bank_emptied"))
        dve_done, act_done, pool_done = sem("dve_done"), sem("act_done"), sem("pool_done")
        ln_var, ln_std, ln_rows = sem("ln_var"), sem("ln_std"), sem("ln_rows")
        ctx_in, ctxn_in = sem("ctx_in"), sem("ctxn_in")
        pos_in, pos_free = sem("pos_in"), sem("pos_free")
        bias_made, bias_used = sem("bias_made"), sem("bias_used")
        qbd_made = sem("qbd_made")
        row_max, probs_made = sem("row_max"), sem("probs_made")
        stage_w_in = sem("stage_w_in")
        mix_half, mix_made, eps_made = sem("mix_half"), sem("mix_made"), sem("eps_made")
        wkv_arg, wkv_exp, wkv_made, sq_made = sem("wkv_arg"), sem("wkv_exp"), sem("wkv_made"), sem("sq_made")
        gate_arg, gate_exp, oh_made, boost_made = sem("gate_arg"), sem("gate_exp"), sem("oh_made"), sem("boost_made")
        hid_made, gated_made, nbg_made, d_vectors = sem("hid_made"), sem("gated_made"), sem("nbg_made"), sem("d_vectors")
        qkb_made, s2_arg, s2_exp, s2_made = sem("qkb_made"), sem("s2_arg"), sem("s2_exp"), sem("s2_made")
        x_made, out_done = sem("x_made"), sem("out_done")
        conv_in, conv_exp, xv_made = sem("conv_in"), sem("conv_exp"), sem("xv_made")
        dt_arg, dt_exp, delta_made = sem("dt_arg"), sem("dt_exp"), sem("delta_made")
        neg_a, da_made, h_made, hc_made, y_made = (sem("neg_a"), sem("da_made"), sem("h_made"), sem("hc_made"),
                                                     sem("y_made"))
        waits_passed = sem("waits_passed")

        def held(eng):
            eng.sem_inc(waits_passed, 1)

        y_taken, sel_made = sem("y_taken"), sem("sel_made")

        SLOTS = ([("A", 0, 4), ("B", 1, 4), ("B", 2, 4), ("B", 3, 4)] + [("C", 4 + e, 1) for e in range(16)]
                 + [("D", 20, 4), ("D", 21, 4), ("E", 22, 2)] + [("F", 23 + e, 1) for e in range(8)])
        filled_at, so_far = {}, [0, 0]
        for st, n, transfers in SLOTS:
            if st in stages:
                so_far[n % 2] += 16 * transfers
            filled_at[n] = so_far[n % 2]

        ctx0, probs0 = (B, B * PAIRS) if "A" in stages else (0, 0)
        marks = {}
        w_in_E = 16 * (("B" in stages) + ("C" in stages) + 2)

        block = ctx.enter_context(nc.Block())

        @block.tensor
        def _(pe):
            fillsV, fillsS = ringV.fills, ringS.fills

            def group(ring, out, pairs, waits=None):
                bank = ring.claim(pe)
                for k, (a, b) in enumerate(pairs):
                    if waits:
                        waits(k)
                    mm = nc.tensor.matmul(out(bank), a, b, start=(k == 0), stop=(k == len(pairs) - 1))
                ring.fill(mm)
                return mm

            def turn(name, src):
                for i in range(NT):
                    if name == "C2":
                        pe.wait_ge(boost_made, i + 1)
                    else:
                        norm = {"A": "A", "B": "B1", "B2": "B2"}.get(name, name)
                        pe.wait_ge(ln_rows, NT * NORMS.index(norm) + i + 1)
                    bank = ringV.claim(pe)
                    for c in range(C):
                        mm = nc.tensor.transpose(ps[:, bank, P * c:P * (c + 1)], src[:, i, P * c:P * (c + 1)], ident)
                    ringV.fill(mm)
                marks["turn " + name] = fillsV.n

            def all_emptied(*rings):
                for ring in rings:
                    pe.wait_ge(ring.emptied, ring.fills.off + ring.fills.n)

            def square(ring, w, rhs, outs=C, ins=C):
                for o in range(outs):
                    mm = group(ring, lambda k: ps[:, k, :], [(w[:, c, P * o:P * (o + 1)], rhs[:, c, :]) for c in range(ins)])
                return mm

            def to_rows(ring, lhs, w, i, ins=C):
                return group(ring, lambda k: ps[:, k, :], [(lhs[:, c, P * i:P * (i + 1)], w[:, c, :]) for c in range(ins)])

            pe.wait_ge(in_consts, 32)

            def stage_a():
                wq, wk, wv, wo = (slot(0, 2048 * j, 2048 * (j + 1), c=C) for j in range(4))
                turn("A", h_tok)
                pe.wait_ge(slot_in[0], filled_at[0])
                all_emptied(ringV)
                square(ringS, wq, hT)
                marks["q"] = fillsS.n

                def k_tile(i):
                    o, (lo, hi) = i // 4, CHUNKS[i % 4]
                    group(ringS, lambda k: ps[:, k, 0:hi - lo],
                          [(wk[:, c, P * o:P * (o + 1)], a_ctxT[:, c, lo:hi]) for c in range(C)])

                def v_tile(i):
                    group(ringS, lambda k: ps[:, k, :], [(a_ctxT[:, c, P * i:P * (i + 1)], wv[:, c, :]) for c in range(C)])

                def v_last():
                    for q in range(4):
                        group(ringV, lambda k: ps[0:LAST, k, 0:P],
                                   [(a_ctxT[:, c, S2 - LAST:S2], wv[:, c, P * q:P * (q + 1)]) for c in range(C)])

                def scores(p, j):
                    lo, hi = CHUNKS[j]
                    return group(ringV, lambda k: ps[:, k, 0:hi - lo], [(a_Qbd[:, p, :], a_KT[:, p // 2, lo:hi])])

                def turn_probs(b, p):
                    pe.wait_ge(probs_made, b * PAIRS + (p + 1))
                    for g in range(4):
                        ring = (ringS, ringV)[g % 2]
                        bank = ring.claim(pe)
                        for j, kt in enumerate(range(4 * g, min(4 * g + 4, KT_TILES))):
                            n = min(P, S2 - P * kt)
                            mm = nc.tensor.transpose(ps[0:n, bank, P * j:P * (j + 1)],
                                                     a_S[:, p % 2, P * kt:P * kt + n], ident)
                        ring.fill(mm)
                        turned_at[ring] = ring.fills.off + ring.fills.n

                turned_at = {}

                def weigh_values(p):
                    pe.wait_ge(ringS.emptied, turned_at[ringS])
                    pe.wait_ge(ringV.emptied, turned_at[ringV])
                    group(ringV, lambda k: ps[:, k, 0:2 * HD],
                          [(a_PT[0:min(P, S2 - P * kt), kt, :], a_V[0:min(P, S2 - P * kt), kt, 2 * HD * p:2 * HD * (p + 1)])
                           for kt in range(KT_TILES)])

                def one_batch(b, first):
                    pe.wait_ge(ctx_in, b * 16 + 16)
                    for i in range(4):
                        k_tile(i)
                    if not first:
                        turn_probs(b - 1, 6)
                    for i in range(4, 8):
                        k_tile(i)
                    if not first:
                        weigh_values(6)
                        turn_probs(b - 1, 7)
                    for i in range(8, 12):
                        k_tile(i)
                    if not first:
                        weigh_values(7)
                    for i in range(12, 16):
                        k_tile(i)
                    kt_at = fillsS.off + fillsS.n
                    pe.wait_ge(qbd_made, b * 4 + 4)
                    for i in range(12):
                        v_tile(i)
                        if i == 0:
                            pe.wait_ge(ringS.emptied, kt_at)
                        if i < 8:
                            scores(i // 4, i % 4)
                    v_last()
                    if first:
                        marks["ctxT read"] = fillsV.n
                    for p in range(6):
                        turn_probs(b, p)
                        for j in range(4):
                            scores(p + 2, j)
                        weigh_values(p)

                one_batch(0, True)
                with pe.Fori(1, B, 1) as b:
                    with fillsV.loop(b, 1, B - 1, 60), fillsS.loop(b, 1, B - 1, 44):
                        one_batch(b, False)
                pe.drain().then_inc(kt_free, 1)
                for p in (6, 7):
                    turn_probs(B - 1, p)
                    weigh_values(p)
                all_emptied(ringV)
                for c in range(C):
                    bank = ringS.claim(pe)
                    for b in range(B):
                        mm = nc.tensor.transpose(ps[:, bank, S * b:S * (b + 1)], a_attn[:, b, P * c:P * (c + 1)], ident[0:S, 0:S])
                    ringS.fill(mm)
                all_emptied(ringS)
                for i in range(NT):
                    to_rows(ringV, a_attnT, wo, i)
                pe.drain().then_inc(slot_free, 1)

            def stage_b():
                wk, wv, wr, wo = (slot(1, 2048 * j, 2048 * (j + 1), c=C) for j in range(4))
                turn("B", h_tok)
                pe.wait_ge(slot_in[1], filled_at[1])
                for j, (w, m) in enumerate(((wk, b_mk), (wv, b_mv), (wr, b_mr))):
                    pe.wait_ge(mix_made, C * (j + 1))
                    square(ringS, w, m)
                marks["kvr"] = fillsS.n
                pe.wait_ge(wkv_made, 1)
                for i in range(NT):
                    to_rows(ringV, b_t[1], wo, i)
                pe.drain().then_inc(slot_free, 1)
                turn("B2", h_tok)
                pe.wait_ge(slot_in[0], filled_at[2])
                wck = slot(2, 0, 8192, c=C)
                pe.wait_ge(mix_made, C * 4)
                marks["kk"] = fillsS.n
                square(ringS, wck, b_mk, outs=16)
                pe.drain().then_inc(slot_free, 1)
                pe.wait_ge(mix_made, C * 5)
                pe.wait_ge(stage_w_in, 16)
                pe.wait_ge(slot_in[1], filled_at[3])
                wcv = slot(3, 0, 8192, c=16)
                for i in range(NT):
                    to_rows(ringS, b_mv, b_wcr, i)
                pe.wait_ge(sq_made, 16)
                for i in range(NT):
                    to_rows(ringV, b_kk, wcv, i, ins=16)
                pe.drain().then_inc(slot_free, 1)

            def router(w):
                for i in range(NT):
                    group(ringV, lambda k: ps[:, k, 0:EXPERTS],
                          [(hT[:, c, P * i:P * (i + 1)], w[:, EXPERTS * c:EXPERTS * (c + 1)]) for c in range(C)])

            def expert_rows(hid, w2, chunks, made, hid_done):
                for i in range(NT):
                    group(ringV, lambda k: ps[:, k, :], [(hid[:, f, P * i:P * (i + 1)], w2[:, f, :]) for f in range(chunks)],
                          (lambda f: pe.wait_ge(made, hid_done + (f + 1))) if i == 0 else None)

            def stage_c():
                turn("C", h_tok)
                all_emptied(ringV)
                router(col("gate_W"))
                for k in range(2):
                    pe.wait_ge(oh_made, k + 1)
                    bank = ringV.claim(pe)
                    for i in range(NT):
                        mm = nc.tensor.transpose(ps[0:EXPERTS, bank, P * i:P * (i + 1)], c_oh[:, k, i, :], ident)
                    ringV.fill(mm)
                    all_emptied(ringV)
                    if k == 0:
                        pe.wait_ge(stage_w_in, 16 * (1 + ("B" in stages)))
                    for i in range(NT):
                        group(ringV, lambda b: ps[:, b, :], [(c_ohT[0:EXPERTS, P * i:P * (i + 1)], c_b2[0:EXPERTS])])
                    if k == 1:
                        turn("C2", c_hid[:, 0:NT, :])
                        all_emptied(ringV)
                    with pe.Fori(0, EXPERTS // 2, 1) as e:
                        with fillsV.loop(e, 0, EXPERTS // 2, 8), fillsS.loop(e, 0, EXPERTS // 2, 16):
                            for j in range(2):
                                pe.wait_ge(slot_in[j], e * 16 + filled_at[4 + 8 * k + j])
                                before = fillsS.off + fillsS.n
                                square(ringS, slot(j, 0, 4096, c=C), hT, outs=8)
                                expert_rows(c_hid, slot(j, 4096, 8192, c=8), 8, ringS.emptied, before)
                                pe.drain().then_inc(slot_free, 1)

            def stage_f():
                turn("F", h_tok)
                all_emptied(ringV)
                router(col("router"))
                def up(n):
                    w = slot(n, 0, 4096, c=C)
                    for f in range(4):
                        for ring, o in ((ringS, f), (ringV, f + 4)):
                            group(ring, lambda k: ps[:, k, :], [(w[:, c, P * o:P * (o + 1)], hT[:, c, :]) for c in range(C)])

                marks["F"] = fillsS.n
                with pe.Fori(0, EXPERTS // 2, 1) as e:
                    with fillsV.loop(e, 0, EXPERTS // 2, 16), fillsS.loop(e, 0, EXPERTS // 2, 8):
                        for j in range(2):
                            pe.wait_ge(slot_in[1 - j], e * 16 + filled_at[23 + j])
                            before = fillsV.off + fillsV.n
                            up(23 + j)
                            expert_rows(c_hid, slot(23 + j, 4096, 6144, c=4), 4, ringV.emptied, before)
                            pe.drain().then_inc(slot_free, 1)

            def stage_d():
                wq_c, wk_s, wk_c, wq_s = (slot(20, 2048 * j, 2048 * (j + 1), c=C) for j in range(4))
                wv_c, wv_s = (slot(21, 2048 * j, 2048 * (j + 1), c=C) for j in range(2))
                wg = slot(21, 4096, 8192, c=8)
                turn("D", h_tok)
                pe.wait_ge(slot_in[0], filled_at[20])
                all_emptied(ringV)
                square(ringS, wq_c, hT)
                square(ringS, wk_c, hT)
                all_emptied(ringS)
                square(ringS, wk_s, d_qcT)
                square(ringS, wq_s, d_kcT)
                marks["qk"] = fillsS.n
                pe.drain().then_inc(slot_free, 1)
                group(ringV, lambda k: ps[0:1, k, :], [(col("bq_s")[:, c:c + 1], d_kcT[:, c, :]) for c in range(C)])
                for b in range(B):
                    group(ringV, lambda k: ps[0:S, k, 0:1],
                          [(d_qcT[:, c, S * b:S * (b + 1)], col("bk_s")[:, c:c + 1]) for c in range(C)])
                pe.wait_ge(slot_in[1], filled_at[21])
                for b in range(B):
                    group(ringV, lambda k: ps[0:S, k, :],
                          [(hT[:, c, S * b:S * (b + 1)], wv_c[:, c, :]) for c in range(C)])
                all_emptied(ringS, ringV)
                pe.wait_ge(d_vectors, 1)

                with pe.Fori(0, B, 1) as b:
                    with fillsV.loop(b, 0, B, 8), fillsS.loop(b, 0, B, 4):
                        pe.wait_ge(qkb_made, b + 1)
                        pe.wait_ge(ctx_in, b * 16 + (16 * ctx0 + 16))
                        for lo, hi in CHUNKS:
                            group(ringV, lambda k: ps[0:S, k, 0:hi - lo],
                                  [(d_qk_b[:, c, :], d_ctxT[:, c, lo:hi]) for c in range(C)])
                        bank = ringV.claim(pe)
                        for c in range(C):
                            if c == 0:
                                pe.wait_ge(sel_made, b + 1)
                            nc.tensor.matmul(ps[:, bank, 0:S], d_sel[:, c, :], d_g2T[:, c, bass.ds(b * S, S)], start=(c == 0), stop=False)
                        mm = nc.tensor.matmul(ps[:, bank, 0:S], d_ones, d_bqk[:, bass.ds(b * S, S)], start=False, stop=True)
                        ringV.fill(mm)
                        pe.wait_ge(probs_made, b + (probs0 + 1))
                        held(pe)
                        for g in range(5):
                            ring = (ringS, ringV)[g % 2]
                            bank = ring.claim(pe)
                            held(pe)
                            for j, kt in enumerate(range(3 * g, min(3 * g + 3, KT_TILES))):
                                n = min(P, S2 - P * kt)
                                mm = nc.tensor.transpose(ps[0:n, bank, S * j:S * (j + 1)], d_S[:, P * kt:P * kt + n], ident[0:S, 0:S])
                            ring.fill(mm)
                        pe.wait_ge(s2_made, b + 1)
                        group(ringS, lambda k: ps[0:S, k, 0:S], [(d_P2, col("interp"))])
                        all_emptied(ringS, ringV)
                        pe.wait_ge(ctxn_in, b * 32 + 32)
                        group(ringV, lambda k: ps[0:S, k, :],
                                   [(d_PT[0:min(P, S2 - P * kt), kt, :], d_ctx[0:min(P, S2 - P * kt), kt, :])
                               for kt in range(KT_TILES)])
                marks["D loop end"] = fillsV.n
                all_emptied(ringV)
                for c in range(C):
                    bank = ringS.claim(pe)
                    for b in range(B):
                        mm = nc.tensor.transpose(ps[:, bank, S * b:S * (b + 1)], d_pc[:, b, P * c:P * (c + 1)], ident[0:S, 0:S])
                    ringS.fill(mm)
                for c in range(C):
                    bank = ringS.claim(pe)
                    for b in range(B):
                        mm = nc.tensor.matmul(ps[:, bank, S * b:S * (b + 1)], d_Vc[:, b, P * c:P * (c + 1)], d_P2T[:, b, :],
                                              start=(b == 0), stop=(b == B - 1), skip_group_check=True)
                    ringS.fill(mm)
                all_emptied(ringS)
                square(ringS, wv_s, d_pcT)
                all_emptied(ringS)
                for o in range(C):
                    group(ringS, lambda k: ps[:, k, :],
                          [(wg[:, c, P * o:P * (o + 1)], (d_c2s, d_s2c)[c // 4][:, c % 4, :]) for c in range(8)])
                marks["gate end"] = fillsS.n
                pe.drain().then_inc(slot_free, 1)
                pe.wait_ge(gated_made, 1)
                for i in range(NT):
                    bank = ringV.claim(pe)
                    for c in range(C):
                        mm = nc.tensor.transpose(ps[:, bank, P * c:P * (c + 1)], d_gate[:, c, P * i:P * (i + 1)], ident)
                    ringV.fill(mm)

            def stage_e():
                w_in, w_out = slot(22, 0, 4096, c=C), slot(22, 4096, 8192, c=8)
                turn("E", h_tok)
                pe.wait_ge(slot_in[0], filled_at[22])
                all_emptied(ringV)
                marks["conv"] = fillsV.n
                square(ringV, w_in, hT, outs=8)
                pe.wait_ge(stage_w_in, w_in_E)
                pe.wait_ge(xv_made, 8)
                group(ringS, lambda k: ps[0:S, k, :], [(e_wx[:, c, :], e_xv[:, c, :]) for c in range(8)])
                all_emptied(ringS)
                for c in range(8):
                    group(ringS, lambda k: ps[:, k, :], [(e_wdt[0:RANK, P * c:P * (c + 1)], e_ssm[0:RANK, :])])
                marks["dt"] = fillsS.n
                for n in range(2 * NS):
                    group(ringS, lambda k: ps[:, k, :],
                          [(ident[0:S, RANK + n:RANK + n + 1].broadcast_to([S, P]), e_ssm[0:S, :])])
                marks["bc"] = fillsS.n
                pe.wait_ge(ringV.emptied, fillsV.n)
                for c in range(8):
                    if c >= 4:
                        pe.wait_ge(y_taken, c - 3)
                    for g in range(NS // G):
                        pe.wait_ge(hc_made, c * (NS // G) + g + 1)
                        for n in range(G):
                            mm = nc.tensor.matmul(ps[:, c % 4, :], ident, e_hC[:, g % 2, N * n:N * (n + 1)],
                                                  start=(g == 0 and n == 0), stop=(g == NS // G - 1 and n == G - 1))
                        mm.then_inc(y_made, 1)
                pe.wait_ge(y_taken, 8)
                for i in range(NT):
                    to_rows(ringV, e_dx, w_out, i, ins=8)
                pe.drain().then_inc(slot_free, 1)

            for st, run, n in (("A", stage_a, 1), ("B", stage_b, 3), ("C", stage_c, 16), ("D", stage_d, 2), ("E", stage_e, 1),
                               ("F", stage_f, 8)):
                if st in stages:
                    run()
                else:
                    pe.sem_inc(slot_free, n)
                    if st == "A":
                        pe.sem_inc(kt_free, 1)


        @block.scalar
        def _(act):
            takes = ringS.takes
            norms = [0]

            def norm():
                norms[0] += 1
                act.wait_ge(ln_var, norms[0])
                nc.scalar.activation(ln_sd, ln_mv[:, :, 1], ACT.Sqrt, bias=ln_eps).then_inc(ln_std, 1)

            def from_bank(out, part, func, **kw):
                bank = ringS.take(act)
                ringS.empty(nc.scalar.activation(out, part(bank), func, **kw))

            def whole(k):
                return ps[:, k, :]

            act.wait_ge(in_consts, 32)
            act.wait_ge(eps_made, 1)

            def stage_a():
                norm()
                for o in range(C):
                    from_bank(a_QT[:, o, :], whole, ACT.Copy, scale=float(HD) ** -0.5)

                def k_tile(i):
                    o, (lo, hi) = i // 4, CHUNKS[i % 4]
                    from_bank(a_KT[:, o, lo:hi], lambda k: ps[:, k, 0:hi - lo], ACT.Copy)

                def turn_probs():
                    for g in (0, 2):
                        from_bank(a_PT[:, 4 * g:4 * g + 4, :], lambda k: ps[:, k, :].rearrange("p (j n) -> p j n", j=4),
                                  ACT.Copy)

                def exps(b, p):
                    act.wait_ge(row_max, b * PAIRS + (p + 1))
                    nc.scalar.activation(a_S[:, p % 2, :], a_S[:, p % 2, :], ACT.Exp, bias=a_nm[:, p:p + 1],
                                         accum_out=a_rs[:, p:p + 1]).then_inc(probs_made, 1)

                def one_batch(b, first):
                    for i in range(4):
                        k_tile(i)
                    if not first:
                        turn_probs()
                    for i in range(4, 8):
                        k_tile(i)
                    if not first:
                        turn_probs()
                    for i in range(8, 16):
                        k_tile(i)
                    for i in range(12):
                        from_bank(a_V[:, i, :], whole, ACT.Copy)
                        if i == 5:
                            exps(b, 0)
                        if i == 9:
                            exps(b, 1)
                    for p in range(6):
                        turn_probs()
                        exps(b, p + 2)

                one_batch(0, True)
                with act.Fori(1, B, 1) as b:
                    with takes.loop(b, 1, B - 1, 44):
                        one_batch(b, False)
                turn_probs()
                turn_probs()
                for c in range(C):
                    from_bank(a_attnT[:, c, :], whole, ACT.Copy)

            def stage_b():
                nc.scalar.activation(b_w, col("decay"), ACT.Exp).then_inc(wkv_exp, 1)
                norm()
                norm()

                def halves(mixes, mark):
                    act.wait_ge(ringV.emptied, marks[mark])
                    for name, dst in mixes:
                        for c in range(C):
                            nc.scalar.activation(dst[:, c, :], b_xxT[:, c, :], ACT.Copy, scale=col(name)[:, c:c + 1]) \
                                .then_inc(mix_half, 1)

                halves([("mix_k", b_mk), ("mix_v", b_mv), ("mix_r", b_mr)], "turn B")

                def by_time(k):
                    return ps[:, k, :].rearrange("p (t s) -> p t s", t=B)

                for dst, func, scale in ((b_k, ACT.Copy, 1.0), (b_v, ACT.Copy, 1.0), (b_r, ACT.Exp, -1.0)):
                    for c in range(C):
                        from_bank(dst[:, c, :].rearrange("p (s t) -> p t s", t=B), by_time, func, scale=scale)
                for k, buf in enumerate((2, 3, 4, 5)):
                    act.wait_ge(wkv_arg, k + 1)
                    v = flat(b_t[buf])
                    nc.scalar.activation(v, v, ACT.Exp).then_inc(wkv_exp, 1)
                norm()
                halves([("cmix_k", b_mk), ("cmix_r", b_mv)], "turn B2")
                for f in range(16):
                    from_bank(b_kk[:, f, :], whole, ACT.Relu)
                for i in range(NT):
                    from_bank(b_t[4][:, i, :], whole, ACT.Exp, scale=-1.0)

            gates = [0]

            def gate_exps():
                gates[0] += 1
                act.wait_ge(gate_arg, gates[0])
                for i in range(NT):
                    nc.scalar.activation(c_e8[:, i, :], c_m8[:, i, :], ACT.Exp, bias=c_nmx[:, i:i + 1],
                                         accum_out=c_sum[:, i:i + 1]).then_inc(gate_exp, 1)

            def stage_c():
                norm()
                gate_exps()
                for k in range(2):
                    with act.Fori(0, EXPERTS // 2, 1) as e:
                        with takes.loop(e, 0, EXPERTS // 2, 16):
                            for j in range(2):
                                for f in range(8):
                                    from_bank(c_hid[:, f, :], whole, ACT.Relu, bias=wbuf[:, j, 8192 + f:8193 + f])
                norm()

            def stage_d():
                norm()
                for dst, bias in ((d_qcT, "bq_c"), (d_kcT, "bk_c")):
                    for c in range(C):
                        from_bank(dst[:, c, :], whole, ACT.Identity, bias=col(bias)[:, c:c + 1])
                for dst in (d_qkT, d_g2T):
                    for c in range(C):
                        from_bank(dst[:, c, :], whole, ACT.Copy)
                with act.Fori(0, B, 1) as b:
                    with takes.loop(b, 0, B, 4):
                        act.wait_ge(row_max, b + (probs0 + 1))
                        nc.scalar.activation(d_S, d_S, ACT.Exp, bias=d_nm[0:S, 0:1],
                                             accum_out=d_rs[0:S, 0:1]).then_inc(probs_made, 1)
                        act.wait_ge(s2_arg, b + 1)
                        nc.scalar.activation(d_P2, d_P2, ACT.Exp, bias=d_nm[:, 1:2],
                                             accum_out=d_rs[:, 1:2]).then_inc(s2_exp, 1)
                        for g in (0, 2):
                            from_bank(d_PT[:, 3 * g:3 * g + 3, :],
                                      lambda k: ps[:, k, 0:3 * S].rearrange("p (j n) -> p j n", j=3), ACT.Copy)
                        from_bank(d_PT[0:LAST, KT_TILES - 1, :], lambda k: ps[0:LAST, k, 0:S], ACT.Copy)
                        from_bank(d_P2T[:, b, :], lambda k: ps[0:S, k, 0:S], ACT.Copy)
                for dst in (d_pcT, d_s2c):
                    for c in range(C):
                        from_bank(dst[:, c, :], whole, ACT.Copy)
                for c in range(C):
                    from_bank(d_c2s[:, c, :], whole, ACT.Identity, bias=col("bv_s")[:, c:c + 1])
                act.wait_ge(nbg_made, 1)
                for c in range(C):
                    from_bank(d_gate[:, c, :], whole, ACT.Exp, scale=-1.0, bias=d_nbg[:, c:c + 1])

            def stage_e():
                nc.scalar.activation(e_negA, col("A_log"), ACT.Exp).then_inc(neg_a, 1)
                norm()
                for c in range(8):
                    act.wait_ge(ringV.emptied, marks["conv"] + c + 1)
                    nc.scalar.activation(e_de[:, c, :], e_dx[:, c, :], ACT.Exp, scale=-1.0).then_inc(conv_exp, 1)
                from_bank(e_ssm[0:S], lambda k: ps[0:S, k, :], ACT.Copy)
                for c in range(8):
                    from_bank(e_de[:, c, :], whole, ACT.Identity, bias=col("b_dt")[:, c:c + 1])
                act.wait_ge(dt_arg, 1)
                nc.scalar.activation(flat(e_dx), flat(e_dx), ACT.Exp).then_inc(dt_exp, 1)
                act.wait_ge(dt_arg, 2)
                nc.scalar.activation(flat(e_h), flat(e_dA), ACT.Ln).then_inc(dt_exp, 1)
                for n in range(NS):
                    from_bank(e_B[:, N * n:N * (n + 1)], whole, ACT.Copy)
                for n in range(NS):
                    from_bank(e_C[n // 8][:, N * (n % 8):N * (n % 8 + 1)], whole, ACT.Copy)
                act.wait_ge(delta_made, 1)
                act.wait_ge(neg_a, 2)
                for c in range(8):
                    for g in range(NS // G):
                        k = c * (NS // G) + g
                        if k >= 2:
                            act.wait_ge(h_made, k - 1)
                        for n in range(G):
                            a = NS * c + G * g + n
                            ins = nc.scalar.activation(e_dA[:, g % 2, N * n:N * (n + 1)], e_de[:, c, :], ACT.Exp,
                                                       scale=e_negA[:, a:a + 1])
                        ins.then_inc(da_made, 1)

            def stage_f():
                norm()
                gate_exps()
                with act.Fori(0, EXPERTS // 2, 1) as e:
                    with takes.loop(e, 0, EXPERTS // 2, 8):
                        for j in range(2):
                            for f in range(4):
                                bank = ringS.take(act)
                                nc.scalar.activation(c_h1[:, f, :], ps[:, bank, :], ACT.Copy)
                                ringS.empty(nc.scalar.activation(c_e[:, f, :], ps[:, bank, :], ACT.Exp, scale=-1.0))

            for st, run in (("A", stage_a), ("B", stage_b), ("C", stage_c), ("D", stage_d), ("E", stage_e), ("F", stage_f)):
                if st in stages:
                    run()

        @block.gpsimd
        def _(pool):
            chain = Chain(pool, pool_done)
            pool.wait_ge(in_consts, 32)

            def stage_a():
                def one_batch(b, first):
                    pool.wait_ge(pos_in, b * 64 + 64)
                    held(pool)
                    nc.gpsimd.tensor_scalar(a_dist, a_dist.bitcast(I32), a_qpos.bitcast(I32), None, ALU.subtract)
                    chain.link(nc.gpsimd.tensor_scalar(a_mask, a_mask.bitcast(I32), 0.0, -1e30, ALU.is_equal, ALU.mult))
                    chain.link(nc.gpsimd.tensor_tensor(a_dist, a_dist, a_mask, ALU.add))
                    for p in range(PAIRS):
                        if not first or p >= 2:
                            pool.wait_ge(row_max, b * PAIRS + (p - 1))
                            held(pool)
                        nc.gpsimd.tensor_scalar(a_bias[:, p % 2, :], a_dist, col("slopes")[:, p:p + 1], None,
                                                ALU.mult).then_inc(bias_made, 1)

                one_batch(0, True)
                with pool.Fori(1, B, 1) as b:
                    with chain.loop(b, 1, B - 1, 2):
                        one_batch(b, False)

            def stage_e():
                pool.wait_ge(ringS.emptied, marks["bc"])
                for k in range(8 * NS // G):
                    g = k % (NS // G)
                    pool.wait_ge(h_made, k + 1)
                    if k >= 2:
                        pool.wait_ge(y_made, k - 1)
                    c_rows = e_C[g // 2][:, G * N * (g % 2):G * N * (g % 2 + 1)]
                    nc.gpsimd.tensor_tensor(e_hC[:, g % 2, :], e_h[:, g % 2, :], c_rows, ALU.mult).then_inc(hc_made, 1)

            def stage_d():
                def pick(b):
                    pool.wait_ge(ctx_in, b * 16 + (16 * ctx0 + 16))
                    held(pool)
                    rows_of = d_ctxT[:, :, 0:S * STRIDE].rearrange("p c (i r) -> p c i r", r=STRIDE)
                    for k in range(2):
                        ins = nc.gpsimd.tensor_copy(d_sel[:, :, S * k:S * (k + 1)], rows_of[:, :, :, PICK + k])
                    ins.then_inc(sel_made, 1)

                pick(0)
                with pool.Fori(1, B, 1) as b:
                    pool.wait_ge(s2_arg, b)
                    pick(b)

            if "A" in stages:
                stage_a()
            if "D" in stages:
                stage_d()
            if "E" in stages:
                stage_e()

        @block.vector
        def _(dve):
            V = nc.vector
            chain = Chain(dve, dve_done)
            link = chain.link
            takes = ringV.takes
            norms = [0]
            halves_seen = [0]

            def own():
                dve.wait_ge(ringV.emptied, takes.off + takes.n)

            def norm(src, dst):
                for i in range(NT):
                    chain.done(V.bn_stats(ln_st[:, 6 * i:6 * i + 6], src[:, i, :]))
                chain.wait()
                for i in range(NT):
                    ins = V.bn_aggr(ln_mv[:, i, :], ln_st[:, 6 * i:6 * i + 6])
                ins.then_inc(ln_var, 1)
                norms[0] += 1
                dve.wait_ge(ln_std, norms[0])
                link(V.reciprocal(ln_rstd, ln_sd))
                for i in range(NT):
                    V.tensor_scalar(dst[:, i, :], src[:, i, :], ln_mv[:, i, 0:1], ln_rstd[:, i:i + 1],
                                    ALU.subtract, ALU.mult).then_inc(ln_rows, 1)

            def own_rows():
                dve.wait_ge(ln_rows, NT * norms[0])

            def turned(dst, gain=None):
                for i in range(NT):
                    bank = ringV.take(dve)
                    if gain is None:
                        ins = V.tensor_copy(dst[:, :, P * i:P * (i + 1)], ps[:, bank, :].rearrange("p (c n) -> p c n", c=C))
                    else:
                        for c in range(C):
                            ins = V.tensor_scalar(dst[:, c, P * i:P * (i + 1)], ps[:, bank, P * c:P * (c + 1)],
                                                  col(gain + "_g")[:, c:c + 1], col(gain + "_b")[:, c:c + 1],
                                                  ALU.mult, ALU.add)
                    ringV.empty(ins)

            link(V.memset(ln_eps, 1e-5))
            V.memset(a_Qbd, 0.0).then_inc(eps_made, 1)
            dve.wait_ge(eps_made, 1)
            dve.wait_ge(in_consts, 32)
            dve.wait_ge(in_x, 16)

            def stage_a():
                norm(x, h_tok)
                turned(hT)

                def turn_probs():
                    bank = ringV.take(dve)
                    ringV.empty(V.tensor_copy(a_PT[:, 4:8, :], ps[:, bank, :].rearrange("p (j n) -> p j n", j=4)))
                    bank = ringV.take(dve)
                    ringV.empty(V.tensor_copy(a_PT[0:LAST, 12, :], ps[0:LAST, bank, 0:P]))

                def scores(b, p, first):
                    if not first or p:
                        dve.wait_ge(row_max, b * PAIRS + p)
                    dve.wait_ge(bias_made, b * PAIRS + (p + 1))
                    for j, (lo, hi) in enumerate(CHUNKS):
                        bank = ringV.take(dve)
                        held(dve)
                        ringV.empty(V.tensor_tensor_reduce(a_S[:, p % 2, lo:hi], ps[:, bank, 0:hi - lo],
                                                           a_bias[:, p % 2, lo:hi], 1.0, -3e38, ALU.add, ALU.max,
                                                           a_mx[:, j:j + 1]))
                    own()
                    V.tensor_reduce(a_nm[:, p:p + 1], a_mx, AX_X, ALU.max, negate=True).then_inc(row_max, 1)

                def heads_out(b, p):
                    rd = a_rd[:, p:p + 1]
                    link(V.tensor_scalar(rd, a_rs[:, p:p + 1], 1.0, None, ALU.add))
                    link(V.reciprocal(rd, rd))
                    bank = ringV.take(dve)
                    at = 2 * HD * p
                    V.tensor_scalar(a_attn[:, b, at:at + HD], ps[0:S, bank, 0:HD], rd[0:S], None, ALU.mult)
                    ringV.empty(V.tensor_scalar(a_attn[:, b, at + HD:at + 2 * HD], ps[S:P, bank, HD:2 * HD], rd[S:P],
                                                None, ALU.mult))

                def one_batch(b, first):
                    if not first:
                        for p in (6, 7):
                            turn_probs()
                            heads_out(b - 1, p)
                    for r in range(4):
                        dst = a_Qbd[HD * r:HD * (r + 1), :, S * (r % 2):S * (r % 2 + 1)] \
                            .rearrange("p (c k) n -> p k c n", k=2)[:, r // 2]
                        V.tensor_copy(dst, a_QT[HD * r:HD * (r + 1), :, bass.ds(b * S, S)]).then_inc(qbd_made, 1)
                    scores(b, 0, first)
                    scores(b, 1, first)
                    for q in range(4):
                        bank = ringV.take(dve)
                        ringV.empty(V.tensor_copy(a_V[0:LAST, KT_TILES - 1, P * q:P * (q + 1)], ps[0:LAST, bank, 0:P]))
                    for p in range(6):
                        turn_probs()
                        scores(b, p + 2, first)
                        heads_out(b, p)

                dve.wait_ge(ringS.emptied, marks["q"])
                one_batch(0, True)
                with dve.Fori(1, B, 1) as b:
                    with takes.loop(b, 1, B - 1, 60), chain.loop(b, 1, B - 1, 16):
                        one_batch(b, False)
                for p in (6, 7):
                    turn_probs()
                    heads_out(B - 1, p)
                for i in range(NT):
                    bank = ringV.take(dve)
                    ringV.empty(V.tensor_tensor(x[:, i, :], x[:, i, :], ps[:, bank, :], ALU.add))
                own()

            def stage_b():
                norm(x, b_h1)
                own_rows()
                norm(b_h1, h_tok)
                V.tensor_scalar(b_omk[:, 0:12], cols[:, COLS["mix_k"][0]:COLS["mix_k"][0] + 12], -1.0, 1.0, ALU.mult, ALU.add)
                link(V.tensor_scalar(b_omk[:, 12:20], cols[:, COLS["cmix_k"][0]:COLS["cmix_k"][0] + 8], -1.0, 1.0,
                                     ALU.mult, ALU.add))
                turned(b_xxT, "ln1")

                def mixes(first, dsts):
                    own()
                    for j, dst in enumerate(dsts):
                        for c in range(C):
                            halves_seen[0] += 1
                            dve.wait_ge(mix_half, halves_seen[0])
                            k = 4 * (first + j) + c
                            V.scalar_tensor_tensor(out=dst[:, c, S:], in0=b_xxT[:, c, 0:N - S], scalar=b_omk[:, k:k + 1],
                                                   in1=dst[:, c, S:], op0=ALU.mult, op1=ALU.add).then_inc(mix_made, 1)

                mixes(0, (b_mk, b_mv, b_mr))

                PN, PP, E1p, E2p, E1, E2, NUM, DEN = b_t
                dve.wait_ge(wkv_exp, 1)
                link(V.tensor_scalar(b_w, b_w, -1.0, None, ALU.mult))
                dve.wait_ge(ringS.emptied, marks["kvr"])
                for c in range(C):
                    chain.done(V.tensor_scalar(DEN[:, c, :], b_k[:, c, :], 0.0, b_w[:, c:c + 1], ALU.mult, ALU.add))
                chain.wait()
                link(V.memset(timed(DEN)[:, :, 0:1], -BIG))
                link(V.tensor_tensor_scan(flat(PN), flat(DEN), flat(b_k), -BIG, ALU.add, ALU.max))
                chain.done(V.memset(timed(PP)[:, :, 0:1], -BIG))
                link(V.tensor_copy(timed(PP)[:, :, 1:], timed(PN)[:, :, 0:B - 1]))
                for c in range(C):
                    ins = V.scalar_tensor_tensor(out=E1p[:, c, :], in0=PP[:, c, :], scalar=b_w[:, c:c + 1], in1=PN[:, c, :],
                                                 op0=ALU.add, op1=ALU.subtract)
                ins.then_inc(wkv_arg, 1)
                V.tensor_tensor(flat(E2p), flat(b_k), flat(PN), ALU.subtract).then_inc(wkv_arg, 1)
                first = col("first")
                for c in range(C):
                    chain.done(V.scalar_tensor_tensor(out=NUM[:, c, :], in0=b_k[:, c, :], scalar=first[:, c:c + 1],
                                                      in1=PP[:, c, :], op0=ALU.add, op1=ALU.max))
                chain.wait()
                V.tensor_tensor(flat(E1), flat(PP), flat(NUM), ALU.subtract).then_inc(wkv_arg, 1)
                for c in range(C):
                    ins = V.scalar_tensor_tensor(out=E2[:, c, :], in0=b_k[:, c, :], scalar=first[:, c:c + 1],
                                                 in1=NUM[:, c, :], op0=ALU.add, op1=ALU.subtract)
                ins.then_inc(wkv_arg, 1)
                dve.wait_ge(wkv_arg, 4)
                dve.wait_ge(wkv_exp, 3)
                link(V.tensor_tensor(flat(NUM), flat(E2p), flat(b_v), ALU.mult))
                link(V.tensor_tensor_scan(flat(PN), flat(E1p), flat(NUM), 0.0, ALU.mult, ALU.add))
                link(V.tensor_tensor_scan(flat(DEN), flat(E1p), flat(E2p), 0.0, ALU.mult, ALU.add))
                dve.wait_ge(wkv_exp, 5)
                link(V.tensor_tensor(flat(NUM), flat(E2), flat(b_v), ALU.mult))
                for acc, out in ((PN, NUM), (DEN, E2)):
                    link(V.tensor_tensor(timed(E1p)[:, :, 1:], timed(E1)[:, :, 1:], timed(acc)[:, :, 0:B - 1], ALU.mult))
                    link(V.tensor_tensor(timed(out)[:, :, 1:], timed(out)[:, :, 1:], timed(E1p)[:, :, 1:], ALU.add))
                link(V.tensor_scalar(flat(b_r), flat(b_r), 1.0, None, ALU.add))
                link(V.tensor_tensor(flat(E2), flat(E2), flat(b_r), ALU.mult))
                link(V.reciprocal(flat(E2), flat(E2)))
                for c in range(C):
                    ins = V.tensor_tensor(b_mk[:, c, :].rearrange("p (t s) -> p s t", t=B),
                                          NUM[:, c, :].rearrange("p (s t) -> p s t", t=B),
                                          E2[:, c, :].rearrange("p (s t) -> p s t", t=B), ALU.mult)
                ins.then_inc(wkv_made, 1)
                for i in range(NT):
                    bank = ringV.take(dve)
                    ringV.empty(V.tensor_tensor(b_h1[:, i, :], b_h1[:, i, :], ps[:, bank, :], ALU.add))
                own()
                norm(b_h1, h_tok)
                turned(b_xxT, "ln2")
                mixes(3, (b_mk, b_mv))
                for f in range(16):
                    dve.wait_ge(ringS.emptied, marks["kk"] + f + 1)
                    V.tensor_tensor(b_kk[:, f, :], b_kk[:, f, :], b_kk[:, f, :], ALU.mult).then_inc(sq_made, 1)
                dve.wait_ge(ringS.emptied, marks["kk"] + 16 + NT)
                rr = b_t[4]
                link(V.tensor_scalar(flat(rr), flat(rr), 1.0, None, ALU.add))
                link(V.reciprocal(flat(rr), flat(rr)))
                for i in range(NT):
                    chain.done(V.tensor_tensor(x[:, i, :], x[:, i, :], b_h1[:, i, :], ALU.add))
                    bank = ringV.take(dve)
                    ringV.empty(V.tensor_tensor(rr[:, i, :], rr[:, i, :], ps[:, bank, :], ALU.mult))
                    own()
                    chain.wait()
                    link(V.tensor_tensor(x[:, i, :], x[:, i, :], rr[:, i, :], ALU.add))

            gates = [0]

            def route(bias):
                for i in range(NT):
                    bank = ringV.take(dve)
                    if bias:
                        ins = V.tensor_tensor(c_lg[:, i, :], ps[:, bank, 0:EXPERTS], row("gate_b", EXPERTS), ALU.add)
                    else:
                        ins = V.tensor_copy(c_lg[:, i, :], ps[:, bank, 0:EXPERTS])
                    ringV.empty(ins)
                own()
                for i in range(NT):
                    link(V.max(c_m8[:, i, :], c_lg[:, i, :]))
                    chain.done(V.max_index(c_ix[:, i, :].bitcast(U32), c_m8[:, i, :], c_lg[:, i, :]))
                chain.wait()
                V.tensor_scalar(c_nmx, c_m8[:, :, 0], -1.0, None, ALU.mult).then_inc(gate_arg, 1)
                link(V.tensor_copy(c_ixf, c_ix.bitcast(U32)))
                for k in range(2):
                    for i in range(NT):
                        ins = V.tensor_scalar(c_oh[:, k, i, :], col("iota"), c_ixf[:, i, k:k + 1], None, ALU.is_equal)
                    link(ins)
                    V.tensor_copy(c_sum[:, 0:0 + 1], c_sum[:, 0:0 + 1]) if False else None
                gates[0] += 1
                dve.wait_ge(gate_exp, NT * gates[0])

            def add_expert(k, j, e):
                link(V.tensor_copy(c_gate_e[:, j, :], c_oh[:, k, :, bass.ds(e * 2 + j, 1)].rearrange("p t o -> p (t o)")))
                own()

            def weighted_rows(j):
                for i in range(NT):
                    bank = ringV.take(dve)
                    ringV.empty(V.scalar_tensor_tensor(out=c_acc[:, i, :], in0=ps[:, bank, :], scalar=c_gate_e[:, j, i:i + 1],
                                                       in1=c_acc[:, i, :], op0=ALU.mult, op1=ALU.add))

            def stage_c():
                norm(x, h_tok)
                turned(hT)
                route(True)
                V.drain().then_inc(oh_made, 1)
                link(V.reciprocal(c_sum, c_sum))
                for k in range(2):
                    chain.done(V.tensor_tensor(c_w[:, 4 * k:4 * k + 4], c_e8[:, :, k], c_sum, ALU.mult))
                chain.wait()
                for k in range(2):
                    bank = ringV.take(dve)
                    ringV.empty(V.tensor_copy(c_ohT[0:EXPERTS], ps[0:EXPERTS, bank, :]))
                    for i in range(NT):
                        bank = ringV.take(dve)
                        ringV.empty(V.tensor_copy(c_acc[:, i, :], ps[:, bank, :]))
                    if k == 1:
                        turned(hT)
                    with dve.Fori(0, EXPERTS // 2, 1) as e:
                        with takes.loop(e, 0, EXPERTS // 2, 8), chain.loop(e, 0, EXPERTS // 2, 2):
                            for j in range(2):
                                add_expert(k, j, e)
                                weighted_rows(j)
                    own()
                    for i in range(NT):
                        if k == 0:
                            V.scalar_tensor_tensor(out=c_hid[:, i, :], in0=c_acc[:, i, :], scalar=0.5, in1=h_tok[:, i, :],
                                                   op0=ALU.mult, op1=ALU.add).then_inc(boost_made, 1)
                        prior = (h_tok, c_res)[k]
                        chain.done(V.scalar_tensor_tensor(out=c_res[:, i, :], in0=c_acc[:, i, :],
                                                          scalar=c_w[:, 4 * k + i:4 * k + i + 1], in1=prior[:, i, :],
                                                          op0=ALU.mult, op1=ALU.add))
                    chain.wait()
                    if k == 0:
                        V.drain().then_inc(oh_made, 1)
                norm(c_res, c_acc)
                own_rows()
                for i in range(NT):
                    link(V.tensor_tensor(c_acc[:, i, :], c_acc[:, i, :], row("gamma"), ALU.mult))
                    link(V.tensor_tensor(c_acc[:, i, :], c_acc[:, i, :], row("beta"), ALU.add))
                    link(V.tensor_tensor(x[:, i, :], x[:, i, :], c_acc[:, i, :], ALU.add))

            def stage_f():
                norm(x, h_tok)
                turned(hT)
                route(False)
                sums = c_sum
                link(V.tensor_tensor(sums, c_e8[:, :, 0], c_e8[:, :, 1], ALU.add))
                link(V.reciprocal(sums, sums))
                for k in range(2):
                    chain.done(V.tensor_tensor(c_w[:, 4 * k:4 * k + 4], c_e8[:, :, k], sums, ALU.mult))
                chain.wait()
                for i in range(NT):
                    link(V.tensor_scalar(c_oh[:, 2, i, :], c_oh[:, 0, i, :], c_w[:, i:i + 1], None, ALU.mult))
                    link(V.scalar_tensor_tensor(out=c_oh[:, 2, i, :], in0=c_oh[:, 1, i, :], scalar=c_w[:, 4 + i:5 + i],
                                                in1=c_oh[:, 2, i, :], op0=ALU.mult, op1=ALU.add))
                link(V.memset(c_acc, 0.0))
                with dve.Fori(0, EXPERTS // 2, 1) as e:
                    with takes.loop(e, 0, EXPERTS // 2, 16), chain.loop(e, 0, EXPERTS // 2, 26):
                        for j in range(2):
                            for f in range(4):
                                dve.wait_ge(ringS.emptied, e * 8 + (marks["F"] + 4 * j + f + 1))
                                link(V.tensor_scalar(c_e[:, f, :], c_e[:, f, :], 1.0, None, ALU.add))
                                link(V.reciprocal(c_e[:, f, :], c_e[:, f, :]))
                                link(V.tensor_tensor(c_e[:, f, :], c_e[:, f, :], c_h1[:, f, :], ALU.mult))
                                bank = ringV.take(dve)
                                ringV.empty(V.tensor_tensor(c_hid[:, f, :], c_e[:, f, :], ps[:, bank, :], ALU.mult))
                            add_expert(2, j, e)
                            weighted_rows(j)
                own()
                for i in range(NT):
                    link(V.tensor_tensor(x[:, i, :], x[:, i, :], c_acc[:, i, :], ALU.add))

            def stage_d():
                scale = float(D) ** -0.5
                V.tensor_scalar(d_nbg, col("bg"), -1.0, None, ALU.mult).then_inc(nbg_made, 1)
                norm(x, h_tok)
                V.memset(d_ones, 1.0).then_inc(d_vectors, 1)
                turned(hT)
                bank = ringV.take(dve)
                ringV.empty(V.tensor_copy(d_bqk, ps[0:1, bank, :]))
                for b in range(B):
                    bank = ringV.take(dve)
                    ringV.empty(V.tensor_copy(d_qbk[0:S, b:b + 1], ps[0:S, bank, 0:1]))
                for b in range(B):
                    bank = ringV.take(dve)
                    ringV.empty(V.tensor_tensor(d_Vc[:, b, :], ps[0:S, bank, :], row("bv_c")[0:S], ALU.add))
                own()
                dve.wait_ge(ringS.emptied, marks["qk"])
                with dve.Fori(0, B, 1) as b:
                    with takes.loop(b, 0, B, 8), chain.loop(b, 0, B, 3):
                        V.tensor_copy(d_qk_b, d_qkT[:, :, bass.ds(b * S, S)]).then_inc(qkb_made, 1)
                        link(V.tensor_copy(d_qb1[0:S], d_qbk[0:S, bass.ds(b, 1)]))
                        for lo, hi in CHUNKS:
                            bank = ringV.take(dve)
                            ringV.empty(V.tensor_scalar(d_S[:, lo:hi], ps[0:S, bank, 0:hi - lo], d_qb1[0:S], scale,
                                                        ALU.add, ALU.mult))
                        own()
                        V.tensor_reduce(d_nm[0:S, 0:1], d_S, AX_X, ALU.max, negate=True).then_inc(row_max, 1)
                        bank = ringV.take(dve)
                        ringV.empty(V.tensor_scalar(d_P2, ps[:, bank, 0:S], scale, None, ALU.mult))
                        own()
                        V.tensor_reduce(d_nm[:, 1:2], d_P2, AX_X, ALU.max, negate=True).then_inc(s2_arg, 1)
                        dve.wait_ge(s2_exp, b + 1)
                        chain.done(V.reciprocal(d_rd[0:S, 0:1], d_rs[0:S, 0:1]))
                        link(V.reciprocal(d_rd[:, 1:2], d_rs[:, 1:2]))
                        V.tensor_scalar(d_P2, d_P2, d_rd[:, 1:2], None, ALU.mult).then_inc(s2_made, 1)
                        for g in (1, 3):
                            bank = ringV.take(dve)
                            ringV.empty(V.tensor_copy(d_PT[:, 3 * g:3 * g + 3, :],
                                                      ps[:, bank, 0:3 * S].rearrange("p (j n) -> p j n", j=3)))
                        bank = ringV.take(dve)
                        ringV.empty(V.tensor_scalar(d_pc[:, b, :], ps[0:S, bank, :], d_rd[0:S, 0:1], None, ALU.mult))
                dve.wait_ge(ringS.emptied, marks["gate end"])
                link(V.tensor_scalar(flat(d_gate), flat(d_gate), 1.0, None, ALU.add))
                link(V.reciprocal(flat(d_gate), flat(d_gate)))
                link(V.tensor_tensor(flat(d_c2s), flat(d_c2s), flat(d_s2c), ALU.subtract))
                link(V.tensor_tensor(flat(d_gate), flat(d_gate), flat(d_c2s), ALU.mult))
                V.tensor_tensor(flat(d_gate), flat(d_gate), flat(d_s2c), ALU.add).then_inc(gated_made, 1)
                for i in range(NT):
                    bank = ringV.take(dve)
                    ringV.empty(V.tensor_tensor(x[:, i, :], x[:, i, :], ps[:, bank, :], ALU.add))
                own()

            def stage_e():
                norm(x, h_tok)
                turned(hT)
                dve.wait_ge(neg_a, 1)
                V.tensor_scalar(e_negA, e_negA, -1.0, None, ALU.mult).then_inc(neg_a, 1)
                cw, cb = col("conv_w"), col("conv_b")

                def silu(c):
                    dve.wait_ge(conv_exp, c + 1)
                    link(V.tensor_scalar(e_de[:, c, :], e_de[:, c, :], 1.0, None, ALU.add))
                    link(V.reciprocal(e_de[:, c, :], e_de[:, c, :]))
                    V.tensor_tensor(e_xv[:, c, :], e_dx[:, c, :], e_de[:, c, :], ALU.mult).then_inc(xv_made, 1)

                for c in range(8):
                    bank = ringV.take(dve)
                    v = ps[:, bank, :].rearrange("p (b s) -> p b s", b=B)
                    cv = e_dx[:, c, :].rearrange("p (b s) -> p b s", b=B)
                    link(V.tensor_scalar(cv, v, cw[:, 4 * c + 3:4 * c + 4], cb[:, c:c + 1], ALU.mult, ALU.add))
                    for d in (1, 2, 3):
                        w = cw[:, 4 * c + 3 - d:4 * c + 4 - d]
                        ins = V.scalar_tensor_tensor(out=cv[:, :, d:], in0=v[:, :, 0:S - d], scalar=w, in1=cv[:, :, d:],
                                                     op0=ALU.mult, op1=ALU.add)
                        if d < 3:
                            link(ins)
                    ringV.empty(ins)
                    if c:
                        silu(c - 1)
                silu(7)
                dve.wait_ge(xv_made, 8)
                z, u, w, ln, q = (flat(v) for v in (e_de, e_dx, e_dA, e_h, e_hC))
                dve.wait_ge(ringS.emptied, marks["dt"])
                V.scalar_tensor_tensor(out=u, in0=z, scalar=-1.0, in1=z, op0=ALU.mult, op1=ALU.min).then_inc(dt_arg, 1)
                dve.wait_ge(dt_exp, 1)
                V.tensor_scalar(w, u, 1.0, None, ALU.add).then_inc(dt_arg, 1)
                dve.wait_ge(dt_exp, 2)
                link(V.scalar_tensor_tensor(out=ln, in0=u, scalar=1 / 64, in1=ln, op0=ALU.is_ge, op1=ALU.mult))
                link(V.tensor_scalar(q, u, -0.25, 1 / 3, ALU.mult, ALU.add))
                link(V.tensor_tensor(q, q, u, ALU.mult))
                link(V.scalar_tensor_tensor(out=q, in0=q, scalar=-0.5, in1=u, op0=ALU.add, op1=ALU.mult))
                link(V.scalar_tensor_tensor(out=q, in0=q, scalar=1.0, in1=u, op0=ALU.add, op1=ALU.mult))
                link(V.scalar_tensor_tensor(out=q, in0=u, scalar=1 / 64, in1=q, op0=ALU.is_lt, op1=ALU.mult))
                link(V.tensor_tensor(ln, ln, q, ALU.add))
                link(V.scalar_tensor_tensor(out=z, in0=z, scalar=0.0, in1=ln, op0=ALU.max, op1=ALU.add))
                link(V.tensor_tensor(u, z, flat(e_xv), ALU.mult))
                V.memset(z.rearrange("p (b s) -> p b s", s=S)[:, :, 0:1], 1e28).then_inc(delta_made, 1)
                dve.wait_ge(ringS.emptied, marks["bc"])

                def y_rows(c):
                    dve.wait_ge(y_made, (NS // G) * (c + 1))
                    V.scalar_tensor_tensor(out=e_dx[:, c, :], in0=e_xv[:, c, :], scalar=col("D")[:, c:c + 1],
                                           in1=ps[:, c % 4, :], op0=ALU.mult, op1=ALU.add).then_inc(y_taken, 1)

                for c in range(8):
                    for g in range(NS // G):
                        k = c * (NS // G) + g
                        if k >= 2:
                            dve.wait_ge(hc_made, k - 1)
                        h = e_h[:, g % 2, :]
                        dx = e_dx[:, c:c + 1, :].broadcast_to([P, G, N])
                        link(V.tensor_tensor(h.rearrange("p (n k) -> p n k", n=G), dx,
                                             e_B[:, G * N * g:G * N * (g + 1)].rearrange("p (n k) -> p n k", n=G), ALU.mult))
                        dve.wait_ge(da_made, k + 1)
                        V.tensor_tensor_scan(h, e_dA[:, g % 2, :], h, 0.0, ALU.mult, ALU.add).then_inc(h_made, 1)
                        if g == 1 and c:
                            y_rows(c - 1)
                V.drain().then_inc(brows_free, 1)
                y_rows(7)
                for i in range(NT):
                    bank = ringV.take(dve)
                    ringV.empty(V.tensor_tensor(x[:, i, :], x[:, i, :], ps[:, bank, :], ALU.add))
                own()

            for st, run in (("A", stage_a), ("B", stage_b), ("C", stage_c), ("D", stage_d), ("E", stage_e), ("F", stage_f)):
                if st in stages:
                    run()
            V.drain().then_inc(x_made, 1)

        @block.sync
        def _(sp):
            sp.dma_start(x[:], t["x"]).then_inc(in_x, 16)
            sp.dma_start(cols[:], t["cols"]).then_inc(in_consts, 16)
            sp.dma_start(rows[:], t["rows"].partition_broadcast(P)).then_inc(in_consts, 16)

            def load(n, src, per):
                for a in range(0, src.shape[1], per):
                    sp.dma_start(wbuf[:, n % 2, a:a + per], src[:, a:a + per]).then_inc(slot_in[n % 2], 16)

            def load_ctxT(dst, b):
                sp.dma_start(dst, t["ctxT"][b]).then_inc(ctx_in, 16)

            if "A" in stages:
                load(0, t["wA"], 2048)

                def load_pos(b):
                    sp.dma_start(a_dist.bitcast(I32), t["kpos"][b].partition_broadcast(P)).then_inc(pos_in, 16)
                    for half in (0, S):
                        sp.dma_start(a_mask[half:half + S].bitcast(I32), t["mask"][b]).then_inc(pos_in, 16)
                    sp.dma_start(a_qpos.bitcast(I32), t["qpos"][b]).then_inc(pos_in, 16)

                load_ctxT(a_ctxT, 0)
                load_pos(0)
                with sp.Fori(1, B, 1) as b:
                    sp.wait_ge(ringV.emptied, (b - 1) * 60 + marks["ctxT read"])
                    load_ctxT(a_ctxT, b)
                    sp.wait_ge(bias_made, b * PAIRS)
                    load_pos(b)
            if "B" in stages:
                sp.wait_ge(kt_free, 1)
                load(1, t["wB1"], 2048)
                sp.wait_ge(slot_free, 1)
                load(2, t["wB2"], 2048)
                sp.wait_ge(ln_rows, NT * NORMS.index("B0") + 1)
                sp.dma_start(b_wcr, t["wcr"].rearrange("p (c n) -> p c n", c=C)).then_inc(stage_w_in, 16)
                sp.wait_ge(slot_free, 2)
                load(3, t["wB3"], 2048)
            if "C" in stages:
                sp.wait_ge(ln_rows, NT * NORMS.index("C") + 1)
                sp.dma_start(c_b2[0:EXPERTS], t["b2"]).then_inc(stage_w_in, 16)
                for first in (4, 12):
                    with sp.Fori(0, EXPERTS // 2, 1) as e:
                        for j in range(2):
                            sp.wait_ge(slot_free, e * 2 + (first + j - 1))
                            sp.dma_start(wbuf[:, j, :], t["wC"][e * 2 + j]).then_inc(slot_in[j], 16)
            if "D" in stages:
                sp.wait_ge(slot_free, 19)
                load(20, t["wD1"], 2048)
                sp.wait_ge(slot_free, 20)
                load(21, t["wD2"], 2048)
                sp.wait_ge(ln_rows, NT * NORMS.index("D") + 1)
                load_ctxT(d_ctxT, 0)

                def load_ctx(b):
                    full = (KT_TILES - 1) * P
                    sp.dma_start(d_ctx[:, 0:KT_TILES - 1, :],
                                 t["ctx"][b][0:full].rearrange("(k p) d -> p k d", p=P)).then_inc(ctxn_in, 16)
                    sp.dma_start(d_ctx[0:LAST, KT_TILES - 1, :], t["ctx"][b][full:S2]).then_inc(ctxn_in, 16)

                sp.wait_ge(slot_free, 21)
                load_ctx(0)
                with sp.Fori(1, B, 1) as b:
                    sp.wait_ge(s2_arg, b)
                    load_ctxT(d_ctxT, b)
                    sp.wait_ge(ringV.emptied, b * 8 + (marks["D loop end"] - 8 * B))
                    load_ctx(b)
                sp.wait_ge(ringV.emptied, marks["D loop end"])
            if "E" in stages:
                sp.wait_ge(slot_free, 21)
                load(22, t["wE"], 4096)
                sp.wait_ge(ln_rows, NT * NORMS.index("E") + 1)
                sp.dma_start(e_wx, t["wx"].rearrange("p (c n) -> p c n", c=8)).then_inc(stage_w_in, 16)
                sp.dma_start(e_wdt[0:RANK], t["wdt"]).then_inc(stage_w_in, 16)
            if "F" in stages:
                if "E" in stages:
                    sp.wait_ge(brows_free, 1)
                sp.wait_ge(slot_free, 22)
                sp.dma_start(wbuf[:, 1, 0:6144], t["wF"][0]).then_inc(slot_in[1], 16)
                sp.wait_ge(slot_free, 23)
                sp.dma_start(wbuf[:, 0, 0:6144], t["wF"][1]).then_inc(slot_in[0], 16)
                with sp.Fori(1, EXPERTS // 2, 1) as e:
                    for j in range(2):
                        sp.wait_ge(slot_free, e * 2 + (22 + j))
                        sp.dma_start(wbuf[:, 1 - j, 0:6144], t["wF"][e * 2 + j]).then_inc(slot_in[1 - j], 16)
            sp.wait_ge(x_made, 1)
            sp.dma_start(t["out"], x[:]).then_inc(out_done, 16)
            sp.wait_ge(out_done, 16)



def by_partition(m):
    k, n = m.shape
    return np.ascontiguousarray(m.reshape(k // P, P, n).transpose(1, 0, 2).reshape(P, (k // P) * n))


def side_by_side(*parts):
    return np.concatenate(parts, axis=-1)


def layout(i):
    f = {k: np.asarray(v) for k, v in i.items()}
    L0x, L0a, L0f, L1x, L1a, L1f = "L0_xattn_", "L0_attn_", "L0_ffn_", "L1_xattn_", "L1_attn_", "L1_ffn_"
    f32 = np.float32

    def vec(v):
        return v.reshape(-1, P).T

    slopes = np.repeat(np.array([(2.0 ** (-8.0 / HEADS)) ** (h + 1) for h in range(HEADS)], f32).reshape(PAIRS, 2).T, S, axis=0)
    weight = ((1 + 2 * np.arange(S)) / 128).astype(f32)
    interp = np.concatenate([np.diag(1 - weight), np.diag(weight)]).astype(f32)
    packed = {
        "ln1_g": vec(f[L0a + "ln1_g"]), "ln1_b": vec(f[L0a + "ln1_b"]), "ln2_g": vec(f[L0a + "ln2_g"]),
        "ln2_b": vec(f[L0a + "ln2_b"]), "mix_k": vec(f[L0a + "time_mix_k"]), "mix_v": vec(f[L0a + "time_mix_v"]),
        "mix_r": vec(f[L0a + "time_mix_r"]), "decay": vec(f[L0a + "time_decay"]), "first": vec(f[L0a + "time_first"]),
        "cmix_k": vec(f[L0a + "cmix_k"]), "cmix_r": vec(f[L0a + "cmix_r"]),
        "bq_c": vec(f[L1x + "bq_c"]), "bk_s": vec(f[L1x + "bk_s"]), "bv_s": vec(f[L1x + "bv_s"]),
        "bq_s": vec(f[L1x + "bq_s"]), "bk_c": vec(f[L1x + "bk_c"]), "bg": vec(f[L1x + "bg"]),
        "conv_w": by_partition(f[L1a + "conv_w"].reshape(DI, TAPS)), "conv_b": vec(f[L1a + "conv_b"]),
        "b_dt": vec(f[L1a + "b_dt"]), "A_log": by_partition(f[L1a + "A_log"]), "D": vec(f[L1a + "D"]),
        "ident": np.eye(P, dtype=f32), "slopes": slopes, "interp": interp,
        "iota": np.tile(np.arange(EXPERTS, dtype=f32), (P, 1)),
        "gate_W": by_partition(f[L0f + "gate_W"]), "router": by_partition(f[L1f + "router_w"].T),
    }
    ctx = f["ctx_1024"]
    a, m = f["itok_BxS_8_8191"], f["itok_BxS2_1_8191"]
    experts = [side_by_side(by_partition(f[L0f + "W1"][e]), by_partition(f[L0f + "W2"][e]), vec(f[L0f + "b1"][e]))
               for e in range(EXPERTS)]
    return {
        "x": f["x"].reshape(NT, P, D).transpose(1, 0, 2),
        "cols": side_by_side(*[packed[n] for n in COLS]),
        "rows": side_by_side(f[L0f + "ln_gamma"], f[L0f + "ln_beta"], f[L1x + "bv_c"], f[L0f + "gate_b"]),
        "ctxT": ctx.transpose(0, 2, 1).reshape(B, C, P, S2).transpose(0, 2, 1, 3),
        "ctx": ctx,
        "mask": f["mask_BxSxS2_if1"],
        "qpos": np.concatenate([a, a], axis=1).reshape(B, P, 1),
        "kpos": m,
        "b2": f[L0f + "b2"],
        "wA": side_by_side(*[by_partition(f[L0x + n].T) for n in ("W_q", "W_k", "W_v", "W_o")]),
        "wB1": side_by_side(*[by_partition(f[L0a + n].T) for n in ("Wk", "Wv", "Wr", "Wo")]),
        "wB2": by_partition(f[L0a + "Wck"].T),
        "wB3": by_partition(f[L0a + "Wcv"].T),
        "wcr": by_partition(f[L0a + "Wcr"].T),
        "wC": np.stack(experts),
        "wD1": side_by_side(by_partition(f[L1x + "Wq_c"].T), by_partition(f[L1x + "Wk_s"]),
                            by_partition(f[L1x + "Wk_c"].T), by_partition(f[L1x + "Wq_s"])),
        "wD2": side_by_side(by_partition(f[L1x + "Wv_c"].T), by_partition(f[L1x + "Wv_s"].T),
                            by_partition(f[L1x + "Wg"].T)),
        "wE": side_by_side(by_partition(f[L1a + "W_in"]), by_partition(f[L1a + "W_out"])),
        "wx": by_partition(f[L1a + "W_x"]),
        "wdt": f[L1a + "W_dt"],
        "wF": np.stack([side_by_side(by_partition(f[L1f + "up_proj"][e]), by_partition(f[L1f + "down_proj"][e]))
                        for e in range(EXPERTS)]),
    }


def kernel(**inputs):
    import concourse.bacc as bacc
    from concourse.bass_utils import run_bass_kernel_spmd

    nc = bacc.Bacc("TRN2", target_bir_lowering=False, num_devices=1)
    arrays = {n: np.ascontiguousarray(v) for n, v in layout(inputs).items()}
    t = {n: nc.dram_tensor("in_" + n, v.shape, mybir.dt.from_np(v.dtype), kind="ExternalInput").ap() for n, v in arrays.items()}
    t["out"] = nc.dram_tensor("out", (P, NT, D), F32, kind="ExternalOutput").ap()
    perceiver_kernel(nc, t)
    r = run_bass_kernel_spmd(nc, [{"in_" + n: v for n, v in arrays.items()}], core_ids=[0])
    return np.asarray(r.results[0]["out"]).transpose(1, 0, 2).reshape(B, S, D)
```

```python
from contextlib import ExitStack, contextmanager

import numpy as np

import concourse.bass as bass
from concourse import mybir

F32 = mybir.dt.float32
F16 = mybir.dt.float16
I32 = mybir.dt.int32
U32 = mybir.dt.uint32
ALU = mybir.AluOpType
ACT = mybir.ActivationFunctionType
AX_X = mybir.AxisListType.X

P = 128
B, S, D = 8, 64, 512
S2 = 1601
N = B * S
C = D // P
NT = N // P
HEADS, HD = 16, 32
PAIRS = HEADS // 2
KT_TILES = (S2 + P - 1) // P
LAST = S2 - (KT_TILES - 1) * P
CHUNKS = [(0, 401), (401, 801), (801, 1201), (1201, 1601)]
EXPERTS = 8
FF = 4 * D
HID = 1024
DI, NS, TAPS, RANK = 1024, 16, 4, 32
SLOT = 8200
TILES_C = NT + EXPERTS - 1
TILES_F = 2 * NT + EXPERTS - 1
BIG = 1e38
STRIDE, PICK = 25, 12

COLS = {}
_at = 0
for _name, _n in [("ln1_g", 4), ("ln1_b", 4), ("ln2_g", 4), ("ln2_b", 4), ("mix_k", 4), ("mix_v", 4), ("mix_r", 4),
                  ("decay", 4), ("first", 4), ("cmix_k", 4), ("cmix_r", 4), ("bq_c", 4), ("bk_s", 4), ("bv_s", 4),
                  ("bq_s", 4), ("bk_c", 4), ("bg", 4), ("conv_w", 32), ("conv_b", 8), ("b_dt", 8), ("A_log", 128),
                  ("D", 8), ("ident", 128), ("slopes", 8), ("interp", 64), ("iota", 8), ("gate_W", 32), ("router", 32)]:
    COLS[_name] = (_at, _n)
    _at += _n
NCOLS = _at
ROWS = {"gamma": 0, "beta": 512, "bv_c": 1024, "gate_b": 1536}
NROWS = 1544


class Side:

    def __init__(self):
        self.n, self.off = 0, 0

    @contextmanager
    def loop(self, i, first, trips, per, step=1):
        was = self.n
        if per:
            self.off = (i - first) * (per // step)
        yield
        assert self.n - was == per, (self.n - was, per)
        self.off = 0
        self.n = was + per * (trips // step)


class Chain(Side):

    def __init__(self, eng, sem):
        super().__init__()
        self.eng, self.sem = eng, sem

    def done(self, ins):
        ins.then_inc(self.sem, 1)
        self.n += 1

    def wait(self):
        self.eng.wait_ge(self.sem, self.off + self.n)

    def link(self, ins):
        self.done(ins)
        self.wait()


class Ring:

    def __init__(self, banks, filled, emptied):
        self.banks, self.filled, self.emptied = banks, filled, emptied
        self.fills, self.takes = Side(), Side()

    def claim(self, pe):
        k, r = self.fills.n, len(self.banks)
        if k >= r:
            pe.wait_ge(self.emptied, self.fills.off + (k - r + 1))
        return self.banks[k % r]

    def fill(self, ins):
        ins.then_inc(self.filled, 1)
        self.fills.n += 1

    def take(self, eng):
        eng.wait_ge(self.filled, self.takes.off + (self.takes.n + 1))
        return self.banks[self.takes.n % len(self.banks)]

    def empty(self, ins):
        ins.then_inc(self.emptied, 1)
        self.takes.n += 1


def perceiver_kernel(nc, t, stages="ABCDEF"):
    with ExitStack() as ctx:
        def sb(name, shape, dt=F32):
            return ctx.enter_context(nc.sbuf_tensor(name, shape, dt))

        def sem(name):
            return ctx.enter_context(nc.semaphore(name))

        ps = ctx.enter_context(nc.psum_tensor("ps", [P, 8, 512], F32))

        cols = sb("cols", [P, NCOLS])
        rows = sb("rows", [P, NROWS])
        x = sb("x", [P, NT, D])
        hn = sb("hn", [P, 2 * NT * D])
        wbuf = sb("wbuf", [P, 2, SLOT])
        small = sb("small", [P, 512])
        arena = sb("arena", [P, 27800])

        def col(name):
            a, n = COLS[name]
            return cols[:, a:a + n]

        def row(name, n=512):
            return rows[:, ROWS[name]:ROWS[name] + n]

        ident = col("ident")
        h_tok = hn[:, 0:NT * D].rearrange("p (t d) -> p t d", t=NT)
        hT = hn[:, NT * D:].rearrange("p (c n) -> p c n", c=C)

        def slot(n, a, b, **kw):
            v = wbuf[:, n % 2, a:b]
            return v.rearrange("p (c n) -> p c n", **kw) if kw else v

        class Carve:
            def __init__(self):
                self.at = 0

            def take(self, n, c=None):
                v = arena[:, self.at:self.at + n]
                self.at += n
                assert self.at <= 27800, self.at
                return v if c is None else v.rearrange("p (c n) -> p c n", c=c)

        sm = [0]

        def stat(n):
            v = small[:, sm[0]:sm[0] + n]
            sm[0] += n
            assert sm[0] <= 512
            return v

        ar = Carve()
        a_ctxT = ar.take(C * S2, C)
        a_V = ar.take(KT_TILES * D, KT_TILES)
        a_S = ar.take(2 * S2, 2)
        a_PT = ar.take(KT_TILES * P, KT_TILES)
        a_dist = ar.take(S2)
        a_mask = ar.take(S2)
        a_bias = ar.take(2 * S2, 2)
        a_Qbd = ar.take(PAIRS * P, PAIRS)
        a_QT = ar.take(C * N, C)
        a_KT = wbuf[:, 1, 0:C * S2].rearrange("p (c n) -> p c n", c=C)
        a_attn = hn[0:S, 0:B * D].rearrange("p (b d) -> p b d", b=B)
        a_attnT = a_QT
        a_qpos = stat(1)
        a_mx, a_nm, a_rs, a_rd = stat(4), stat(8), stat(8), stat(8)

        ar = Carve()
        b_xxT, b_mk, b_mv, b_mr = (ar.take(C * N, C) for _ in range(4))
        b_k, b_v, b_r = (ar.take(C * N, C) for _ in range(3))
        b_h1 = ar.take(NT * D, NT)
        b_wcr = ar.take(C * D, C)
        b_t = [b_xxT, b_mk, b_mv, b_mr] + [ar.take(C * N, C) for _ in range(4)]
        b_kk = arena[:, 3 * C * N:3 * C * N + 16 * N].rearrange("p (c n) -> p c n", c=16)
        b_w, b_omk = stat(4), stat(20)

        ar = Carve()

        def half(n, c=None):
            v = ar.take(n // 2).bitcast(F16)
            return v if c is None else v.rearrange("p (c n) -> p c n", c=c)

        c_acc, c_res = ar.take(NT * D, NT), ar.take(NT * D, NT)
        c_hid = ar.take(8 * P, 8)
        c_h1, c_h2, c_e, c_rows = (ar.take(4 * P, 4) for _ in range(4))
        c_xg = ar.take(C * P, C)
        c_hi, c_lo = half(NT * D, NT), half(NT * D, NT)
        c_ohi, c_olo = half(D), half(D)
        c_sel = half(2 * NT * P).rearrange("p (k t n) -> p k t n", k=2, t=NT)
        c_sel2 = half(NT * P, NT)
        c_selT = half(N)
        c_selT2 = half(N)
        c_const = ar.take(3 * P + 17)
        c_iota, c_before, c_all = (c_const[:, P * j:P * (j + 1)] for j in range(3))
        c_j, c_p = c_const[:, 3 * P:3 * P + 16], c_const[:, 3 * P + 16:3 * P + 17]
        c_rk = ar.take((NT + 1) * EXPERTS, NT + 1)
        c_diag = ar.take(NT * P, NT)
        c_bc = ar.take(2 * N, 2)
        c_cmp = ar.take(16 * EXPERTS, 16)
        c_ohc = c_cmp[:, 0:NT, :]
        c_te = ar.take(2 * 16, 2)
        c_w16 = half(2 * NT * 4).rearrange("p (k t n) -> p k t n", k=2, t=NT)
        c_wcol = ar.take(2)
        c_oh = ar.take(3 * NT * 8).rearrange("p (k t e) -> p k t e", k=3, t=NT)
        c_lg, c_m8, c_e8, c_ixf = (ar.take(NT * 8, NT) for _ in range(4))
        c_ix = ar.take(NT * 8, NT)
        c_ohT = ar.take(N)
        c_b2 = ar.take(D)
        c_gate_e = ar.take(8).rearrange("p (k t) -> p k t", k=2)
        c_sum, c_w, c_nmx = stat(4), stat(8), stat(4)
        c_tl, c_tend, c_tst = stat(8), stat(8), stat(8)
        c_slot = stat(8).rearrange("p (k t) -> p k t", k=2)

        ar = Carve()
        d_ctxT = ar.take(C * S2, C)
        d_qkT, d_g2T = ar.take(C * N, C), ar.take(C * N, C)
        d_qcT, d_kcT = ar.take(C * N, C), ar.take(C * N, C)
        d_Vc = ar.take(B * D, B)[0:S]
        d_S = ar.take(S2)[0:S]
        d_PT = ar.take(KT_TILES * S, KT_TILES)
        d_qk_b = ar.take(C * S, C)
        d_sel = ar.take(C * P, C)
        d_P2 = ar.take(S)
        d_P2T = ar.take(B * S, B)[0:S]
        d_bqk = ar.take(N)[0:1]
        d_ones = ar.take(P)[0:1]
        d_ctx = wbuf[:, 0, 0:KT_TILES * D].rearrange("p (c n) -> p c n", c=KT_TILES)
        d_pc = hn[0:S, 0:B * D].rearrange("p (b d) -> p b d", b=B)
        d_pcT, d_c2s, d_s2c, d_gate = d_qkT, d_qcT, d_kcT, d_g2T
        d_qbk, d_qb1, d_nm, d_rs, d_rd = stat(8), stat(1), stat(2), stat(2), stat(2)

        ar = Carve()
        e_xv, e_dx, e_de = (ar.take(8 * N, 8) for _ in range(3))
        G = 4
        e_dA, e_h, e_hC = (ar.take(2 * G * N, 2) for _ in range(3))
        e_wx = ar.take(512, 8)
        e_wdt = ar.take(DI)
        e_ssm = ar.take(N)
        e_B = wbuf[:, 1, 0:NS * N]
        e_C = [hn[:, 0:8 * N], wbuf[:, 0, 0:8 * N]]
        e_negA = stat(128)

        ln_eps, ln_sd, ln_rstd, ln_st, d_nbg = stat(1), stat(4), stat(4), stat(24), stat(4)
        ln_mv = stat(8).rearrange("p (t k) -> p t k", k=2)

        def flat(v):
            return v.rearrange("p c n -> p (c n)")

        def timed(v):
            return v.rearrange("p c (s t) -> p (c s) t", t=B)

        NORMS = [n for n in ("A", "B0", "B1", "B2", "C", "C2", "D", "E", "F") if n[0] in stages]
        TURNS = [n for n in ("A", "B", "B2", "C", "D", "E", "F") if n[0] in stages]

        in_consts, in_x = sem("in_consts"), sem("in_x")
        slot_in = [sem("slot0_in"), sem("slot1_in")]
        slot_free, kt_free, brows_free = sem("slot_free"), sem("kt_free"), sem("brows_free")
        ringV = Ring([0, 1, 2, 3], sem("vector_bank_filled"), sem("vector_bank_emptied"))
        ringS = Ring([4, 5, 6, 7], sem("scalar_bank_filled"), sem("scalar_bank_emptied"))
        dve_done, act_done, pool_done = sem("dve_done"), sem("act_done"), sem("pool_done")
        ln_var, ln_std, ln_rows = sem("ln_var"), sem("ln_std"), sem("ln_rows")
        ctx_in, ctxn_in = sem("ctx_in"), sem("ctxn_in")
        pos_in, pos_free = sem("pos_in"), sem("pos_free")
        bias_made, bias_used = sem("bias_made"), sem("bias_used")
        qbd_made = sem("qbd_made")
        row_max, probs_made = sem("row_max"), sem("probs_made")
        stage_w_in = sem("stage_w_in")
        mix_half, mix_made, eps_made = sem("mix_half"), sem("mix_made"), sem("eps_made")
        wkv_arg, wkv_exp, wkv_made, sq_made = sem("wkv_arg"), sem("wkv_exp"), sem("wkv_made"), sem("sq_made")
        gate_arg, gate_exp, oh_made, boost_made = sem("gate_arg"), sem("gate_exp"), sem("oh_made"), sem("boost_made")
        place_known, diag_made, split_made = sem("place_known"), sem("diag_made"), sem("split_made")
        sel_made2, out_split, scattered = sem("gather_made"), sem("out_split"), sem("scattered")
        tiles_known, wcol_made, hid_made = sem("tiles_known"), sem("wcol_made"), sem("hid_made")
        gated_made, nbg_made, d_vectors = sem("gated_made"), sem("nbg_made"), sem("d_vectors")
        qkb_made, s2_arg, s2_exp, s2_made = sem("qkb_made"), sem("s2_arg"), sem("s2_exp"), sem("s2_made")
        x_made, out_done = sem("x_made"), sem("out_done")
        conv_in, conv_exp, xv_made = sem("conv_in"), sem("conv_exp"), sem("xv_made")
        dt_arg, dt_exp, delta_made = sem("dt_arg"), sem("dt_exp"), sem("delta_made")
        neg_a, da_made, h_made, hc_made, y_made = (sem("neg_a"), sem("da_made"), sem("h_made"), sem("hc_made"),
                                                     sem("y_made"))
        waits_passed = sem("waits_passed")

        def held(eng):
            eng.sem_inc(waits_passed, 1)

        y_taken, sel_made = sem("y_taken"), sem("sel_made")

        SLOTS = ([("A", 0, 4), ("B", 1, 4), ("B", 2, 4), ("B", 3, 4)] + [("C", 4 + e, 1) for e in range(2 * TILES_C)]
                 + [("D", 26, 4), ("D", 27, 4), ("E", 28, 2)] + [("F", 29 + e, 1) for e in range(TILES_F)])
        filled_at, so_far = {}, [0, 0]
        for st, n, transfers in SLOTS:
            if st in stages:
                so_far[n % 2] += 16 * transfers
            filled_at[n] = so_far[n % 2]

        ctx0, probs0 = (B, B * PAIRS) if "A" in stages else (0, 0)
        marks = {}
        w_in_E = 16 * (("B" in stages) + 2 * ("C" in stages) + 2)
        w_in_F = 16 * (("B" in stages) + 2 * ("C" in stages) + 2 * ("E" in stages) + 1)

        block = ctx.enter_context(nc.Block())

        @block.tensor
        def _(pe):
            fillsV, fillsS = ringV.fills, ringS.fills

            def group(ring, out, pairs, waits=None):
                bank = ring.claim(pe)
                for k, (a, b) in enumerate(pairs):
                    if waits:
                        waits(k)
                    mm = nc.tensor.matmul(out(bank), a, b, start=(k == 0), stop=(k == len(pairs) - 1))
                ring.fill(mm)
                return mm

            def turn(name, src):
                for i in range(NT):
                    norm = {"B": "B1"}.get(name, name)
                    pe.wait_ge(ln_rows, NT * NORMS.index(norm) + i + 1)
                    bank = ringV.claim(pe)
                    for c in range(C):
                        mm = nc.tensor.transpose(ps[:, bank, P * c:P * (c + 1)], src[:, i, P * c:P * (c + 1)], ident)
                    ringV.fill(mm)
                marks["turn " + name] = fillsV.n

            def all_emptied(*rings):
                for ring in rings:
                    pe.wait_ge(ring.emptied, ring.fills.off + ring.fills.n)

            def square(ring, w, rhs, outs=C, ins=C):
                for o in range(outs):
                    mm = group(ring, lambda k: ps[:, k, :], [(w[:, c, P * o:P * (o + 1)], rhs[:, c, :]) for c in range(ins)])
                return mm

            def to_rows(ring, lhs, w, i, ins=C):
                return group(ring, lambda k: ps[:, k, :], [(lhs[:, c, P * i:P * (i + 1)], w[:, c, :]) for c in range(ins)])

            pe.wait_ge(in_consts, 32)

            def stage_a():
                wq, wk, wv, wo = (slot(0, 2048 * j, 2048 * (j + 1), c=C) for j in range(4))
                turn("A", h_tok)
                pe.wait_ge(slot_in[0], filled_at[0])
                all_emptied(ringV)
                square(ringS, wq, hT)
                marks["q"] = fillsS.n

                def k_tile(i):
                    o, (lo, hi) = i // 4, CHUNKS[i % 4]
                    group(ringS, lambda k: ps[:, k, 0:hi - lo],
                          [(wk[:, c, P * o:P * (o + 1)], a_ctxT[:, c, lo:hi]) for c in range(C)])

                def v_tile(i):
                    group(ringS, lambda k: ps[:, k, :], [(a_ctxT[:, c, P * i:P * (i + 1)], wv[:, c, :]) for c in range(C)])

                def v_last():
                    for q in range(4):
                        group(ringV, lambda k: ps[0:LAST, k, 0:P],
                                   [(a_ctxT[:, c, S2 - LAST:S2], wv[:, c, P * q:P * (q + 1)]) for c in range(C)])

                def scores(p, j):
                    lo, hi = CHUNKS[j]
                    return group(ringV, lambda k: ps[:, k, 0:hi - lo], [(a_Qbd[:, p, :], a_KT[:, p // 2, lo:hi])])

                def turn_probs(b, p):
                    pe.wait_ge(probs_made, b * PAIRS + (p + 1))
                    for g in range(4):
                        ring = (ringS, ringV)[g % 2]
                        bank = ring.claim(pe)
                        for j, kt in enumerate(range(4 * g, min(4 * g + 4, KT_TILES))):
                            n = min(P, S2 - P * kt)
                            mm = nc.tensor.transpose(ps[0:n, bank, P * j:P * (j + 1)],
                                                     a_S[:, p % 2, P * kt:P * kt + n], ident)
                        ring.fill(mm)
                        turned_at[ring] = ring.fills.off + ring.fills.n

                turned_at = {}

                def weigh_values(p):
                    pe.wait_ge(ringS.emptied, turned_at[ringS])
                    pe.wait_ge(ringV.emptied, turned_at[ringV])
                    group(ringV, lambda k: ps[:, k, 0:2 * HD],
                          [(a_PT[0:min(P, S2 - P * kt), kt, :], a_V[0:min(P, S2 - P * kt), kt, 2 * HD * p:2 * HD * (p + 1)])
                           for kt in range(KT_TILES)])

                def one_batch(b, first):
                    pe.wait_ge(ctx_in, b * 16 + 16)
                    for i in range(4):
                        k_tile(i)
                    if not first:
                        turn_probs(b - 1, 6)
                    for i in range(4, 8):
                        k_tile(i)
                    if not first:
                        weigh_values(6)
                        turn_probs(b - 1, 7)
                    for i in range(8, 12):
                        k_tile(i)
                    if not first:
                        weigh_values(7)
                    for i in range(12, 16):
                        k_tile(i)
                    kt_at = fillsS.off + fillsS.n
                    pe.wait_ge(qbd_made, b * 4 + 4)
                    for i in range(12):
                        v_tile(i)
                        if i == 0:
                            pe.wait_ge(ringS.emptied, kt_at)
                        if i < 8:
                            scores(i // 4, i % 4)
                    v_last()
                    if first:
                        marks["ctxT read"] = fillsV.n
                    for p in range(6):
                        turn_probs(b, p)
                        for j in range(4):
                            scores(p + 2, j)
                        weigh_values(p)

                one_batch(0, True)
                with pe.Fori(1, B, 1) as b:
                    with fillsV.loop(b, 1, B - 1, 60), fillsS.loop(b, 1, B - 1, 44):
                        one_batch(b, False)
                pe.drain().then_inc(kt_free, 1)
                for p in (6, 7):
                    turn_probs(B - 1, p)
                    weigh_values(p)
                all_emptied(ringV)
                for c in range(C):
                    bank = ringS.claim(pe)
                    for b in range(B):
                        mm = nc.tensor.transpose(ps[:, bank, S * b:S * (b + 1)], a_attn[:, b, P * c:P * (c + 1)], ident[0:S, 0:S])
                    ringS.fill(mm)
                all_emptied(ringS)
                for i in range(NT):
                    to_rows(ringV, a_attnT, wo, i)
                pe.drain().then_inc(slot_free, 1)

            def stage_b():
                wk, wv, wr, wo = (slot(1, 2048 * j, 2048 * (j + 1), c=C) for j in range(4))
                turn("B", h_tok)
                pe.wait_ge(slot_in[1], filled_at[1])
                for j, (w, m) in enumerate(((wk, b_mk), (wv, b_mv), (wr, b_mr))):
                    pe.wait_ge(mix_made, C * (j + 1))
                    square(ringS, w, m)
                marks["kvr"] = fillsS.n
                pe.wait_ge(wkv_made, 1)
                for i in range(NT):
                    to_rows(ringV, b_t[1], wo, i)
                pe.drain().then_inc(slot_free, 1)
                turn("B2", h_tok)
                pe.wait_ge(slot_in[0], filled_at[2])
                wck = slot(2, 0, 8192, c=C)
                pe.wait_ge(mix_made, C * 4)
                marks["kk"] = fillsS.n
                square(ringS, wck, b_mk, outs=16)
                pe.drain().then_inc(slot_free, 1)
                pe.wait_ge(mix_made, C * 5)
                pe.wait_ge(stage_w_in, 16)
                pe.wait_ge(slot_in[1], filled_at[3])
                wcv = slot(3, 0, 8192, c=16)
                for i in range(NT):
                    to_rows(ringS, b_mv, b_wcr, i)
                pe.wait_ge(sq_made, 16)
                for i in range(NT):
                    to_rows(ringV, b_kk, wcv, i, ins=16)
                pe.drain().then_inc(slot_free, 1)

            def router(w):
                for i in range(NT):
                    group(ringV, lambda k: ps[:, k, 0:EXPERTS],
                          [(hT[:, c, P * i:P * (i + 1)], w[:, EXPERTS * c:EXPERTS * (c + 1)]) for c in range(C)])

            def ranks():
                bank = ringV.claim(pe)
                for i in range(NT + 1):
                    parts = [(c_all, c_ohc[:, m, :]) for m in range(min(i, NT))]
                    if i < NT:
                        parts.append((c_before, c_ohc[:, i, :]))
                    for m, (a, b) in enumerate(parts):
                        mm = nc.tensor.matmul(ps[:, bank, EXPERTS * i:EXPERTS * (i + 1)], a, b, start=(m == 0),
                                              stop=(m == len(parts) - 1))
                ringV.fill(mm)

            diags = [0]

            def places_everywhere():
                diags[0] += 1
                pe.wait_ge(diag_made, diags[0])
                bank = ringV.claim(pe)
                for i in range(NT):
                    mm = nc.tensor.matmul(ps[:, bank, P * i:P * (i + 1)], c_all, c_diag[:, i, :], start=True, stop=True)
                ringV.fill(mm)

            tiles_done = [0]

            def tiles(n_tiles, first_slot, up, down_chunks, w2_at, start_sums, gate=False):
                g0 = fillsS.n
                t0 = tiles_done[0]
                banks = [(fillsV.n + i) % 4 for i in range(NT)]
                pe.wait_ge(ringV.emptied, fillsV.n)
                start_sums(banks)

                def gather(j):
                    pe.wait_ge(sel_made2, j + (t0 + 1))
                    bank = ringS.claim(pe)
                    for c in range(C):
                        for i in range(NT):
                            for m, rows_of in enumerate((c_hi, c_lo)):
                                mm = nc.tensor.matmul(ps[:, bank, P * c:P * (c + 1)], rows_of[:, i, P * c:P * (c + 1)],
                                                      c_sel[:, 0, i, :], start=(i == 0 and m == 0),
                                                      stop=(i == NT - 1 and m == 1))
                    ringS.fill(mm)

                def products(j, k):
                    for half_of in range(2):
                        bank = ringS.claim(pe)
                        for f in range(4):
                            o = 4 * half_of + f
                            for c in range(C):
                                mm = nc.tensor.matmul(ps[:, bank, P * f:P * (f + 1)], up(k)[:, c, P * o:P * (o + 1)],
                                                      c_xg[:, c, :], start=(c == 0), stop=(c == C - 1))
                        ringS.fill(mm)

                def scatter(j, last=False):
                    pe.wait_ge(out_split, j + (t0 + 1))
                    for i in range(NT):
                        for m, part in enumerate((c_ohi, c_olo)):
                            mm = nc.tensor.matmul(ps[:, banks[i], :], c_selT[:, P * i:P * (i + 1)], part, start=False,
                                                  stop=(last and m == 1))
                        if last:
                            ringV.fill(mm)
                    if not last:
                        mm.then_inc(scattered, 1)

                def down(j, k):
                    bank = ringS.claim(pe)
                    w2 = wbuf[:, k % 2, w2_at:w2_at + D * down_chunks].rearrange("p (c n) -> p c n", c=down_chunks)
                    for f in range(down_chunks):
                        mm = nc.tensor.matmul(ps[:, bank, :], c_hid[:, f, :], w2[:, f, :], start=(f == 0),
                                              stop=(f == down_chunks - 1))
                    ringS.fill(mm)

                def step(j, k, slot_count, first=False, last=False):
                    pe.wait_ge(slot_in[k % 2], slot_count)
                    if first:
                        pe.wait_ge(ringS.emptied, g0 + 1)
                    else:
                        pe.wait_ge(ringS.emptied, j * 4 + g0)
                    products(j, k)
                    at = fillsS.off + fillsS.n
                    if not last:
                        gather(j + 1)
                    if not first:
                        scatter(j - 1)
                    if gate:
                        pe.wait_ge(hid_made, j + 1)
                    else:
                        pe.wait_ge(ringS.emptied, at)
                    down(j, k)
                    pe.drain().then_inc(slot_free, 1)

                gather(0)
                step(0, first_slot, filled_at[first_slot], first=True)
                loops = (n_tiles - 3) // 2
                with pe.Fori(0, loops, 1) as it:
                    with fillsS.loop(it, 0, loops, 8):
                        for m in range(2):
                            k = first_slot + 1 + m
                            step(it * 2 + (1 + m), k, it * 16 + filled_at[k])
                for j in (n_tiles - 2, n_tiles - 1):
                    step(j, first_slot + j, filled_at[first_slot + j], last=(j == n_tiles - 1))
                scatter(n_tiles - 1, last=True)
                tiles_done[0] += n_tiles
                marks.setdefault("tiles", []).append(g0)

            def stage_c():
                turn("C", h_tok)
                all_emptied(ringV)
                router(col("gate_W"))
                pe.wait_ge(stage_w_in, 16 * (2 + ("B" in stages)))
                for k in range(2):
                    pe.wait_ge(oh_made, k + 1)
                    bank = ringV.claim(pe)
                    for i in range(NT):
                        mm = nc.tensor.transpose(ps[0:EXPERTS, bank, P * i:P * (i + 1)], c_oh[:, k, i, :], ident)
                    ringV.fill(mm)
                    ranks()
                    places_everywhere()
                    all_emptied(ringV)
                    pe.wait_ge(split_made, k + 1)

                    def bias_rows(banks):
                        for i in range(NT):
                            nc.tensor.matmul(ps[:, banks[i], :], c_ohT[0:EXPERTS, P * i:P * (i + 1)], c_b2[0:EXPERTS],
                                             start=True, stop=False)

                    tiles(TILES_C, 4 + TILES_C * k, lambda s: slot(s, 0, 4096, c=C), 8, 4096, bias_rows)

            def stage_f():
                turn("F", h_tok)
                all_emptied(ringV)
                router(col("router"))
                pe.wait_ge(stage_w_in, w_in_F)
                pe.wait_ge(oh_made, (2 if "C" in stages else 0) + 1)
                ranks()
                for _ in range(4):
                    places_everywhere()
                all_emptied(ringV)
                pe.wait_ge(split_made, (2 if "C" in stages else 0) + 1)

                def residual(banks):
                    for i in range(NT):
                        nc.tensor.matmul(ps[:, banks[i], :], ident, x[:, i, :], start=True, stop=False)

                tiles(TILES_F, 29, lambda s: slot(s, 0, 4096, c=C), 4, 4096, residual, gate=True)

            def stage_d():
                wq_c, wk_s, wk_c, wq_s = (slot(26, 2048 * j, 2048 * (j + 1), c=C) for j in range(4))
                wv_c, wv_s = (slot(27, 2048 * j, 2048 * (j + 1), c=C) for j in range(2))
                wg = slot(27, 4096, 8192, c=8)
                turn("D", h_tok)
                pe.wait_ge(slot_in[0], filled_at[26])
                all_emptied(ringV)
                square(ringS, wq_c, hT)
                square(ringS, wk_c, hT)
                all_emptied(ringS)
                square(ringS, wk_s, d_qcT)
                square(ringS, wq_s, d_kcT)
                marks["qk"] = fillsS.n
                pe.drain().then_inc(slot_free, 1)
                group(ringV, lambda k: ps[0:1, k, :], [(col("bq_s")[:, c:c + 1], d_kcT[:, c, :]) for c in range(C)])
                for b in range(B):
                    group(ringV, lambda k: ps[0:S, k, 0:1],
                          [(d_qcT[:, c, S * b:S * (b + 1)], col("bk_s")[:, c:c + 1]) for c in range(C)])
                pe.wait_ge(slot_in[1], filled_at[27])
                for b in range(B):
                    group(ringV, lambda k: ps[0:S, k, :],
                          [(hT[:, c, S * b:S * (b + 1)], wv_c[:, c, :]) for c in range(C)])
                all_emptied(ringS, ringV)
                pe.wait_ge(d_vectors, 1)

                with pe.Fori(0, B, 1) as b:
                    with fillsV.loop(b, 0, B, 8), fillsS.loop(b, 0, B, 4):
                        pe.wait_ge(qkb_made, b + 1)
                        pe.wait_ge(ctx_in, b * 16 + (16 * ctx0 + 16))
                        for lo, hi in CHUNKS:
                            group(ringV, lambda k: ps[0:S, k, 0:hi - lo],
                                  [(d_qk_b[:, c, :], d_ctxT[:, c, lo:hi]) for c in range(C)])
                        bank = ringV.claim(pe)
                        for c in range(C):
                            if c == 0:
                                pe.wait_ge(sel_made, b + 1)
                            nc.tensor.matmul(ps[:, bank, 0:S], d_sel[:, c, :], d_g2T[:, c, bass.ds(b * S, S)], start=(c == 0), stop=False)
                        mm = nc.tensor.matmul(ps[:, bank, 0:S], d_ones, d_bqk[:, bass.ds(b * S, S)], start=False, stop=True)
                        ringV.fill(mm)
                        pe.wait_ge(probs_made, b + (probs0 + 1))
                        held(pe)
                        for g in range(5):
                            ring = (ringS, ringV)[g % 2]
                            bank = ring.claim(pe)
                            held(pe)
                            for j, kt in enumerate(range(3 * g, min(3 * g + 3, KT_TILES))):
                                n = min(P, S2 - P * kt)
                                mm = nc.tensor.transpose(ps[0:n, bank, S * j:S * (j + 1)], d_S[:, P * kt:P * kt + n], ident[0:S, 0:S])
                            ring.fill(mm)
                        pe.wait_ge(s2_made, b + 1)
                        group(ringS, lambda k: ps[0:S, k, 0:S], [(d_P2, col("interp"))])
                        all_emptied(ringS, ringV)
                        pe.wait_ge(ctxn_in, b * 32 + 32)
                        group(ringV, lambda k: ps[0:S, k, :],
                                   [(d_PT[0:min(P, S2 - P * kt), kt, :], d_ctx[0:min(P, S2 - P * kt), kt, :])
                               for kt in range(KT_TILES)])
                marks["D loop end"] = fillsV.n
                all_emptied(ringV)
                for c in range(C):
                    bank = ringS.claim(pe)
                    for b in range(B):
                        mm = nc.tensor.transpose(ps[:, bank, S * b:S * (b + 1)], d_pc[:, b, P * c:P * (c + 1)], ident[0:S, 0:S])
                    ringS.fill(mm)
                for c in range(C):
                    bank = ringS.claim(pe)
                    for b in range(B):
                        mm = nc.tensor.matmul(ps[:, bank, S * b:S * (b + 1)], d_Vc[:, b, P * c:P * (c + 1)], d_P2T[:, b, :],
                                              start=(b == 0), stop=(b == B - 1), skip_group_check=True)
                    ringS.fill(mm)
                all_emptied(ringS)
                square(ringS, wv_s, d_pcT)
                all_emptied(ringS)
                for o in range(C):
                    group(ringS, lambda k: ps[:, k, :],
                          [(wg[:, c, P * o:P * (o + 1)], (d_c2s, d_s2c)[c // 4][:, c % 4, :]) for c in range(8)])
                marks["gate end"] = fillsS.n
                pe.drain().then_inc(slot_free, 1)
                pe.wait_ge(gated_made, 1)
                for i in range(NT):
                    bank = ringV.claim(pe)
                    for c in range(C):
                        mm = nc.tensor.transpose(ps[:, bank, P * c:P * (c + 1)], d_gate[:, c, P * i:P * (i + 1)], ident)
                    ringV.fill(mm)

            def stage_e():
                w_in, w_out = slot(28, 0, 4096, c=C), slot(28, 4096, 8192, c=8)
                turn("E", h_tok)
                pe.wait_ge(slot_in[0], filled_at[28])
                all_emptied(ringV)
                marks["conv"] = fillsV.n
                square(ringV, w_in, hT, outs=8)
                pe.wait_ge(stage_w_in, w_in_E)
                pe.wait_ge(xv_made, 8)
                group(ringS, lambda k: ps[0:S, k, :], [(e_wx[:, c, :], e_xv[:, c, :]) for c in range(8)])
                all_emptied(ringS)
                for c in range(8):
                    group(ringS, lambda k: ps[:, k, :], [(e_wdt[0:RANK, P * c:P * (c + 1)], e_ssm[0:RANK, :])])
                marks["dt"] = fillsS.n
                for n in range(2 * NS):
                    group(ringS, lambda k: ps[:, k, :],
                          [(ident[0:S, RANK + n:RANK + n + 1].broadcast_to([S, P]), e_ssm[0:S, :])])
                marks["bc"] = fillsS.n
                pe.wait_ge(ringV.emptied, fillsV.n)
                for c in range(8):
                    if c >= 4:
                        pe.wait_ge(y_taken, c - 3)
                    for g in range(NS // G):
                        pe.wait_ge(hc_made, c * (NS // G) + g + 1)
                        for n in range(G):
                            mm = nc.tensor.matmul(ps[:, c % 4, :], ident, e_hC[:, g % 2, N * n:N * (n + 1)],
                                                  start=(g == 0 and n == 0), stop=(g == NS // G - 1 and n == G - 1))
                        mm.then_inc(y_made, 1)
                pe.wait_ge(y_taken, 8)
                for i in range(NT):
                    to_rows(ringV, e_dx, w_out, i, ins=8)
                pe.drain().then_inc(slot_free, 1)

            for st, run, n in (("A", stage_a, 1), ("B", stage_b, 3), ("C", stage_c, 2 * TILES_C), ("D", stage_d, 2),
                               ("E", stage_e, 1), ("F", stage_f, TILES_F)):
                if st in stages:
                    run()
                else:
                    pe.sem_inc(slot_free, n)
                    if st == "A":
                        pe.sem_inc(kt_free, 1)


        @block.scalar
        def _(act):
            takes = ringS.takes
            norms = [0]

            def norm():
                norms[0] += 1
                act.wait_ge(ln_var, norms[0])
                nc.scalar.activation(ln_sd, ln_mv[:, :, 1], ACT.Sqrt, bias=ln_eps).then_inc(ln_std, 1)

            def from_bank(out, part, func, **kw):
                bank = ringS.take(act)
                ringS.empty(nc.scalar.activation(out, part(bank), func, **kw))

            def whole(k):
                return ps[:, k, :]

            act.wait_ge(in_consts, 32)
            act.wait_ge(eps_made, 1)

            def stage_a():
                norm()
                for o in range(C):
                    from_bank(a_QT[:, o, :], whole, ACT.Copy, scale=float(HD) ** -0.5)

                def k_tile(i):
                    o, (lo, hi) = i // 4, CHUNKS[i % 4]
                    from_bank(a_KT[:, o, lo:hi], lambda k: ps[:, k, 0:hi - lo], ACT.Copy)

                def turn_probs():
                    for g in (0, 2):
                        from_bank(a_PT[:, 4 * g:4 * g + 4, :], lambda k: ps[:, k, :].rearrange("p (j n) -> p j n", j=4),
                                  ACT.Copy)

                def exps(b, p):
                    act.wait_ge(row_max, b * PAIRS + (p + 1))
                    nc.scalar.activation(a_S[:, p % 2, :], a_S[:, p % 2, :], ACT.Exp, bias=a_nm[:, p:p + 1],
                                         accum_out=a_rs[:, p:p + 1]).then_inc(probs_made, 1)

                def one_batch(b, first):
                    for i in range(4):
                        k_tile(i)
                    if not first:
                        turn_probs()
                    for i in range(4, 8):
                        k_tile(i)
                    if not first:
                        turn_probs()
                    for i in range(8, 16):
                        k_tile(i)
                    for i in range(12):
                        from_bank(a_V[:, i, :], whole, ACT.Copy)
                        if i == 5:
                            exps(b, 0)
                        if i == 9:
                            exps(b, 1)
                    for p in range(6):
                        turn_probs()
                        exps(b, p + 2)

                one_batch(0, True)
                with act.Fori(1, B, 1) as b:
                    with takes.loop(b, 1, B - 1, 44):
                        one_batch(b, False)
                turn_probs()
                turn_probs()
                for c in range(C):
                    from_bank(a_attnT[:, c, :], whole, ACT.Copy)

            def stage_b():
                nc.scalar.activation(b_w, col("decay"), ACT.Exp).then_inc(wkv_exp, 1)
                norm()
                norm()

                def halves(mixes, mark):
                    act.wait_ge(ringV.emptied, marks[mark])
                    for name, dst in mixes:
                        for c in range(C):
                            nc.scalar.activation(dst[:, c, :], b_xxT[:, c, :], ACT.Copy, scale=col(name)[:, c:c + 1]) \
                                .then_inc(mix_half, 1)

                halves([("mix_k", b_mk), ("mix_v", b_mv), ("mix_r", b_mr)], "turn B")

                def by_time(k):
                    return ps[:, k, :].rearrange("p (t s) -> p t s", t=B)

                for dst, func, scale in ((b_k, ACT.Copy, 1.0), (b_v, ACT.Copy, 1.0), (b_r, ACT.Exp, -1.0)):
                    for c in range(C):
                        from_bank(dst[:, c, :].rearrange("p (s t) -> p t s", t=B), by_time, func, scale=scale)
                for k, buf in enumerate((2, 3, 4, 5)):
                    act.wait_ge(wkv_arg, k + 1)
                    v = flat(b_t[buf])
                    nc.scalar.activation(v, v, ACT.Exp).then_inc(wkv_exp, 1)
                norm()
                halves([("cmix_k", b_mk), ("cmix_r", b_mv)], "turn B2")
                for f in range(16):
                    from_bank(b_kk[:, f, :], whole, ACT.Relu)
                for i in range(NT):
                    from_bank(b_t[4][:, i, :], whole, ACT.Exp, scale=-1.0)

            gates = [0]

            def gate_exps():
                gates[0] += 1
                act.wait_ge(gate_arg, gates[0])
                for i in range(NT):
                    nc.scalar.activation(c_e8[:, i, :], c_m8[:, i, :], ACT.Exp, bias=c_nmx[:, i:i + 1],
                                         accum_out=c_sum[:, i:i + 1]).then_inc(gate_exp, 1)

            def tiles(n_tiles, hidden, first_slot, weight=None):
                scale = {} if weight is None else {"scale": weight}

                def gathered():
                    from_bank(c_xg, lambda k: ps[:, k, :].rearrange("p (c n) -> p c n", c=C), ACT.Copy)

                def step(j, k, last=False):
                    hidden(k)
                    if not last:
                        gathered()
                    if scale:
                        act.wait_ge(wcol_made, j + 1)
                    bank = ringS.take(act)
                    nc.scalar.activation(c_ohi, ps[:, bank, :], ACT.Copy, **scale)
                    ringS.empty(nc.scalar.activation(flat(c_rows), ps[:, bank, :], ACT.Copy, **scale))

                gathered()
                step(0, first_slot)
                loops = (n_tiles - 3) // 2
                with act.Fori(0, loops, 1) as it:
                    with takes.loop(it, 0, loops, 8):
                        for m in range(2):
                            step(it * 2 + (1 + m), first_slot + 1 + m)
                for j in (n_tiles - 2, n_tiles - 1):
                    step(j, first_slot + j, last=(j == n_tiles - 1))

            def stage_c():
                norm()
                gate_exps()

                def hidden(k):
                    for half_of in range(2):
                        bank = ringS.take(act)
                        for f in range(4):
                            o = 4 * half_of + f
                            ins = nc.scalar.activation(c_hid[:, o, :], ps[:, bank, P * f:P * (f + 1)], ACT.Relu,
                                                       bias=wbuf[:, k % 2, 8192 + o:8193 + o])
                        ringS.empty(ins)

                for k in range(2):
                    tiles(TILES_C, hidden, 4 + TILES_C * k)
                norm()

            def stage_d():
                norm()
                for dst, bias in ((d_qcT, "bq_c"), (d_kcT, "bk_c")):
                    for c in range(C):
                        from_bank(dst[:, c, :], whole, ACT.Identity, bias=col(bias)[:, c:c + 1])
                for dst in (d_qkT, d_g2T):
                    for c in range(C):
                        from_bank(dst[:, c, :], whole, ACT.Copy)
                with act.Fori(0, B, 1) as b:
                    with takes.loop(b, 0, B, 4):
                        act.wait_ge(row_max, b + (probs0 + 1))
                        nc.scalar.activation(d_S, d_S, ACT.Exp, bias=d_nm[0:S, 0:1],
                                             accum_out=d_rs[0:S, 0:1]).then_inc(probs_made, 1)
                        act.wait_ge(s2_arg, b + 1)
                        nc.scalar.activation(d_P2, d_P2, ACT.Exp, bias=d_nm[:, 1:2],
                                             accum_out=d_rs[:, 1:2]).then_inc(s2_exp, 1)
                        for g in (0, 2):
                            from_bank(d_PT[:, 3 * g:3 * g + 3, :],
                                      lambda k: ps[:, k, 0:3 * S].rearrange("p (j n) -> p j n", j=3), ACT.Copy)
                        from_bank(d_PT[0:LAST, KT_TILES - 1, :], lambda k: ps[0:LAST, k, 0:S], ACT.Copy)
                        from_bank(d_P2T[:, b, :], lambda k: ps[0:S, k, 0:S], ACT.Copy)
                for dst in (d_pcT, d_s2c):
                    for c in range(C):
                        from_bank(dst[:, c, :], whole, ACT.Copy)
                for c in range(C):
                    from_bank(d_c2s[:, c, :], whole, ACT.Identity, bias=col("bv_s")[:, c:c + 1])
                act.wait_ge(nbg_made, 1)
                for c in range(C):
                    from_bank(d_gate[:, c, :], whole, ACT.Exp, scale=-1.0, bias=d_nbg[:, c:c + 1])

            def stage_e():
                nc.scalar.activation(e_negA, col("A_log"), ACT.Exp).then_inc(neg_a, 1)
                norm()
                for c in range(8):
                    act.wait_ge(ringV.emptied, marks["conv"] + c + 1)
                    nc.scalar.activation(e_de[:, c, :], e_dx[:, c, :], ACT.Exp, scale=-1.0).then_inc(conv_exp, 1)
                from_bank(e_ssm[0:S], lambda k: ps[0:S, k, :], ACT.Copy)
                for c in range(8):
                    from_bank(e_de[:, c, :], whole, ACT.Identity, bias=col("b_dt")[:, c:c + 1])
                act.wait_ge(dt_arg, 1)
                nc.scalar.activation(flat(e_dx), flat(e_dx), ACT.Exp).then_inc(dt_exp, 1)
                act.wait_ge(dt_arg, 2)
                nc.scalar.activation(flat(e_h), flat(e_dA), ACT.Ln).then_inc(dt_exp, 1)
                for n in range(NS):
                    from_bank(e_B[:, N * n:N * (n + 1)], whole, ACT.Copy)
                for n in range(NS):
                    from_bank(e_C[n // 8][:, N * (n % 8):N * (n % 8 + 1)], whole, ACT.Copy)
                act.wait_ge(delta_made, 1)
                act.wait_ge(neg_a, 2)
                for c in range(8):
                    for g in range(NS // G):
                        k = c * (NS // G) + g
                        if k >= 2:
                            act.wait_ge(h_made, k - 1)
                        for n in range(G):
                            a = NS * c + G * g + n
                            ins = nc.scalar.activation(e_dA[:, g % 2, N * n:N * (n + 1)], e_de[:, c, :], ACT.Exp,
                                                       scale=e_negA[:, a:a + 1])
                        ins.then_inc(da_made, 1)

            def stage_f():
                norm()
                gate_exps()

                def hidden(k):
                    bank = ringS.take(act)
                    nc.scalar.activation(flat(c_h1), ps[:, bank, :], ACT.Copy)
                    ringS.empty(nc.scalar.activation(flat(c_e), ps[:, bank, :], ACT.Exp, scale=-1.0))
                    from_bank(flat(c_h2), whole, ACT.Copy)

                tiles(TILES_F, hidden, 29, weight=c_wcol[:, 0:1])

            for st, run in (("A", stage_a), ("B", stage_b), ("C", stage_c), ("D", stage_d), ("E", stage_e), ("F", stage_f)):
                if st in stages:
                    run()

        @block.gpsimd
        def _(pool):
            chain = Chain(pool, pool_done)
            pool.wait_ge(in_consts, 32)

            def stage_a():
                def one_batch(b, first):
                    pool.wait_ge(pos_in, b * 64 + 64)
                    held(pool)
                    nc.gpsimd.tensor_scalar(a_dist, a_dist.bitcast(I32), a_qpos.bitcast(I32), None, ALU.subtract)
                    chain.link(nc.gpsimd.tensor_scalar(a_mask, a_mask.bitcast(I32), 0.0, -1e30, ALU.is_equal, ALU.mult))
                    chain.link(nc.gpsimd.tensor_tensor(a_dist, a_dist, a_mask, ALU.add))
                    for p in range(PAIRS):
                        if not first or p >= 2:
                            pool.wait_ge(row_max, b * PAIRS + (p - 1))
                            held(pool)
                        nc.gpsimd.tensor_scalar(a_bias[:, p % 2, :], a_dist, col("slopes")[:, p:p + 1], None,
                                                ALU.mult).then_inc(bias_made, 1)

                one_batch(0, True)
                with pool.Fori(1, B, 1) as b:
                    with chain.loop(b, 1, B - 1, 2):
                        one_batch(b, False)

            def stage_e():
                pool.wait_ge(ringS.emptied, marks["bc"])
                for k in range(8 * NS // G):
                    g = k % (NS // G)
                    pool.wait_ge(h_made, k + 1)
                    if k >= 2:
                        pool.wait_ge(y_made, k - 1)
                    c_rows = e_C[g // 2][:, G * N * (g % 2):G * N * (g % 2 + 1)]
                    nc.gpsimd.tensor_tensor(e_hC[:, g % 2, :], e_h[:, g % 2, :], c_rows, ALU.mult).then_inc(hc_made, 1)

            def stage_d():
                def pick(b):
                    pool.wait_ge(ctx_in, b * 16 + (16 * ctx0 + 16))
                    held(pool)
                    rows_of = d_ctxT[:, :, 0:S * STRIDE].rearrange("p c (i r) -> p c i r", r=STRIDE)
                    for k in range(2):
                        ins = nc.gpsimd.tensor_copy(d_sel[:, :, S * k:S * (k + 1)], rows_of[:, :, :, PICK + k])
                    ins.then_inc(sel_made, 1)

                pick(0)
                with pool.Fori(1, B, 1) as b:
                    pool.wait_ge(s2_arg, b)
                    pick(b)

            if "A" in stages:
                stage_a()
            if "D" in stages:
                stage_d()
            if "E" in stages:
                stage_e()

        @block.vector
        def _(dve):
            V = nc.vector
            chain = Chain(dve, dve_done)
            link = chain.link
            takes = ringV.takes
            norms = [0]
            halves_seen = [0]

            def own():
                dve.wait_ge(ringV.emptied, takes.off + takes.n)

            def norm(src, dst):
                for i in range(NT):
                    chain.done(V.bn_stats(ln_st[:, 6 * i:6 * i + 6], src[:, i, :]))
                chain.wait()
                for i in range(NT):
                    ins = V.bn_aggr(ln_mv[:, i, :], ln_st[:, 6 * i:6 * i + 6])
                ins.then_inc(ln_var, 1)
                norms[0] += 1
                dve.wait_ge(ln_std, norms[0])
                link(V.reciprocal(ln_rstd, ln_sd))
                for i in range(NT):
                    V.tensor_scalar(dst[:, i, :], src[:, i, :], ln_mv[:, i, 0:1], ln_rstd[:, i:i + 1],
                                    ALU.subtract, ALU.mult).then_inc(ln_rows, 1)

            def own_rows():
                dve.wait_ge(ln_rows, NT * norms[0])

            def turned(dst, gain=None):
                for i in range(NT):
                    bank = ringV.take(dve)
                    if gain is None:
                        ins = V.tensor_copy(dst[:, :, P * i:P * (i + 1)], ps[:, bank, :].rearrange("p (c n) -> p c n", c=C))
                    else:
                        for c in range(C):
                            ins = V.tensor_scalar(dst[:, c, P * i:P * (i + 1)], ps[:, bank, P * c:P * (c + 1)],
                                                  col(gain + "_g")[:, c:c + 1], col(gain + "_b")[:, c:c + 1],
                                                  ALU.mult, ALU.add)
                    ringV.empty(ins)

            link(V.memset(ln_eps, 1e-5))
            V.memset(a_Qbd, 0.0).then_inc(eps_made, 1)
            dve.wait_ge(eps_made, 1)
            dve.wait_ge(in_consts, 32)
            dve.wait_ge(in_x, 16)

            def stage_a():
                norm(x, h_tok)
                turned(hT)

                def turn_probs():
                    bank = ringV.take(dve)
                    ringV.empty(V.tensor_copy(a_PT[:, 4:8, :], ps[:, bank, :].rearrange("p (j n) -> p j n", j=4)))
                    bank = ringV.take(dve)
                    ringV.empty(V.tensor_copy(a_PT[0:LAST, 12, :], ps[0:LAST, bank, 0:P]))

                def scores(b, p, first):
                    if not first or p:
                        dve.wait_ge(row_max, b * PAIRS + p)
                    dve.wait_ge(bias_made, b * PAIRS + (p + 1))
                    for j, (lo, hi) in enumerate(CHUNKS):
                        bank = ringV.take(dve)
                        held(dve)
                        ringV.empty(V.tensor_tensor_reduce(a_S[:, p % 2, lo:hi], ps[:, bank, 0:hi - lo],
                                                           a_bias[:, p % 2, lo:hi], 1.0, -3e38, ALU.add, ALU.max,
                                                           a_mx[:, j:j + 1]))
                    own()
                    V.tensor_reduce(a_nm[:, p:p + 1], a_mx, AX_X, ALU.max, negate=True).then_inc(row_max, 1)

                def heads_out(b, p):
                    rd = a_rd[:, p:p + 1]
                    link(V.tensor_scalar(rd, a_rs[:, p:p + 1], 1.0, None, ALU.add))
                    link(V.reciprocal(rd, rd))
                    bank = ringV.take(dve)
                    at = 2 * HD * p
                    V.tensor_scalar(a_attn[:, b, at:at + HD], ps[0:S, bank, 0:HD], rd[0:S], None, ALU.mult)
                    ringV.empty(V.tensor_scalar(a_attn[:, b, at + HD:at + 2 * HD], ps[S:P, bank, HD:2 * HD], rd[S:P],
                                                None, ALU.mult))

                def one_batch(b, first):
                    if not first:
                        for p in (6, 7):
                            turn_probs()
                            heads_out(b - 1, p)
                    for r in range(4):
                        dst = a_Qbd[HD * r:HD * (r + 1), :, S * (r % 2):S * (r % 2 + 1)] \
                            .rearrange("p (c k) n -> p k c n", k=2)[:, r // 2]
                        V.tensor_copy(dst, a_QT[HD * r:HD * (r + 1), :, bass.ds(b * S, S)]).then_inc(qbd_made, 1)
                    scores(b, 0, first)
                    scores(b, 1, first)
                    for q in range(4):
                        bank = ringV.take(dve)
                        ringV.empty(V.tensor_copy(a_V[0:LAST, KT_TILES - 1, P * q:P * (q + 1)], ps[0:LAST, bank, 0:P]))
                    for p in range(6):
                        turn_probs()
                        scores(b, p + 2, first)
                        heads_out(b, p)

                dve.wait_ge(ringS.emptied, marks["q"])
                one_batch(0, True)
                with dve.Fori(1, B, 1) as b:
                    with takes.loop(b, 1, B - 1, 60), chain.loop(b, 1, B - 1, 16):
                        one_batch(b, False)
                for p in (6, 7):
                    turn_probs()
                    heads_out(B - 1, p)
                for i in range(NT):
                    bank = ringV.take(dve)
                    ringV.empty(V.tensor_tensor(x[:, i, :], x[:, i, :], ps[:, bank, :], ALU.add))
                own()

            def stage_b():
                norm(x, b_h1)
                own_rows()
                norm(b_h1, h_tok)
                V.tensor_scalar(b_omk[:, 0:12], cols[:, COLS["mix_k"][0]:COLS["mix_k"][0] + 12], -1.0, 1.0, ALU.mult, ALU.add)
                link(V.tensor_scalar(b_omk[:, 12:20], cols[:, COLS["cmix_k"][0]:COLS["cmix_k"][0] + 8], -1.0, 1.0,
                                     ALU.mult, ALU.add))
                turned(b_xxT, "ln1")

                def mixes(first, dsts):
                    own()
                    for j, dst in enumerate(dsts):
                        for c in range(C):
                            halves_seen[0] += 1
                            dve.wait_ge(mix_half, halves_seen[0])
                            k = 4 * (first + j) + c
                            V.scalar_tensor_tensor(out=dst[:, c, S:], in0=b_xxT[:, c, 0:N - S], scalar=b_omk[:, k:k + 1],
                                                   in1=dst[:, c, S:], op0=ALU.mult, op1=ALU.add).then_inc(mix_made, 1)

                mixes(0, (b_mk, b_mv, b_mr))

                PN, PP, E1p, E2p, E1, E2, NUM, DEN = b_t
                dve.wait_ge(wkv_exp, 1)
                link(V.tensor_scalar(b_w, b_w, -1.0, None, ALU.mult))
                dve.wait_ge(ringS.emptied, marks["kvr"])
                for c in range(C):
                    chain.done(V.tensor_scalar(DEN[:, c, :], b_k[:, c, :], 0.0, b_w[:, c:c + 1], ALU.mult, ALU.add))
                chain.wait()
                link(V.memset(timed(DEN)[:, :, 0:1], -BIG))
                link(V.tensor_tensor_scan(flat(PN), flat(DEN), flat(b_k), -BIG, ALU.add, ALU.max))
                chain.done(V.memset(timed(PP)[:, :, 0:1], -BIG))
                link(V.tensor_copy(timed(PP)[:, :, 1:], timed(PN)[:, :, 0:B - 1]))
                for c in range(C):
                    ins = V.scalar_tensor_tensor(out=E1p[:, c, :], in0=PP[:, c, :], scalar=b_w[:, c:c + 1], in1=PN[:, c, :],
                                                 op0=ALU.add, op1=ALU.subtract)
                ins.then_inc(wkv_arg, 1)
                V.tensor_tensor(flat(E2p), flat(b_k), flat(PN), ALU.subtract).then_inc(wkv_arg, 1)
                first = col("first")
                for c in range(C):
                    chain.done(V.scalar_tensor_tensor(out=NUM[:, c, :], in0=b_k[:, c, :], scalar=first[:, c:c + 1],
                                                      in1=PP[:, c, :], op0=ALU.add, op1=ALU.max))
                chain.wait()
                V.tensor_tensor(flat(E1), flat(PP), flat(NUM), ALU.subtract).then_inc(wkv_arg, 1)
                for c in range(C):
                    ins = V.scalar_tensor_tensor(out=E2[:, c, :], in0=b_k[:, c, :], scalar=first[:, c:c + 1],
                                                 in1=NUM[:, c, :], op0=ALU.add, op1=ALU.subtract)
                ins.then_inc(wkv_arg, 1)
                dve.wait_ge(wkv_arg, 4)
                dve.wait_ge(wkv_exp, 3)
                link(V.tensor_tensor(flat(NUM), flat(E2p), flat(b_v), ALU.mult))
                link(V.tensor_tensor_scan(flat(PN), flat(E1p), flat(NUM), 0.0, ALU.mult, ALU.add))
                link(V.tensor_tensor_scan(flat(DEN), flat(E1p), flat(E2p), 0.0, ALU.mult, ALU.add))
                dve.wait_ge(wkv_exp, 5)
                link(V.tensor_tensor(flat(NUM), flat(E2), flat(b_v), ALU.mult))
                for acc, out in ((PN, NUM), (DEN, E2)):
                    link(V.tensor_tensor(timed(E1p)[:, :, 1:], timed(E1)[:, :, 1:], timed(acc)[:, :, 0:B - 1], ALU.mult))
                    link(V.tensor_tensor(timed(out)[:, :, 1:], timed(out)[:, :, 1:], timed(E1p)[:, :, 1:], ALU.add))
                link(V.tensor_scalar(flat(b_r), flat(b_r), 1.0, None, ALU.add))
                link(V.tensor_tensor(flat(E2), flat(E2), flat(b_r), ALU.mult))
                link(V.reciprocal(flat(E2), flat(E2)))
                for c in range(C):
                    ins = V.tensor_tensor(b_mk[:, c, :].rearrange("p (t s) -> p s t", t=B),
                                          NUM[:, c, :].rearrange("p (s t) -> p s t", t=B),
                                          E2[:, c, :].rearrange("p (s t) -> p s t", t=B), ALU.mult)
                ins.then_inc(wkv_made, 1)
                for i in range(NT):
                    bank = ringV.take(dve)
                    ringV.empty(V.tensor_tensor(b_h1[:, i, :], b_h1[:, i, :], ps[:, bank, :], ALU.add))
                own()
                norm(b_h1, h_tok)
                turned(b_xxT, "ln2")
                mixes(3, (b_mk, b_mv))
                for f in range(16):
                    dve.wait_ge(ringS.emptied, marks["kk"] + f + 1)
                    V.tensor_tensor(b_kk[:, f, :], b_kk[:, f, :], b_kk[:, f, :], ALU.mult).then_inc(sq_made, 1)
                dve.wait_ge(ringS.emptied, marks["kk"] + 16 + NT)
                rr = b_t[4]
                link(V.tensor_scalar(flat(rr), flat(rr), 1.0, None, ALU.add))
                link(V.reciprocal(flat(rr), flat(rr)))
                for i in range(NT):
                    chain.done(V.tensor_tensor(x[:, i, :], x[:, i, :], b_h1[:, i, :], ALU.add))
                    bank = ringV.take(dve)
                    ringV.empty(V.tensor_tensor(rr[:, i, :], rr[:, i, :], ps[:, bank, :], ALU.mult))
                    own()
                    chain.wait()
                    link(V.tensor_tensor(x[:, i, :], x[:, i, :], rr[:, i, :], ALU.add))

            gates = [0]

            def route(bias):
                for i in range(NT):
                    bank = ringV.take(dve)
                    if bias:
                        ins = V.tensor_tensor(c_lg[:, i, :], ps[:, bank, 0:EXPERTS], row("gate_b", EXPERTS), ALU.add)
                    else:
                        ins = V.tensor_copy(c_lg[:, i, :], ps[:, bank, 0:EXPERTS])
                    ringV.empty(ins)
                own()
                for i in range(NT):
                    link(V.max(c_m8[:, i, :], c_lg[:, i, :]))
                    chain.done(V.max_index(c_ix[:, i, :].bitcast(U32), c_m8[:, i, :], c_lg[:, i, :]))
                chain.wait()
                V.tensor_scalar(c_nmx, c_m8[:, :, 0], -1.0, None, ALU.mult).then_inc(gate_arg, 1)
                link(V.tensor_copy(c_ixf, c_ix.bitcast(U32)))
                for k in range(2):
                    for i in range(NT):
                        ins = V.tensor_scalar(c_oh[:, k, i, :], col("iota"), c_ixf[:, i, k:k + 1], None, ALU.is_equal)
                    link(ins)
                gates[0] += 1
                dve.wait_ge(gate_exp, NT * gates[0])

            tiles_done = [0]

            def places(n_tiles, oh, which, expert_row):
                bank = ringV.take(dve)
                ringV.empty(V.tensor_copy(flat(c_rk), ps[:, bank, 0:(NT + 1) * EXPERTS]))
                own()
                count = c_rk[:, NT, :]
                link(V.tensor_scalar(c_tl, count, 0.0, None, ALU.is_gt))
                for full in range(1, NT):
                    link(V.scalar_tensor_tensor(out=c_tl, in0=count, scalar=float(P * full), in1=c_tl, op0=ALU.is_gt,
                                                op1=ALU.add))
                chain.done(V.memset(c_tst, 1.0))
                chain.wait()
                link(V.tensor_tensor_scan(c_tend, c_tst, c_tl, 0.0, ALU.mult, ALU.add))
                link(V.tensor_tensor(c_tst, c_tend, c_tl, ALU.subtract))
                link(V.tensor_scalar(c_tst, c_tst, float(P), None, ALU.mult))
                ranked = c_rk[:, 0:NT, :]
                link(V.tensor_tensor(ranked, ranked, c_tst.rearrange("p (o e) -> p o e", o=1).broadcast_to([P, NT, EXPERTS]),
                                     ALU.add))
                link(V.tensor_tensor(c_cmp[:, 0:n_tiles, :],
                                     c_tend.rearrange("p (o e) -> p o e", o=1).broadcast_to([P, n_tiles, EXPERTS]),
                                     c_j[:, 0:n_tiles].rearrange("p (j o) -> p j o", o=1).broadcast_to([P, n_tiles, EXPERTS]),
                                     ALU.is_le))
                link(V.tensor_reduce(c_te[:, expert_row, 0:n_tiles], c_cmp[:, 0:n_tiles, :], AX_X, ALU.add))
                V.tensor_scalar(c_te[:, expert_row, 0:n_tiles].bitcast(I32), c_te[:, expert_row, 0:n_tiles],
                                float(EXPERTS - 1), None, ALU.min).then_inc(tiles_known, 1)
                for k in which:
                    link(V.tensor_tensor(c_cmp[:, 0:NT, :], ranked, oh(k), ALU.mult))
                    link(V.tensor_reduce(c_slot[:, k, :], c_cmp[:, 0:NT, :], AX_X, ALU.add))
                    for i in range(NT):
                        ins = V.tensor_scalar(c_diag[:, i, :], ident, c_slot[:, k, i:i + 1], None, ALU.mult)
                    ins.then_inc(diag_made, 1)
                    bank = ringV.take(dve)
                    ringV.empty(V.tensor_copy(c_bc[:, k, :], ps[:, bank, :]))

            def split(src):
                link(V.tensor_copy(c_hi, src))
                V.tensor_tensor(c_lo, src, c_hi, ALU.subtract).then_inc(split_made, 1)

            def tiles(n_tiles, which, hidden, g0, weigh=None):
                t0 = tiles_done[0]

                def gather_matrix():
                    for i in range(NT):
                        ins = V.tensor_scalar(c_sel[:, 0, i, :], c_iota, c_slot[:, which[0], i:i + 1], None, ALU.is_equal)
                    if len(which) == 2:
                        chain.done(ins)
                        for i in range(NT):
                            ins = V.tensor_scalar(c_sel2[:, i, :], c_iota, c_slot[:, which[1], i:i + 1], None, ALU.is_equal)
                        link(ins)
                        ins = V.tensor_tensor(c_sel[:, 0], c_sel[:, 0], c_sel2, ALU.add)
                    ins.then_inc(sel_made2, 1)

                def step(j, first=False, last=False):
                    if not last:
                        slots_now = c_slot[:, which[0]:which[-1] + 1, :]
                        dve.wait_ge(sel_made2, j + (t0 + 1))
                        link(V.tensor_scalar(slots_now, slots_now, -float(P), None, ALU.add))
                        dve.wait_ge(ringS.emptied, (g0 + 1) if first else j * 4 + g0)
                        gather_matrix()
                    hidden(j)
                    if not first:
                        dve.wait_ge(scattered, j + scattered0[0])
                    for m, k in enumerate(which):
                        link(V.tensor_scalar((c_selT, c_selT2)[m], c_bc[:, k, :], c_p, None, ALU.is_equal))
                    if weigh:
                        weigh(j)
                    if len(which) == 2:
                        link(V.tensor_tensor(c_selT, c_selT, c_selT2, ALU.add))
                    bcs = c_bc[:, which[0]:which[-1] + 1, :]
                    link(V.tensor_scalar(bcs, bcs, -float(P), None, ALU.add))
                    dve.wait_ge(ringS.emptied, j * 4 + (g0 + (4 if last else 5)))
                    V.tensor_tensor(c_olo, flat(c_rows), c_ohi, ALU.subtract).then_inc(out_split, 1)

                gather_matrix()
                per = chain.n
                step(0, first=True)
                per = chain.n - per
                loops = (n_tiles - 3) // 2
                with dve.Fori(0, loops, 1) as it:
                    with chain.loop(it, 0, loops, 2 * per):
                        for m in range(2):
                            step(it * 2 + (1 + m))
                step(n_tiles - 2)
                step(n_tiles - 1, last=True)
                tiles_done[0] += n_tiles
                scattered0[0] += n_tiles - 1

            scattered0 = [0]

            def stage_c():
                norm(x, h_tok)
                turned(hT)
                route(True)
                link(V.reciprocal(c_sum, c_sum))
                for k in range(2):
                    chain.done(V.tensor_tensor(c_w[:, 4 * k:4 * k + 4], c_e8[:, :, k], c_sum, ALU.mult))
                chain.wait()
                dve.wait_ge(stage_w_in, 16 * (2 + ("B" in stages)))
                for k in range(2):
                    V.tensor_copy(c_ohc, c_oh[:, k]).then_inc(oh_made, 1)
                    bank = ringV.take(dve)
                    ringV.empty(V.tensor_copy(c_ohT[0:EXPERTS], ps[0:EXPERTS, bank, :]))
                    places(TILES_C, lambda m: c_oh[:, m], (k,), k)
                    if k == 0:
                        split(h_tok)
                    tiles(TILES_C, (k,), lambda j: None, marks["tiles"][k])
                    for i in range(NT):
                        bank = ringV.take(dve)
                        ringV.empty(V.tensor_copy(c_acc[:, i, :], ps[:, bank, :]))
                    own()
                    prior = flat((h_tok, c_res)[k])
                    if k == 0:
                        boost = flat(c_res)
                        link(V.scalar_tensor_tensor(out=boost, in0=flat(c_acc), scalar=0.5, in1=prior,
                                                    op0=ALU.mult, op1=ALU.add))
                        split(c_res)
                        dve.wait_ge(split_made, 2)
                    for i in range(NT):
                        chain.done(V.scalar_tensor_tensor(out=c_res[:, i, :], in0=c_acc[:, i, :],
                                                          scalar=c_w[:, 4 * k + i:4 * k + i + 1],
                                                          in1=(h_tok, c_res)[k][:, i, :], op0=ALU.mult, op1=ALU.add))
                    chain.wait()
                norm(c_res, c_acc)
                own_rows()
                for i in range(NT):
                    link(V.tensor_tensor(c_acc[:, i, :], c_acc[:, i, :], row("gamma"), ALU.mult))
                    link(V.tensor_tensor(c_acc[:, i, :], c_acc[:, i, :], row("beta"), ALU.add))
                    link(V.tensor_tensor(x[:, i, :], x[:, i, :], c_acc[:, i, :], ALU.add))

            def stage_f():
                norm(x, h_tok)
                turned(hT)
                route(False)
                link(V.tensor_tensor(c_sum, c_e8[:, :, 0], c_e8[:, :, 1], ALU.add))
                link(V.reciprocal(c_sum, c_sum))
                for k in range(2):
                    chain.done(V.tensor_tensor(c_w[:, 4 * k:4 * k + 4], c_e8[:, :, k], c_sum, ALU.mult))
                chain.wait()
                dve.wait_ge(stage_w_in, w_in_F)
                V.tensor_tensor(c_ohc, c_oh[:, 0], c_oh[:, 1], ALU.add).then_inc(oh_made, 1)
                places(TILES_F, lambda m: c_oh[:, m], (0, 1), 0)
                weights_of = flat(c_acc).rearrange("p (k n) -> p k n", k=4)[:, 0:2]
                picked = flat(c_res).rearrange("p (k n) -> p k n", k=4)[:, 0:2]
                for k in range(2):
                    for i in range(NT):
                        ins = V.tensor_scalar(c_diag[:, i, :], ident, c_w[:, 4 * k + i:4 * k + i + 1], None, ALU.mult)
                    ins.then_inc(diag_made, 1)
                    bank = ringV.take(dve)
                    ringV.empty(V.tensor_copy(weights_of[:, k, :], ps[:, bank, :]))
                split(h_tok)

                def hidden(j):
                    dve.wait_ge(ringS.emptied, j * 4 + (marks["tiles"][-1] + 3))
                    link(V.tensor_scalar(flat(c_e), flat(c_e), 1.0, None, ALU.add))
                    link(V.reciprocal(flat(c_e), flat(c_e)))
                    link(V.tensor_tensor(flat(c_e), flat(c_e), flat(c_h1), ALU.mult))
                    V.tensor_tensor(c_hid[:, 0:4, :], c_e, c_h2, ALU.mult).then_inc(hid_made, 1)

                def weigh(j):
                    link(V.tensor_tensor(picked[:, 0], c_selT, weights_of[:, 0], ALU.mult))
                    link(V.tensor_tensor(picked[:, 1], c_selT2, weights_of[:, 1], ALU.mult))
                    link(V.tensor_tensor(picked[:, 0], picked[:, 0], picked[:, 1], ALU.add))
                    V.tensor_reduce(c_wcol[:, 0:1], picked[:, 0], AX_X, ALU.add).then_inc(wcol_made, 1)

                tiles(TILES_F, (0, 1), hidden, marks["tiles"][-1], weigh)
                for i in range(NT):
                    bank = ringV.take(dve)
                    ringV.empty(V.tensor_copy(x[:, i, :], ps[:, bank, :]))
                own()

            def stage_d():
                scale = float(D) ** -0.5
                V.tensor_scalar(d_nbg, col("bg"), -1.0, None, ALU.mult).then_inc(nbg_made, 1)
                norm(x, h_tok)
                V.memset(d_ones, 1.0).then_inc(d_vectors, 1)
                turned(hT)
                bank = ringV.take(dve)
                ringV.empty(V.tensor_copy(d_bqk, ps[0:1, bank, :]))
                for b in range(B):
                    bank = ringV.take(dve)
                    ringV.empty(V.tensor_copy(d_qbk[0:S, b:b + 1], ps[0:S, bank, 0:1]))
                for b in range(B):
                    bank = ringV.take(dve)
                    ringV.empty(V.tensor_tensor(d_Vc[:, b, :], ps[0:S, bank, :], row("bv_c")[0:S], ALU.add))
                own()
                dve.wait_ge(ringS.emptied, marks["qk"])
                with dve.Fori(0, B, 1) as b:
                    with takes.loop(b, 0, B, 8), chain.loop(b, 0, B, 3):
                        V.tensor_copy(d_qk_b, d_qkT[:, :, bass.ds(b * S, S)]).then_inc(qkb_made, 1)
                        link(V.tensor_copy(d_qb1[0:S], d_qbk[0:S, bass.ds(b, 1)]))
                        for lo, hi in CHUNKS:
                            bank = ringV.take(dve)
                            ringV.empty(V.tensor_scalar(d_S[:, lo:hi], ps[0:S, bank, 0:hi - lo], d_qb1[0:S], scale,
                                                        ALU.add, ALU.mult))
                        own()
                        V.tensor_reduce(d_nm[0:S, 0:1], d_S, AX_X, ALU.max, negate=True).then_inc(row_max, 1)
                        bank = ringV.take(dve)
                        ringV.empty(V.tensor_scalar(d_P2, ps[:, bank, 0:S], scale, None, ALU.mult))
                        own()
                        V.tensor_reduce(d_nm[:, 1:2], d_P2, AX_X, ALU.max, negate=True).then_inc(s2_arg, 1)
                        dve.wait_ge(s2_exp, b + 1)
                        chain.done(V.reciprocal(d_rd[0:S, 0:1], d_rs[0:S, 0:1]))
                        link(V.reciprocal(d_rd[:, 1:2], d_rs[:, 1:2]))
                        V.tensor_scalar(d_P2, d_P2, d_rd[:, 1:2], None, ALU.mult).then_inc(s2_made, 1)
                        for g in (1, 3):
                            bank = ringV.take(dve)
                            ringV.empty(V.tensor_copy(d_PT[:, 3 * g:3 * g + 3, :],
                                                      ps[:, bank, 0:3 * S].rearrange("p (j n) -> p j n", j=3)))
                        bank = ringV.take(dve)
                        ringV.empty(V.tensor_scalar(d_pc[:, b, :], ps[0:S, bank, :], d_rd[0:S, 0:1], None, ALU.mult))
                dve.wait_ge(ringS.emptied, marks["gate end"])
                link(V.tensor_scalar(flat(d_gate), flat(d_gate), 1.0, None, ALU.add))
                link(V.reciprocal(flat(d_gate), flat(d_gate)))
                link(V.tensor_tensor(flat(d_c2s), flat(d_c2s), flat(d_s2c), ALU.subtract))
                link(V.tensor_tensor(flat(d_gate), flat(d_gate), flat(d_c2s), ALU.mult))
                V.tensor_tensor(flat(d_gate), flat(d_gate), flat(d_s2c), ALU.add).then_inc(gated_made, 1)
                for i in range(NT):
                    bank = ringV.take(dve)
                    ringV.empty(V.tensor_tensor(x[:, i, :], x[:, i, :], ps[:, bank, :], ALU.add))
                own()

            def stage_e():
                norm(x, h_tok)
                turned(hT)
                dve.wait_ge(neg_a, 1)
                V.tensor_scalar(e_negA, e_negA, -1.0, None, ALU.mult).then_inc(neg_a, 1)
                cw, cb = col("conv_w"), col("conv_b")

                def silu(c):
                    dve.wait_ge(conv_exp, c + 1)
                    link(V.tensor_scalar(e_de[:, c, :], e_de[:, c, :], 1.0, None, ALU.add))
                    link(V.reciprocal(e_de[:, c, :], e_de[:, c, :]))
                    V.tensor_tensor(e_xv[:, c, :], e_dx[:, c, :], e_de[:, c, :], ALU.mult).then_inc(xv_made, 1)

                for c in range(8):
                    bank = ringV.take(dve)
                    v = ps[:, bank, :].rearrange("p (b s) -> p b s", b=B)
                    cv = e_dx[:, c, :].rearrange("p (b s) -> p b s", b=B)
                    link(V.tensor_scalar(cv, v, cw[:, 4 * c + 3:4 * c + 4], cb[:, c:c + 1], ALU.mult, ALU.add))
                    for d in (1, 2, 3):
                        w = cw[:, 4 * c + 3 - d:4 * c + 4 - d]
                        ins = V.scalar_tensor_tensor(out=cv[:, :, d:], in0=v[:, :, 0:S - d], scalar=w, in1=cv[:, :, d:],
                                                     op0=ALU.mult, op1=ALU.add)
                        if d < 3:
                            link(ins)
                    ringV.empty(ins)
                    if c:
                        silu(c - 1)
                silu(7)
                dve.wait_ge(xv_made, 8)
                z, u, w, ln, q = (flat(v) for v in (e_de, e_dx, e_dA, e_h, e_hC))
                dve.wait_ge(ringS.emptied, marks["dt"])
                V.scalar_tensor_tensor(out=u, in0=z, scalar=-1.0, in1=z, op0=ALU.mult, op1=ALU.min).then_inc(dt_arg, 1)
                dve.wait_ge(dt_exp, 1)
                V.tensor_scalar(w, u, 1.0, None, ALU.add).then_inc(dt_arg, 1)
                dve.wait_ge(dt_exp, 2)
                link(V.scalar_tensor_tensor(out=ln, in0=u, scalar=1 / 64, in1=ln, op0=ALU.is_ge, op1=ALU.mult))
                link(V.tensor_scalar(q, u, -0.25, 1 / 3, ALU.mult, ALU.add))
                link(V.tensor_tensor(q, q, u, ALU.mult))
                link(V.scalar_tensor_tensor(out=q, in0=q, scalar=-0.5, in1=u, op0=ALU.add, op1=ALU.mult))
                link(V.scalar_tensor_tensor(out=q, in0=q, scalar=1.0, in1=u, op0=ALU.add, op1=ALU.mult))
                link(V.scalar_tensor_tensor(out=q, in0=u, scalar=1 / 64, in1=q, op0=ALU.is_lt, op1=ALU.mult))
                link(V.tensor_tensor(ln, ln, q, ALU.add))
                link(V.scalar_tensor_tensor(out=z, in0=z, scalar=0.0, in1=ln, op0=ALU.max, op1=ALU.add))
                link(V.tensor_tensor(u, z, flat(e_xv), ALU.mult))
                V.memset(z.rearrange("p (b s) -> p b s", s=S)[:, :, 0:1], 1e28).then_inc(delta_made, 1)
                dve.wait_ge(ringS.emptied, marks["bc"])

                def y_rows(c):
                    dve.wait_ge(y_made, (NS // G) * (c + 1))
                    V.scalar_tensor_tensor(out=e_dx[:, c, :], in0=e_xv[:, c, :], scalar=col("D")[:, c:c + 1],
                                           in1=ps[:, c % 4, :], op0=ALU.mult, op1=ALU.add).then_inc(y_taken, 1)

                for c in range(8):
                    for g in range(NS // G):
                        k = c * (NS // G) + g
                        if k >= 2:
                            dve.wait_ge(hc_made, k - 1)
                        h = e_h[:, g % 2, :]
                        dx = e_dx[:, c:c + 1, :].broadcast_to([P, G, N])
                        link(V.tensor_tensor(h.rearrange("p (n k) -> p n k", n=G), dx,
                                             e_B[:, G * N * g:G * N * (g + 1)].rearrange("p (n k) -> p n k", n=G), ALU.mult))
                        dve.wait_ge(da_made, k + 1)
                        V.tensor_tensor_scan(h, e_dA[:, g % 2, :], h, 0.0, ALU.mult, ALU.add).then_inc(h_made, 1)
                        if g == 1 and c:
                            y_rows(c - 1)
                V.drain().then_inc(brows_free, 1)
                y_rows(7)
                for i in range(NT):
                    bank = ringV.take(dve)
                    ringV.empty(V.tensor_tensor(x[:, i, :], x[:, i, :], ps[:, bank, :], ALU.add))
                own()

            for st, run in (("A", stage_a), ("B", stage_b), ("C", stage_c), ("D", stage_d), ("E", stage_e), ("F", stage_f)):
                if st in stages:
                    run()
            V.drain().then_inc(x_made, 1)

        @block.sync
        def _(sp):
            sp.dma_start(x[:], t["x"]).then_inc(in_x, 16)
            sp.dma_start(cols[:], t["cols"]).then_inc(in_consts, 16)
            sp.dma_start(rows[:], t["rows"].partition_broadcast(P)).then_inc(in_consts, 16)

            def load(n, src, per):
                for a in range(0, src.shape[1], per):
                    sp.dma_start(wbuf[:, n % 2, a:a + per], src[:, a:a + per]).then_inc(slot_in[n % 2], 16)

            def load_ctxT(dst, b):
                sp.dma_start(dst, t["ctxT"][b]).then_inc(ctx_in, 16)

            def tile_weights(n_tiles, first_slot, weights, width, row_of):
                def one(j, k, free):
                    sp.wait_ge(slot_free, free)
                    e = sp.value_load(c_te[0:1, row_of, bass.ds(j, 1)].bitcast(I32), min_val=0, max_val=EXPERTS - 1)
                    sp.dma_start(wbuf[:, k % 2, 0:width],
                                 weights[bass.ds(e, 1)].rearrange("o p n -> (o p) n")).then_inc(slot_in[k % 2], 16)

                one(0, first_slot, first_slot - 1)
                with sp.Fori(0, (n_tiles - 1) // 2, 1) as it:
                    for m in range(2):
                        one(it * 2 + (1 + m), first_slot + 1 + m, it * 2 + (first_slot + m))

            if "A" in stages:
                load(0, t["wA"], 2048)

                def load_pos(b):
                    sp.dma_start(a_dist.bitcast(I32), t["kpos"][b].partition_broadcast(P)).then_inc(pos_in, 16)
                    for half in (0, S):
                        sp.dma_start(a_mask[half:half + S].bitcast(I32), t["mask"][b]).then_inc(pos_in, 16)
                    sp.dma_start(a_qpos.bitcast(I32), t["qpos"][b]).then_inc(pos_in, 16)

                load_ctxT(a_ctxT, 0)
                load_pos(0)
                with sp.Fori(1, B, 1) as b:
                    sp.wait_ge(ringV.emptied, (b - 1) * 60 + marks["ctxT read"])
                    load_ctxT(a_ctxT, b)
                    sp.wait_ge(bias_made, b * PAIRS)
                    load_pos(b)
            if "B" in stages:
                sp.wait_ge(kt_free, 1)
                load(1, t["wB1"], 2048)
                sp.wait_ge(slot_free, 1)
                load(2, t["wB2"], 2048)
                sp.wait_ge(ln_rows, NT * NORMS.index("B0") + 1)
                sp.dma_start(b_wcr, t["wcr"].rearrange("p (c n) -> p c n", c=C)).then_inc(stage_w_in, 16)
                sp.wait_ge(slot_free, 2)
                load(3, t["wB3"], 2048)
            if "C" in stages:
                sp.wait_ge(ln_rows, NT * NORMS.index("C") + 1)
                sp.dma_start(c_b2[0:EXPERTS], t["b2"]).then_inc(stage_w_in, 16)
                sp.dma_start(c_const, t["sel"]).then_inc(stage_w_in, 16)
                for k in range(2):
                    sp.wait_ge(tiles_known, k + 1)
                    tile_weights(TILES_C, 4 + TILES_C * k, t["wC"], SLOT, k)
            if "D" in stages:
                sp.wait_ge(slot_free, 25)
                load(26, t["wD1"], 2048)
                sp.wait_ge(slot_free, 26)
                load(27, t["wD2"], 2048)
                sp.wait_ge(ln_rows, NT * NORMS.index("D") + 1)
                load_ctxT(d_ctxT, 0)

                def load_ctx(b):
                    full = (KT_TILES - 1) * P
                    sp.dma_start(d_ctx[:, 0:KT_TILES - 1, :],
                                 t["ctx"][b][0:full].rearrange("(k p) d -> p k d", p=P)).then_inc(ctxn_in, 16)
                    sp.dma_start(d_ctx[0:LAST, KT_TILES - 1, :], t["ctx"][b][full:S2]).then_inc(ctxn_in, 16)

                sp.wait_ge(slot_free, 27)
                load_ctx(0)
                with sp.Fori(1, B, 1) as b:
                    sp.wait_ge(s2_arg, b)
                    load_ctxT(d_ctxT, b)
                    sp.wait_ge(ringV.emptied, b * 8 + (marks["D loop end"] - 8 * B))
                    load_ctx(b)
                sp.wait_ge(ringV.emptied, marks["D loop end"])
            if "E" in stages:
                sp.wait_ge(slot_free, 27)
                load(28, t["wE"], 4096)
                sp.wait_ge(ln_rows, NT * NORMS.index("E") + 1)
                sp.dma_start(e_wx, t["wx"].rearrange("p (c n) -> p c n", c=8)).then_inc(stage_w_in, 16)
                sp.dma_start(e_wdt[0:RANK], t["wdt"]).then_inc(stage_w_in, 16)
            if "F" in stages:
                if "E" in stages:
                    sp.wait_ge(brows_free, 1)
                sp.wait_ge(ln_rows, NT * NORMS.index("F") + 1)
                sp.dma_start(c_const, t["sel"]).then_inc(stage_w_in, 16)
                sp.wait_ge(tiles_known, (2 if "C" in stages else 0) + 1)
                tile_weights(TILES_F, 29, t["wF"], 6144, 0)
            sp.wait_ge(x_made, 1)
            sp.dma_start(t["out"], x[:]).then_inc(out_done, 16)
            sp.wait_ge(out_done, 16)



def by_partition(m):
    k, n = m.shape
    return np.ascontiguousarray(m.reshape(k // P, P, n).transpose(1, 0, 2).reshape(P, (k // P) * n))


def side_by_side(*parts):
    return np.concatenate(parts, axis=-1)


def layout(i):
    f = {k: np.asarray(v) for k, v in i.items()}
    L0x, L0a, L0f, L1x, L1a, L1f = "L0_xattn_", "L0_attn_", "L0_ffn_", "L1_xattn_", "L1_attn_", "L1_ffn_"
    f32 = np.float32

    def vec(v):
        return v.reshape(-1, P).T

    slopes = np.repeat(np.array([(2.0 ** (-8.0 / HEADS)) ** (h + 1) for h in range(HEADS)], f32).reshape(PAIRS, 2).T, S, axis=0)
    weight = ((1 + 2 * np.arange(S)) / 128).astype(f32)
    interp = np.concatenate([np.diag(1 - weight), np.diag(weight)]).astype(f32)
    packed = {
        "ln1_g": vec(f[L0a + "ln1_g"]), "ln1_b": vec(f[L0a + "ln1_b"]), "ln2_g": vec(f[L0a + "ln2_g"]),
        "ln2_b": vec(f[L0a + "ln2_b"]), "mix_k": vec(f[L0a + "time_mix_k"]), "mix_v": vec(f[L0a + "time_mix_v"]),
        "mix_r": vec(f[L0a + "time_mix_r"]), "decay": vec(f[L0a + "time_decay"]), "first": vec(f[L0a + "time_first"]),
        "cmix_k": vec(f[L0a + "cmix_k"]), "cmix_r": vec(f[L0a + "cmix_r"]),
        "bq_c": vec(f[L1x + "bq_c"]), "bk_s": vec(f[L1x + "bk_s"]), "bv_s": vec(f[L1x + "bv_s"]),
        "bq_s": vec(f[L1x + "bq_s"]), "bk_c": vec(f[L1x + "bk_c"]), "bg": vec(f[L1x + "bg"]),
        "conv_w": by_partition(f[L1a + "conv_w"].reshape(DI, TAPS)), "conv_b": vec(f[L1a + "conv_b"]),
        "b_dt": vec(f[L1a + "b_dt"]), "A_log": by_partition(f[L1a + "A_log"]), "D": vec(f[L1a + "D"]),
        "ident": np.eye(P, dtype=f32), "slopes": slopes, "interp": interp,
        "iota": np.tile(np.arange(EXPERTS, dtype=f32), (P, 1)),
        "gate_W": by_partition(f[L0f + "gate_W"]), "router": by_partition(f[L1f + "router_w"].T),
    }
    ctx = f["ctx_1024"]
    a, m = f["itok_BxS_8_8191"], f["itok_BxS2_1_8191"]
    experts = [side_by_side(by_partition(f[L0f + "W1"][e]), by_partition(f[L0f + "W2"][e]), vec(f[L0f + "b1"][e]))
               for e in range(EXPERTS)]
    return {
        "x": f["x"].reshape(NT, P, D).transpose(1, 0, 2),
        "cols": side_by_side(*[packed[n] for n in COLS]),
        "rows": side_by_side(f[L0f + "ln_gamma"], f[L0f + "ln_beta"], f[L1x + "bv_c"], f[L0f + "gate_b"]),
        "ctxT": ctx.transpose(0, 2, 1).reshape(B, C, P, S2).transpose(0, 2, 1, 3),
        "ctx": ctx,
        "mask": f["mask_BxSxS2_if1"],
        "qpos": np.concatenate([a, a], axis=1).reshape(B, P, 1),
        "kpos": m,
        "b2": f[L0f + "b2"],
        "sel": side_by_side(np.tile(np.arange(P), (P, 1)), np.triu(np.ones((P, P)), 1), np.ones((P, P)),
                            np.tile(np.arange(16), (P, 1)), np.arange(P)[:, None]).astype(f32),
        "wA": side_by_side(*[by_partition(f[L0x + n].T) for n in ("W_q", "W_k", "W_v", "W_o")]),
        "wB1": side_by_side(*[by_partition(f[L0a + n].T) for n in ("Wk", "Wv", "Wr", "Wo")]),
        "wB2": by_partition(f[L0a + "Wck"].T),
        "wB3": by_partition(f[L0a + "Wcv"].T),
        "wcr": by_partition(f[L0a + "Wcr"].T),
        "wC": np.stack(experts),
        "wD1": side_by_side(by_partition(f[L1x + "Wq_c"].T), by_partition(f[L1x + "Wk_s"]),
                            by_partition(f[L1x + "Wk_c"].T), by_partition(f[L1x + "Wq_s"])),
        "wD2": side_by_side(by_partition(f[L1x + "Wv_c"].T), by_partition(f[L1x + "Wv_s"].T),
                            by_partition(f[L1x + "Wg"].T)),
        "wE": side_by_side(by_partition(f[L1a + "W_in"]), by_partition(f[L1a + "W_out"])),
        "wx": by_partition(f[L1a + "W_x"]),
        "wdt": f[L1a + "W_dt"],
        "wF": np.stack([side_by_side(by_partition(f[L1f + "up_proj"][e]), by_partition(f[L1f + "down_proj"][e]))
                        for e in range(EXPERTS)]),
    }


def kernel(**inputs):
    import concourse.bacc as bacc
    from concourse.bass_utils import run_bass_kernel_spmd

    nc = bacc.Bacc("TRN2", target_bir_lowering=False, num_devices=1)
    arrays = {n: np.ascontiguousarray(v) for n, v in layout(inputs).items()}
    t = {n: nc.dram_tensor("in_" + n, v.shape, mybir.dt.from_np(v.dtype), kind="ExternalInput").ap() for n, v in arrays.items()}
    t["out"] = nc.dram_tensor("out", (P, NT, D), F32, kind="ExternalOutput").ap()
    perceiver_kernel(nc, t)
    r = run_bass_kernel_spmd(nc, [{"in_" + n: v for n, v in arrays.items()}], core_ids=[0])
    return np.asarray(r.results[0]["out"]).transpose(1, 0, 2).reshape(B, S, D)
```

```python
from contextlib import ExitStack, contextmanager

import numpy as np

import concourse.bass as bass
from concourse import mybir

F32 = mybir.dt.float32
F16 = mybir.dt.float16
I32 = mybir.dt.int32
U32 = mybir.dt.uint32
ALU = mybir.AluOpType
ACT = mybir.ActivationFunctionType
AX_X = mybir.AxisListType.X

P = 128
B, S, D = 8, 64, 512
S2 = 1601
N = B * S
C = D // P
NT = N // P
HEADS, HD = 16, 32
PAIRS = HEADS // 2
KT_TILES = (S2 + P - 1) // P
LAST = S2 - (KT_TILES - 1) * P
CHUNKS = [(0, 401), (401, 801), (801, 1201), (1201, 1601)]
EXPERTS = 8
DI, NS, TAPS, RANK = 1024, 16, 4, 32
SLOT = 8200
TILES_C = NT + EXPERTS - 1
TILES_F = 2 * NT + EXPERTS - 1
BIG = 1e38
STRIDE, PICK = 25, 12

COLS = {}
_at = 0
for _name, _n in [("ln1_g", 4), ("ln1_b", 4), ("ln2_g", 4), ("ln2_b", 4), ("mix_k", 4), ("mix_v", 4), ("mix_r", 4),
                  ("decay", 4), ("first", 4), ("cmix_k", 4), ("cmix_r", 4), ("bq_c", 4), ("bk_s", 4), ("bv_s", 4),
                  ("bq_s", 4), ("bk_c", 4), ("bg", 4), ("conv_w", 32), ("conv_b", 8), ("b_dt", 8), ("A_log", 128),
                  ("D", 8), ("ident", 128), ("slopes", 8), ("interp", 64), ("iota", 8), ("gate_W", 32), ("router", 32)]:
    COLS[_name] = (_at, _n)
    _at += _n
NCOLS = _at
ROWS = {"gamma": 0, "beta": 512, "bv_c": 1024, "gate_b": 1536}
NROWS = 1544


class Side:

    def __init__(self):
        self.n, self.off = 0, 0

    @contextmanager
    def loop(self, i, first, trips, per):
        start = self.n
        if per:
            self.off = (i - first) * per
        yield
        assert self.n - start == per, (self.n - start, per)
        self.off = 0
        self.n = start + per * trips


class Chain(Side):

    def __init__(self, eng, sem):
        super().__init__()
        self.eng, self.sem = eng, sem

    def done(self, ins):
        ins.then_inc(self.sem, 1)
        self.n += 1

    def wait(self):
        self.eng.wait_ge(self.sem, self.off + self.n)

    def link(self, ins):
        self.done(ins)
        self.wait()


class Ring:

    def __init__(self, banks, filled, emptied):
        self.banks, self.filled, self.emptied = banks, filled, emptied
        self.fills, self.takes = Side(), Side()

    def claim(self, pe):
        k, r = self.fills.n, len(self.banks)
        if k >= r:
            pe.wait_ge(self.emptied, self.fills.off + (k - r + 1))
        return self.banks[k % r]

    def fill(self, ins):
        ins.then_inc(self.filled, 1)
        self.fills.n += 1

    def take(self, eng):
        eng.wait_ge(self.filled, self.takes.off + (self.takes.n + 1))
        return self.banks[self.takes.n % len(self.banks)]

    def empty(self, ins):
        ins.then_inc(self.emptied, 1)
        self.takes.n += 1


def perceiver_kernel(nc, t, stages="ABCDEF"):
    with ExitStack() as ctx:
        def sb(name, shape, dt=F32):
            return ctx.enter_context(nc.sbuf_tensor(name, shape, dt))

        def sem(name):
            return ctx.enter_context(nc.semaphore(name))

        ps = ctx.enter_context(nc.psum_tensor("ps", [P, 8, 512], F32))

        cols = sb("cols", [P, NCOLS])
        rows = sb("rows", [P, NROWS])
        x = sb("x", [P, NT, D])
        hn = sb("hn", [P, 2 * NT * D])
        wbuf = sb("wbuf", [P, 2, SLOT])
        small = sb("small", [P, 512])
        arena = sb("arena", [P, 27800])

        def col(name):
            a, n = COLS[name]
            return cols[:, a:a + n]

        def row(name, n=512):
            return rows[:, ROWS[name]:ROWS[name] + n]

        ident = col("ident")
        h_tok = hn[:, 0:NT * D].rearrange("p (t d) -> p t d", t=NT)
        hT = hn[:, NT * D:].rearrange("p (c n) -> p c n", c=C)

        def slot(n, a, b, **kw):
            v = wbuf[:, n % 2, a:b]
            return v.rearrange("p (c n) -> p c n", **kw) if kw else v

        class Carve:
            def __init__(self):
                self.at = 0

            def take(self, n, c=None):
                v = arena[:, self.at:self.at + n]
                self.at += n
                assert self.at <= 27800, self.at
                return v if c is None else v.rearrange("p (c n) -> p c n", c=c)

        sm = [0]

        def stat(n):
            v = small[:, sm[0]:sm[0] + n]
            sm[0] += n
            assert sm[0] <= 512
            return v

        def flat(v):
            return v.rearrange("p c n -> p (c n)")

        def hi_lo(v, c=None):
            n = v.shape[1] // 2
            parts = [v[:, k * n:(k + 1) * n].bitcast(F16) for k in range(2)]
            return parts if c is None else [h.rearrange("p (c n) -> p c n", c=c) for h in parts]

        ar = Carve()
        a_ctx = hi_lo(ar.take(C * S2), C)
        a_V = ar.take(KT_TILES * D).bitcast(F16).rearrange("p (t n) -> p t n", t=KT_TILES)
        a_Vparts = a_V.rearrange("p t (h k n) -> p t h k n", h=PAIRS, k=2)
        a_S = ar.take(2 * S2, 2)
        a_PT = [hi_lo(v, KT_TILES) for v in (ar.take(KT_TILES * P), wbuf[:, 0, 6144:6144 + KT_TILES * P])]
        a_wo = wbuf[:, 0, 0:2048].rearrange("p (c n) -> p c n", c=C)
        a_dist = ar.take(S2)
        a_mask = ar.take(S2)
        a_bias = ar.take(2 * S2, 2)
        a_Qbd_all = ar.take(PAIRS * P)
        a_Qbd = hi_lo(a_Qbd_all, PAIRS)
        a_QT = ar.take(C * N, C)
        a_low = ar.take(2 * HD)
        a_KT = hi_lo(wbuf[:, 1, 0:C * S2], C)
        a_wk, a_wv = hi_lo(wbuf[:, 0, 0:2048], C), hi_lo(wbuf[:, 0, 2048:4096], C)
        a_ctx0 = a_V.rearrange("p t n -> p (t n)").bitcast(F32)[:, 0:C * S2].rearrange("p (c n) -> p c n", c=C)
        a_wq = flat(a_S)[:, 0:C * D].rearrange("p (c n) -> p c n", c=C)
        a_stage = [wbuf[:, 0, 4096:4096 + S2], wbuf[:, 1, C * S2:(C + 1) * S2]]
        a_attn = hn[0:S, 0:B * D].rearrange("p (b d) -> p b d", b=B)
        a_attnT = a_QT
        a_qpos = stat(1)
        a_mx, a_nm, a_rs, a_rd = stat(4), stat(8), stat(8), stat(8)
        SPLIT_AT = (1, 2, 3, 4)
        W_UP, P_UP = 64.0, 1024.0

        ar = Carve()
        b_xxT, b_mk, b_mv, b_mr = (ar.take(C * N, C) for _ in range(4))
        b_k, b_v, b_r = (ar.take(C * N, C) for _ in range(3))
        b_h1 = ar.take(NT * D, NT)
        b_wcr = ar.take(C * D, C)
        b_rr = ar.take(C * N, C)
        ar.take(3 * C * N)
        b_kk = arena[:, 3 * C * N:3 * C * N + 16 * N].rearrange("p (c n) -> p c n", c=16)
        b_w, b_omk = stat(4), stat(20)
        b_wkv = [arena[:, at:at + 8 * N].rearrange("p (k n) -> p k n", k=8)
                 for at in (9 * C * N, 11 * C * N, 0, 2 * C * N)]
        KVR_ORDER = ["k0", "k1", "v0", "r0", "v1", "r1", "k2", "k3", "v2", "r2", "v3", "r3"]


        ar = Carve()

        def half(n, c=None):
            v = ar.take(n // 2).bitcast(F16)
            return v if c is None else v.rearrange("p (c n) -> p c n", c=c)

        c_acc, c_res = ar.take(NT * D, NT), ar.take(NT * D, NT)
        c_hid = ar.take(8 * P, 8)
        c_h1, c_h2, c_e, c_rows = (ar.take(4 * P, 4) for _ in range(4))
        c_xg = ar.take(C * P, C)
        c_hi, c_lo = half(NT * D, NT), half(NT * D, NT)
        c_ohi, c_olo = half(D), half(D)
        c_sel = half(NT * P, NT)
        c_selT = half(N)
        c_const = ar.take(3 * P + 17)
        c_iota, c_before, c_all = (c_const[:, P * j:P * (j + 1)] for j in range(3))
        c_j, c_p = c_const[:, 3 * P:3 * P + 16], c_const[:, 3 * P + 16:3 * P + 17]
        c_rk = ar.take((NT + 1) * EXPERTS, NT + 1)
        c_diag = ar.take(NT * P, NT)
        c_bc = ar.take(2 * N, 2)
        c_cmp = ar.take(16 * EXPERTS, 16)
        c_ohc = c_cmp[:, 0:NT, :]
        c_te = ar.take(2 * 16, 2)
        c_wcol = ar.take(2)
        c_oh = ar.take(2 * NT * 8).rearrange("p (k t e) -> p k t e", k=2, t=NT)
        c_lg, c_m8, c_e8, c_ixf = (ar.take(NT * 8, NT) for _ in range(4))
        c_ix = ar.take(NT * 8, NT)
        c_ohT = ar.take(N)
        c_b2 = ar.take(D)
        c_w2 = hi_lo(ar.take(8 * D), 8)
        c_hid16 = hi_lo(ar.take(8 * P), 8)
        c_sum, c_w, c_nmx = stat(4), stat(8), stat(4)
        c_tl, c_tend, c_tst, c_place = stat(8), stat(8), stat(8), stat(1)
        c_slot = stat(8).rearrange("p (k t) -> p k t", k=2)

        ar = Carve()
        d_ctxT = ar.take(C * S2, C)
        d_qkT, d_g2T = ar.take(C * N, C), ar.take(C * N, C)
        d_qcT, d_kcT = ar.take(C * N, C), ar.take(C * N, C)
        d_Vc = ar.take(NT * D, NT)
        d_S = ar.take(S2)[0:S]
        d_PT = ar.take(KT_TILES * S, KT_TILES)
        d_qk_b = ar.take(C * S, C)
        d_sel = ar.take(C * P, C)
        d_P2 = ar.take(S)
        d_P2_all = ar.take(B * S, B)
        d_P2T = ar.take(NT * P, NT)
        d_bqk = ar.take(N)[0:1]
        d_ones = ar.take(P)[0:1]
        d_ctx = wbuf[:, 0, 0:KT_TILES * D].rearrange("p (c n) -> p c n", c=KT_TILES)
        d_pc = hn[0:S, 0:B * D].rearrange("p (b d) -> p b d", b=B)
        d_pcT, d_c2s, d_s2c, d_gate = d_qkT, d_qcT, d_kcT, d_g2T
        d_qbk, d_qb1, d_nm, d_rs, d_rd = stat(8), stat(1), stat(2), stat(2), stat(2)

        ar = Carve()
        e_xv, e_dx, e_de = (ar.take(8 * N, 8) for _ in range(3))
        G = 4
        e_dA, e_h, e_hC = (ar.take(2 * G * N, 2) for _ in range(3))
        e_wx = ar.take(512, 8)
        e_wdt = ar.take(DI)
        e_ssm = ar.take(N)
        e_B = wbuf[:, 1, 0:NS * N]
        e_C = [hn[:, 0:8 * N], wbuf[:, 0, 0:8 * N]]
        e_negA = stat(128)

        ln_eps, ln_sd, ln_rstd, ln_st, d_nbg = stat(1), stat(4), stat(4), stat(24), stat(4)
        ln_mv = stat(8).rearrange("p (t k) -> p t k", k=2)

        NORMS = [n for n in ("A", "B0", "B1", "B2", "C", "C2", "D", "E", "F") if n[0] in stages]

        in_consts, in_x = sem("in_consts"), sem("in_x")
        slot_in = [sem("slot0_in"), sem("slot1_in")]
        slot_free, kt_free, brows_free = sem("slot_free"), sem("kt_free"), sem("brows_free")
        ringV = Ring([0, 1, 2, 3], sem("vector_bank_filled"), sem("vector_bank_emptied"))
        ringS = Ring([4, 5, 6, 7], sem("scalar_bank_filled"), sem("scalar_bank_emptied"))
        dve_done, pool_done = sem("dve_done"), sem("pool_done")
        ln_var, ln_std, ln_rows = sem("ln_var"), sem("ln_std"), sem("ln_rows")
        ctx_in, ctxn_in = sem("ctx_in"), sem("ctxn_in")
        stage_in = [sem("stage0_in"), sem("stage1_in")]
        w_hi, w_split, ctx_hi, ctx_split, hi_made = (sem("w_hi"), sem("w_split"), sem("ctx_hi"), sem("ctx_split"),
                                                     sem("hi_made"))
        pos_in = sem("pos_in")
        bias_made = [sem("even_bias_made"), sem("odd_bias_made")]
        qbd_made = sem("qbd_made")
        row_max, probs_made = sem("row_max"), sem("probs_made")
        stage_w_in = sem("stage_w_in")
        mix_half, mix_made, eps_made = sem("mix_half"), sem("mix_made"), sem("eps_made")
        wkv_arg, wkv_exp, wkv_made, sq_made = sem("wkv_arg"), sem("wkv_exp"), sem("wkv_made"), sem("sq_made")
        gate_arg, gate_exp, oh_made = sem("gate_arg"), sem("gate_exp"), sem("oh_made")
        diag_made, split_made = sem("diag_made"), sem("split_made")
        gather_made, out_split, scattered = sem("gather_made"), sem("out_split"), sem("scattered")
        shifted = sem("shifted")
        relu_made = sem("relu_made")
        w2_hi, w2_split, hid_hi, hid_split = sem("w2_hi"), sem("w2_split"), sem("hid_hi"), sem("hid_split")
        tiles_known, wcol_made, hid_made = sem("tiles_known"), sem("wcol_made"), sem("hid_made")
        gated_made, nbg_made, d_vectors = sem("gated_made"), sem("nbg_made"), sem("d_vectors")
        qkb_made, s2_arg, s2_exp, s2_made = sem("qkb_made"), sem("s2_arg"), sem("s2_exp"), sem("s2_made")
        x_made, out_done = sem("x_made"), sem("out_done")
        conv_exp, xv_made = sem("conv_exp"), sem("xv_made")
        conv_tap, conv_sum, conv_inv = sem("conv_tap"), sem("conv_sum"), sem("conv_inv")
        dt_arg, dt_exp, dt_ln = sem("dt_arg"), sem("dt_exp"), sem("dt_ln")
        delta_made = sem("delta_made")
        neg_a, da_made, h_made, hc_made, y_made = (sem("neg_a"), sem("da_made"), sem("h_made"), sem("hc_made"),
                                                     sem("y_made"))
        waits_passed = sem("waits_passed")

        def held(eng):
            eng.sem_inc(waits_passed, 1)

        rows_summed = sem("rows_summed")
        y_taken, picked, inputs_made = sem("y_taken"), sem("picked"), sem("inputs_made")

        SLOTS = ([("A", 0, 4), ("B", 1, 4), ("B", 2, 4), ("B", 3, 4)] + [("C", 4 + e, 2) for e in range(2 * TILES_C)]
                 + [("D", 26, 4), ("D", 27, 4), ("E", 28, 2)] + [("F", 29 + e, 2) for e in range(TILES_F)])
        filled_at, so_far = {}, [0, 0]
        for st, n, transfers in SLOTS:
            if st in stages:
                so_far[n % 2] += 16 * transfers
            filled_at[n] = so_far[n % 2]

        ctx0, probs0 = (16, B * PAIRS) if "A" in stages else (0, 0)
        marks = {}
        w_in_E = 16 * (("B" in stages) + 2 * ("C" in stages) + 2)
        w_in_F = 16 * (("B" in stages) + 2 * ("C" in stages) + 2 * ("E" in stages) + 1)

        block = ctx.enter_context(nc.Block())

        @block.tensor
        def _(pe):
            fillsV, fillsS = ringV.fills, ringS.fills

            def group(ring, out, pairs, waits=None):
                bank = ring.claim(pe)
                for k, (a, b) in enumerate(pairs):
                    if waits:
                        waits(k)
                    mm = nc.tensor.matmul(out(bank), a, b, start=(k == 0), stop=(k == len(pairs) - 1))
                ring.fill(mm)
                return mm

            def turn(name, src):
                for i in range(NT):
                    norm = {"B": "B1"}.get(name, name)
                    pe.wait_ge(ln_rows, NT * NORMS.index(norm) + i + 1)
                    bank = ringV.claim(pe)
                    for c in range(C):
                        mm = nc.tensor.transpose(ps[:, bank, P * c:P * (c + 1)], src[:, i, P * c:P * (c + 1)], ident)
                    ringV.fill(mm)
                marks["turn " + name] = fillsV.n

            def all_emptied(*rings):
                for ring in rings:
                    pe.wait_ge(ring.emptied, ring.fills.off + ring.fills.n)

            def square(ring, w, rhs, outs=C, ins=C):
                for o in range(outs):
                    mm = group(ring, lambda k: ps[:, k, :], [(w[:, c, P * o:P * (o + 1)], rhs[:, c, :]) for c in range(ins)])
                return mm

            def to_rows(ring, lhs, w, i, ins=C):
                return group(ring, lambda k: ps[:, k, :], [(lhs[:, c, P * i:P * (i + 1)], w[:, c, :]) for c in range(ins)])

            pe.wait_ge(in_consts, 32)

            def stage_a():
                turn("A", h_tok)
                pe.wait_ge(slot_in[0], 48)
                all_emptied(ringV)
                square(ringS, a_wq, hT)
                marks["q"] = fillsS.n

                pe.wait_ge(w_split, 2)

                def three(a, b):
                    return [(a[0], b[0]), (a[0], b[1]), (a[1], b[0])]

                def cut(halves, c, lo, hi):
                    return [h[:, c, lo:hi] for h in halves]

                def k_tile(i):
                    o, (lo, hi) = i // 4, CHUNKS[i % 4]
                    group(ringS, lambda k: ps[:, k, 0:hi - lo],
                          [m for c in range(C) for m in three(cut(a_wk, c, P * o, P * (o + 1)), cut(a_ctx, c, lo, hi))])

                def v_tile(i):
                    group(ringS, lambda k: ps[:, k, :],
                          [m for c in range(C) for m in three(cut(a_ctx, c, P * i, P * (i + 1)), cut(a_wv, c, 0, D))])

                def v_last():
                    for q in range(4):
                        group(ringV, lambda k: ps[0:LAST, k, 0:P],
                              [m for c in range(C)
                               for m in three(cut(a_ctx, c, S2 - LAST, S2), cut(a_wv, c, P * q, P * (q + 1)))])

                def scores(p, j):
                    lo, hi = CHUNKS[j]
                    return group(ringV, lambda k: ps[:, k, 0:hi - lo],
                                 three([h[:, p, :] for h in a_Qbd], cut(a_KT, p // 2, lo, hi)))

                def turn_probs(b, p):
                    pe.wait_ge(probs_made, b * PAIRS + (p + 1))
                    for g in range(4):
                        ring = (ringS, ringV)[g % 2]
                        bank = ring.claim(pe)
                        for j, kt in enumerate(range(4 * g, min(4 * g + 4, KT_TILES))):
                            n = min(P, S2 - P * kt)
                            mm = nc.tensor.transpose(ps[0:n, bank, P * j:P * (j + 1)],
                                                     a_S[:, p % 2, P * kt:P * kt + n], ident)
                        ring.fill(mm)
                    turned_at[p] = [(ring, ring.fills.off + ring.fills.n) for ring in (ringS, ringV)]

                turned_at = {}

                def weigh_values(p):
                    for ring, count in turned_at[p]:
                        pe.wait_ge(ring.emptied, count)
                    bank = ringV.claim(pe)
                    for kt in range(KT_TILES):
                        n = min(P, S2 - P * kt)
                        nc.tensor.matmul(ps[:, bank, 0:P], a_PT[p % 2][0][0:n, kt, :], a_V[0:n, kt, P * p:P * (p + 1)],
                                         start=(kt == 0), stop=False, skip_group_check=True)
                        mm = nc.tensor.matmul(ps[:, bank, 0:2 * HD], a_PT[p % 2][1][0:n, kt, :],
                                              a_V[0:n, kt, P * p:P * p + 2 * HD], start=False,
                                              stop=(kt == KT_TILES - 1), skip_group_check=True)
                    ringV.fill(mm)

                def head(b, first):
                    pe.wait_ge(ctx_split, b * 4 + 4)
                    for i in range(4):
                        k_tile(i)
                    if not first:
                        turn_probs(b - 1, 6)
                        weigh_values(5)
                    for i in range(4, 8):
                        k_tile(i)
                    if not first:
                        turn_probs(b - 1, 7)
                        weigh_values(6)
                    for i in range(8, 12):
                        k_tile(i)
                    if not first:
                        weigh_values(7)
                    for i in range(12, 16):
                        k_tile(i)
                    kt_at = fillsS.off + fillsS.n
                    pe.wait_ge(qbd_made, b * 8 + 8)
                    for i in range(12):
                        v_tile(i)
                        if i == 0:
                            pe.wait_ge(ringS.emptied, kt_at)
                        if i < 8:
                            scores(i // 4, i % 4)
                    v_last()

                def pairs(b):
                    for p in range(6):
                        turn_probs(b, p)
                        if p:
                            weigh_values(p - 1)
                        for j in range(4):
                            scores(p + 2, j)

                head(0, True)
                with pe.Fori(1, B, 1) as b:
                    with fillsV.loop(b, 1, B - 1, 60), fillsS.loop(b, 1, B - 1, 44):
                        pairs(b - 1)
                        head(b, False)
                pairs(B - 1)
                pe.drain().then_inc(kt_free, 1)
                for p in (6, 7):
                    turn_probs(B - 1, p)
                    weigh_values(p - 1)
                weigh_values(7)
                all_emptied(ringV)
                for c in range(C):
                    bank = ringS.claim(pe)
                    for b in range(B):
                        mm = nc.tensor.transpose(ps[:, bank, S * b:S * (b + 1)], a_attn[:, b, P * c:P * (c + 1)], ident[0:S, 0:S])
                    ringS.fill(mm)
                all_emptied(ringS)
                pe.wait_ge(slot_in[0], filled_at[0])
                for i in range(NT):
                    to_rows(ringV, a_attnT, a_wo, i)
                pe.drain().then_inc(slot_free, 1)

            def stage_b():
                wk, wv, wr, wo = (slot(1, 2048 * j, 2048 * (j + 1), c=C) for j in range(4))
                turn("B", h_tok)
                pe.wait_ge(slot_in[1], filled_at[1])
                marks["kvr"] = fillsS.n
                for name in KVR_ORDER:
                    j, o = "kvr".index(name[0]), int(name[1])
                    pe.wait_ge(mix_made, C * (j + 1))
                    w, m = ((wk, b_mk), (wv, b_mv), (wr, b_mr))[j]
                    group(ringS, lambda k: ps[:, k, :], [(w[:, c, P * o:P * (o + 1)], m[:, c, :]) for c in range(C)])
                banks = [ringV.banks[(fillsV.n + i) % 4] for i in range(NT)]
                all_emptied(ringV)
                for c in range(C):
                    pe.wait_ge(wkv_made, c + 1)
                    for i in range(NT):
                        mm = nc.tensor.matmul(ps[:, banks[i], :], b_k[:, c, P * i:P * (i + 1)], wo[:, c, :],
                                              start=(c == 0), stop=(c == C - 1))
                        if c == C - 1:
                            ringV.fill(mm)
                pe.drain().then_inc(slot_free, 1)
                turn("B2", h_tok)
                pe.wait_ge(slot_in[0], filled_at[2])
                wck = slot(2, 0, 8192, c=C)
                pe.wait_ge(mix_made, C * 4)
                marks["kk"] = fillsS.n
                square(ringS, wck, b_mk, outs=16)
                pe.drain().then_inc(slot_free, 1)
                pe.wait_ge(mix_made, C * 5)
                pe.wait_ge(stage_w_in, 16)
                pe.wait_ge(slot_in[1], filled_at[3])
                wcv = slot(3, 0, 8192, c=16)
                for i in range(NT):
                    to_rows(ringS, b_mv, b_wcr, i)
                pe.wait_ge(sq_made, 16)
                for i in range(NT):
                    to_rows(ringV, b_kk, wcv, i, ins=16)
                pe.drain().then_inc(slot_free, 1)

            def router(w):
                for i in range(NT):
                    group(ringV, lambda k: ps[:, k, 0:EXPERTS],
                          [(hT[:, c, P * i:P * (i + 1)], w[:, EXPERTS * c:EXPERTS * (c + 1)]) for c in range(C)])

            def ranks(ring, chosen):
                bank = ring.claim(pe)
                for i in range(NT + 1):
                    parts = [(c_all, chosen[:, m, :]) for m in range(min(i, NT))]
                    if i < NT:
                        parts.append((c_before, chosen[:, i, :]))
                    for m, (a, b) in enumerate(parts):
                        mm = nc.tensor.matmul(ps[:, bank, EXPERTS * i:EXPERTS * (i + 1)], a, b, start=(m == 0),
                                              stop=(m == len(parts) - 1))
                ring.fill(mm)

            diags = [0]

            def places_everywhere(ring):
                diags[0] += 1
                pe.wait_ge(diag_made, diags[0])
                bank = ring.claim(pe)
                for i in range(NT):
                    mm = nc.tensor.matmul(ps[:, bank, P * i:P * (i + 1)], c_all, c_diag[:, i, :], start=True, stop=True)
                ring.fill(mm)

            tiles_done = [0]

            def tiles(n_tiles, first_slot, up, down_chunks, w2_at, start_sums, gate=False, ahead=None):
                g0 = fillsS.n
                t0 = tiles_done[0]
                banks = [(fillsV.n + i) % 4 for i in range(NT)]
                pe.wait_ge(ringV.emptied, fillsV.n)
                start_sums(banks)

                def gather(j):
                    pe.wait_ge(gather_made, j + (t0 + 1))
                    bank = ringS.claim(pe)
                    for c in range(C):
                        for i in range(NT):
                            for m, rows_of in enumerate((c_hi, c_lo)):
                                mm = nc.tensor.matmul(ps[:, bank, P * c:P * (c + 1)], rows_of[:, i, P * c:P * (c + 1)],
                                                      c_sel[:, i, :], start=(i == 0 and m == 0),
                                                      stop=(i == NT - 1 and m == 1))
                    ringS.fill(mm)

                def products(j, k):
                    for half_of in range(2):
                        bank = ringS.claim(pe)
                        for f in range(4):
                            o = 4 * half_of + f
                            for c in range(C):
                                mm = nc.tensor.matmul(ps[:, bank, P * f:P * (f + 1)], up(k)[:, c, P * o:P * (o + 1)],
                                                      c_xg[:, c, :], start=(c == 0), stop=(c == C - 1))
                        ringS.fill(mm)

                def scatter(j, last=False):
                    pe.wait_ge(out_split, j + (t0 + 1))
                    for i in range(NT):
                        for m, part in enumerate((c_ohi, c_olo)):
                            mm = nc.tensor.matmul(ps[:, banks[i], :], c_selT[:, P * i:P * (i + 1)], part, start=False,
                                                  stop=(last and m == 1))
                        if last:
                            ringV.fill(mm)
                    if not last:
                        mm.then_inc(scattered, 1)

                def down_halves(j):
                    pe.wait_ge(w2_split, j * 2 + 2 * (t0 + 1))
                    pe.wait_ge(hid_split, j * 2 + 2 * (t0 + 1))
                    group(ringS, lambda b: ps[:, b, :],
                          [(c_hid16[m][:, f, :], c_w2[n][:, f, :]) for f in range(down_chunks)
                           for m, n in ((0, 0), (0, 1), (1, 0))])

                def down(j, k):
                    bank = ringS.claim(pe)
                    w2 = wbuf[:, k % 2, w2_at:w2_at + D * down_chunks].rearrange("p (c n) -> p c n", c=down_chunks)
                    for f in range(down_chunks):
                        mm = nc.tensor.matmul(ps[:, bank, :], c_hid[:, f, :], w2[:, f, :], start=(f == 0),
                                              stop=(f == down_chunks - 1))
                    ringS.fill(mm)

                def step(j, k, slot_count, first=False, last=False):
                    pe.wait_ge(slot_in[k % 2], slot_count)
                    if first:
                        pe.wait_ge(ringS.emptied, g0 + 1)
                    else:
                        pe.wait_ge(ringS.emptied, j * 4 + (g0 + (2 if ahead and last else 0)))
                    products(j, k)
                    if not last:
                        gather(j + 1)
                    if not first:
                        scatter(j - 1)
                    if gate:
                        pe.wait_ge(hid_made, j + 1)
                        down(j, k)
                    else:
                        down_halves(j)
                    pe.drain().then_inc(slot_free, 1)

                gather(0)
                step(0, first_slot, filled_at[first_slot], first=True)
                loops = (n_tiles - 3) // 2
                with pe.Fori(0, loops, 1) as it:
                    with fillsS.loop(it, 0, loops, 8):
                        for m in range(2):
                            k = first_slot + 1 + m
                            step(it * 2 + (1 + m), k, it * 32 + filled_at[k])
                for j in (n_tiles - 2, n_tiles - 1):
                    if ahead and j == n_tiles - 2:
                        ahead[0]()
                    step(j, first_slot + j, filled_at[first_slot + j], last=(j == n_tiles - 1))
                if ahead:
                    ahead[1]()
                scatter(n_tiles - 1, last=True)
                tiles_done[0] += n_tiles
                marks.setdefault("tiles", []).append(g0)

            def stage_c():
                turn("C", h_tok)
                all_emptied(ringV)
                router(col("gate_W"))
                pe.wait_ge(stage_w_in, 16 * (2 + ("B" in stages)))

                def route(ring, k):
                    bank = ring.claim(pe)
                    for i in range(NT):
                        mm = nc.tensor.transpose(ps[0:EXPERTS, bank, P * i:P * (i + 1)], c_oh[:, k, i, :], ident)
                    ring.fill(mm)
                    ranks(ring, c_oh[:, k])

                def bias_rows(banks):
                    for i in range(NT):
                        nc.tensor.matmul(ps[:, banks[i], :], c_ohT[0:EXPERTS, P * i:P * (i + 1)], c_b2[0:EXPERTS],
                                         start=True, stop=False)

                pe.wait_ge(oh_made, 1)
                route(ringV, 0)
                places_everywhere(ringV)
                for k in range(2):
                    all_emptied(ringS, ringV)
                    pe.wait_ge(split_made, k + 1)
                    tiles(TILES_C, 4 + TILES_C * k, lambda s: slot(s, 0, 4096, c=C), 8, 4096, bias_rows,
                          ahead=(lambda: route(ringS, 1), lambda: places_everywhere(ringS)) if k == 0 else None)

            def stage_f():
                turn("F", h_tok)
                all_emptied(ringV)
                router(col("router"))
                pe.wait_ge(stage_w_in, w_in_F)
                pe.wait_ge(oh_made, (1 if "C" in stages else 0) + 1)
                ranks(ringV, c_ohc)
                for _ in range(4):
                    places_everywhere(ringV)
                all_emptied(ringV)
                pe.wait_ge(split_made, (2 if "C" in stages else 0) + 1)

                def residual(banks):
                    for i in range(NT):
                        nc.tensor.matmul(ps[:, banks[i], :], ident, x[:, i, :], start=True, stop=False)

                tiles(TILES_F, 29, lambda s: slot(s, 0, 4096, c=C), 4, 4096, residual, gate=True)

            def stage_d():
                wq_c, wk_s, wk_c, wq_s = (slot(26, 2048 * j, 2048 * (j + 1), c=C) for j in range(4))
                wv_c, wv_s = (slot(27, 2048 * j, 2048 * (j + 1), c=C) for j in range(2))
                wg = slot(27, 4096, 8192, c=8)
                turn("D", h_tok)
                pe.wait_ge(slot_in[0], filled_at[26])
                all_emptied(ringV)
                square(ringS, wq_c, hT)
                square(ringS, wk_c, hT)
                all_emptied(ringS)
                square(ringS, wk_s, d_qcT)
                square(ringS, wq_s, d_kcT)
                marks["qk"] = fillsS.n
                pe.drain().then_inc(slot_free, 1)
                group(ringV, lambda k: ps[0:1, k, :], [(col("bq_s")[:, c:c + 1], d_kcT[:, c, :]) for c in range(C)])
                for b in range(B):
                    group(ringV, lambda k: ps[0:S, k, 0:1],
                          [(d_qcT[:, c, S * b:S * (b + 1)], col("bk_s")[:, c:c + 1]) for c in range(C)])
                pe.wait_ge(slot_in[1], filled_at[27])
                for i in range(NT):
                    to_rows(ringV, hT, wv_c, i)
                all_emptied(ringS, ringV)
                pe.wait_ge(d_vectors, 1)

                def scores(b):
                    pe.wait_ge(qkb_made, b + 1)
                    pe.wait_ge(ctx_in, b * 32 + (ctx0 + 32))
                    for lo, hi in CHUNKS:
                        group(ringV, lambda k: ps[0:S, k, 0:hi - lo],
                              [(d_qk_b[:, c, :], d_ctxT[:, c, lo:hi]) for c in range(C)])
                    bank = ringV.claim(pe)
                    pe.wait_ge(picked, b + 1)
                    for c in range(C):
                        nc.tensor.matmul(ps[:, bank, 0:S], d_sel[:, c, :], d_g2T[:, c, bass.ds(b * S, S)],
                                         start=(c == 0), stop=False)
                    mm = nc.tensor.matmul(ps[:, bank, 0:S], d_ones, d_bqk[:, bass.ds(b * S, S)], start=False, stop=True)
                    ringV.fill(mm)

                def turn_probs(b):
                    pe.wait_ge(probs_made, b + (probs0 + 1))
                    held(pe)
                    for g in range(5):
                        ring = (ringS, ringV)[g % 2]
                        bank = ring.claim(pe)
                        held(pe)
                        for j, kt in enumerate(range(3 * g, min(3 * g + 3, KT_TILES))):
                            n = min(P, S2 - P * kt)
                            mm = nc.tensor.transpose(ps[0:n, bank, S * j:S * (j + 1)], d_S[:, P * kt:P * kt + n],
                                                     ident[0:S, 0:S])
                        ring.fill(mm)
                    return [(ring, ring.fills.off + ring.fills.n) for ring in (ringS, ringV)]

                def weigh_ctx(b, turned_at):
                    for ring, count in turned_at:
                        pe.wait_ge(ring.emptied, count)
                    pe.wait_ge(ctxn_in, b * 32 + 32)
                    group(ringV, lambda k: ps[0:S, k, :],
                          [(d_PT[0:min(P, S2 - P * kt), kt, :], d_ctx[0:min(P, S2 - P * kt), kt, :])
                           for kt in range(KT_TILES)])

                marks["D loop start"] = fillsV.n
                scores(0)
                with pe.Fori(1, B, 1) as b:
                    with fillsV.loop(b, 1, B - 1, 8), fillsS.loop(b, 1, B - 1, 3):
                        turned_at = turn_probs(b - 1)
                        scores(b)
                        weigh_ctx(b - 1, turned_at)
                turned_at = turn_probs(B - 1)
                pe.wait_ge(s2_made, B)
                for i in range(NT):
                    group(ringS, lambda k: ps[:, k, 0:S], [(flat(d_P2_all)[:, P * i:P * (i + 1)], col("interp"))])
                all_emptied(ringS)
                for c in range(C):
                    bank = ringS.claim(pe)
                    for i in range(NT):
                        mm = nc.tensor.matmul(ps[:, bank, P * i:P * (i + 1)], d_Vc[:, i, P * c:P * (c + 1)],
                                              d_P2T[:, i, :], start=True, stop=True)
                    ringS.fill(mm)
                weigh_ctx(B - 1, turned_at)
                marks["D loop end"] = fillsV.n
                all_emptied(ringV)
                for c in range(C):
                    bank = ringS.claim(pe)
                    for b in range(B):
                        mm = nc.tensor.transpose(ps[:, bank, S * b:S * (b + 1)], d_pc[:, b, P * c:P * (c + 1)], ident[0:S, 0:S])
                    ringS.fill(mm)
                all_emptied(ringS)
                square(ringS, wv_s, d_pcT)
                all_emptied(ringS)
                marks["gate"] = fillsS.n

                def gated_rows(c):
                    pe.wait_ge(gated_made, c + 1)
                    bank = ringV.claim(pe)
                    for i in range(NT):
                        mm = nc.tensor.transpose(ps[:, bank, P * i:P * (i + 1)], d_gate[:, c, P * i:P * (i + 1)], ident)
                    ringV.fill(mm)

                for o in range(C):
                    group(ringS, lambda k: ps[:, k, :],
                          [(wg[:, c, P * o:P * (o + 1)], (d_c2s, d_s2c)[c // 4][:, c % 4, :]) for c in range(8)])
                    if o:
                        gated_rows(o - 1)
                pe.drain().then_inc(slot_free, 1)
                gated_rows(C - 1)

            def stage_e():
                w_in, w_out = slot(28, 0, 4096, c=C), slot(28, 4096, 8192, c=8)
                turn("E", h_tok)
                pe.wait_ge(slot_in[0], filled_at[28])
                all_emptied(ringV)
                marks["conv"] = fillsV.n
                square(ringV, w_in, hT, outs=8)
                pe.wait_ge(stage_w_in, w_in_E)
                group(ringS, lambda k: ps[0:S, k, :], [(e_wx[:, c, :], e_xv[:, c, :]) for c in range(8)],
                      lambda c: pe.wait_ge(xv_made, c + 1))
                all_emptied(ringS)
                for c in range(8):
                    group(ringS, lambda k: ps[:, k, :], [(e_wdt[0:RANK, P * c:P * (c + 1)], e_ssm[0:RANK, :])])
                marks["dt"] = fillsS.n
                for g in range(NS // G):
                    for first in (0, NS):
                        for n in range(first + G * g, first + G * (g + 1)):
                            group(ringS, lambda k: ps[:, k, :],
                                  [(ident[0:S, RANK + n:RANK + n + 1].broadcast_to([S, P]), e_ssm[0:S, :])])
                all_emptied(ringS, ringV)

                def project(c):
                    pe.wait_ge(y_taken, c + 1)
                    for i in range(NT):
                        mm = nc.tensor.matmul(ps[:, 4 + i, :], e_dx[:, c, P * i:P * (i + 1)], w_out[:, c, :],
                                              start=(c == 0), stop=(c == 7))
                        if c == 7:
                            mm.then_inc(rows_summed, 1)

                for c in range(8):
                    if c >= 4:
                        pe.wait_ge(y_taken, c - 3)
                    for g in range(NS // G):
                        if g == 2 and c:
                            project(c - 1)
                        pe.wait_ge(hc_made, c * (NS // G) + g + 1)
                        for n in range(G):
                            mm = nc.tensor.matmul(ps[:, c % 4, :], ident, e_hC[:, g % 2, N * n:N * (n + 1)],
                                                  start=(g == 0 and n == 0), stop=(g == NS // G - 1 and n == G - 1))
                        mm.then_inc(y_made, 1)
                project(7)
                pe.drain().then_inc(slot_free, 1)

            for st, run, n in (("A", stage_a, 1), ("B", stage_b, 3), ("C", stage_c, 2 * TILES_C), ("D", stage_d, 2),
                               ("E", stage_e, 1), ("F", stage_f, TILES_F)):
                if st in stages:
                    run()
                else:
                    pe.sem_inc(slot_free, n)
                    if st == "A":
                        pe.sem_inc(kt_free, 1)


        @block.scalar
        def _(act):
            takes = ringS.takes
            norms = [0]

            def norm():
                norms[0] += 1
                act.wait_ge(ln_var, norms[0])
                nc.scalar.activation(ln_sd, ln_mv[:, :, 1], ACT.Sqrt, bias=ln_eps).then_inc(ln_std, 1)

            def from_bank(out, part, func, **kw):
                bank = ringS.take(act)
                ringS.empty(nc.scalar.activation(out, part(bank), func, **kw))

            def whole(k):
                return ps[:, k, :]

            act.wait_ge(in_consts, 32)
            act.wait_ge(eps_made, 1)

            def stage_a():
                norm()
                act.wait_ge(slot_in[0], 48)
                for k, dst in enumerate((a_wk, a_wv)):
                    if k:
                        act.wait_ge(w_split, 1)
                    nc.scalar.activation(flat(dst[0]), wbuf[:, 0, 2048 * (k + 1):2048 * (k + 2)], ACT.Copy,
                                         scale=W_UP).then_inc(w_hi, 1)
                seenV = Side()
                seenV.n = marks["turn A"]

                def upper(ring, takes, out, part, scale):
                    act.wait_ge(ring.filled, takes.off + (takes.n + 1))
                    bank = ring.banks[takes.n % len(ring.banks)]
                    nc.scalar.activation(out, part(bank), ACT.Copy, scale=scale).then_inc(hi_made, 1)
                    takes.n += 1

                def ctx_upper(b, c):
                    act.wait_ge(stage_in[c % 2], b * 32 + 16 * (c // 2 - 1))
                    nc.scalar.activation(a_ctx[0][:, c, :], a_stage[c % 2], ACT.Copy).then_inc(ctx_hi, 1)

                act.wait_ge(ctx_in, 16)
                for c in range(C):
                    nc.scalar.activation(a_ctx[0][:, c, :], a_ctx0[:, c, :], ACT.Copy).then_inc(ctx_hi, 1)
                for o in range(C):
                    from_bank(a_QT[:, o, :], whole, ACT.Copy, scale=float(HD) ** -0.5)

                def k_tile(i):
                    o, (lo, hi) = i // 4, CHUNKS[i % 4]
                    upper(ringS, takes, a_KT[0][:, o, lo:hi], lambda k: ps[:, k, 0:hi - lo], 1 / W_UP)

                def turn_probs(p):
                    for g in range(4):
                        ring, side = ((ringS, takes), (ringV, seenV))[g % 2]
                        if g < 3:
                            upper(ring, side, a_PT[p % 2][0][:, 4 * g:4 * g + 4, :],
                                  lambda k: ps[:, k, :].rearrange("p (j n) -> p j n", j=4), P_UP)
                        else:
                            upper(ring, side, a_PT[p % 2][0][0:LAST, 12, :], lambda k: ps[0:LAST, k, 0:P], P_UP)

                def exps(b, p):
                    act.wait_ge(row_max, b * PAIRS + (p + 1))
                    nc.scalar.activation(a_S[:, p % 2, :], a_S[:, p % 2, :], ACT.Exp, bias=a_nm[:, p:p + 1],
                                         accum_out=a_rs[:, p:p + 1]).then_inc(probs_made, 1)

                def odd_bias(b, p):
                    act.wait_ge(bias_made[0], b * 4 + 1)
                    if not isinstance(b, int) or b or p > 1:
                        act.wait_ge(row_max, b * PAIRS + (p - 1))
                    nc.scalar.activation(a_bias[:, 1, :], a_dist, ACT.Copy, scale=col("slopes")[:, p:p + 1]) \
                        .then_inc(bias_made[1], 1)

                def head(b, first):
                    for i in range(4):
                        k_tile(i)
                    if not first:
                        turn_probs(6)
                        exps(b - 1, 7)
                        seenV.n += 1
                    for i in range(4, 8):
                        k_tile(i)
                    if not first:
                        turn_probs(7)
                        seenV.n += 1
                    for i in range(8, 12):
                        k_tile(i)
                    if not first:
                        seenV.n += 1
                    odd_bias(b, 1)
                    for i in range(12, 16):
                        k_tile(i)
                    for i in range(12):
                        upper(ringS, takes, a_Vparts[:, i, :, 0, :], lambda k: ps[:, k, :].rearrange("p (h n) -> p h n", h=PAIRS),
                              1 / W_UP)
                        if i == 5:
                            exps(b, 0)
                        if i == 10:
                            odd_bias(b, 3)
                    seenV.n += 8
                    for q in range(4):
                        upper(ringV, seenV, a_Vparts[0:LAST, KT_TILES - 1, 2 * q:2 * q + 2, 0, :],
                              lambda k: ps[0:LAST, k, 0:P].rearrange("p (h n) -> p h n", h=2), 1 / W_UP)

                def pairs(b, more=True):
                    for p in range(6):
                        turn_probs(p)
                        exps(b, p + 1)
                        seenV.n += 5 if p else 4
                        if p in (2, 4):
                            odd_bias(b, p + 3)
                        if more and p in SPLIT_AT:
                            ctx_upper(b + 1, SPLIT_AT.index(p))

                head(0, True)
                with act.Fori(1, B, 1) as b:
                    with takes.loop(b, 1, B - 1, 44), seenV.loop(b, 1, B - 1, 60):
                        pairs(b - 1)
                        head(b, False)
                pairs(B - 1, more=False)
                turn_probs(6)
                exps(B - 1, 7)
                seenV.n += 1
                turn_probs(7)
                for c in range(C):
                    from_bank(a_attnT[:, c, :], whole, ACT.Copy)

            def stage_b():
                nc.scalar.activation(b_w, col("decay"), ACT.Exp).then_inc(wkv_exp, 1)
                norm()
                norm()

                def halves(mixes, mark):
                    act.wait_ge(ringV.emptied, marks[mark])
                    for name, dst in mixes:
                        for c in range(C):
                            nc.scalar.activation(dst[:, c, :], b_xxT[:, c, :], ACT.Copy, scale=col(name)[:, c:c + 1]) \
                                .then_inc(mix_half, 1)

                halves([("mix_k", b_mk), ("mix_v", b_mv), ("mix_r", b_mr)], "turn B")

                def by_time(k):
                    return ps[:, k, :].rearrange("p (t s) -> p t s", t=B)

                def project(name):
                    dst, func, scale = {"k": (b_k, ACT.Copy, 1.0), "v": (b_v, ACT.Copy, 1.0), "r": (b_r, ACT.Exp, -1.0)}[name[0]]
                    from_bank(dst[:, int(name[1]), :].rearrange("p (s t) -> p t s", t=B), by_time, func, scale=scale)

                def exps(c):
                    act.wait_ge(wkv_arg, c + 1)
                    v = flat(b_wkv[c][:, 0:4])
                    nc.scalar.activation(v, v, ACT.Exp).then_inc(wkv_exp, 1)

                for n, name in enumerate(KVR_ORDER):
                    project(name)
                    if n in (2, 4):
                        exps(n // 2 - 1)
                exps(2)
                exps(3)
                norm()
                halves([("cmix_k", b_mk), ("cmix_r", b_mv)], "turn B2")
                for f in range(16):
                    from_bank(b_kk[:, f, :], whole, ACT.Relu)
                for i in range(NT):
                    from_bank(b_rr[:, i, :], whole, ACT.Exp, scale=-1.0)

            gates = [0]

            def gate_exps():
                gates[0] += 1
                act.wait_ge(gate_arg, gates[0])
                for i in range(NT):
                    nc.scalar.activation(c_e8[:, i, :], c_m8[:, i, :], ACT.Exp, bias=c_nmx[:, i:i + 1],
                                         accum_out=c_sum[:, i:i + 1]).then_inc(gate_exp, 1)

            relus = Side()

            def tiles(n_tiles, hidden, first_slot, scale, weighed=False, ahead=None):
                def gathered():
                    from_bank(c_xg, lambda k: ps[:, k, :].rearrange("p (c n) -> p c n", c=C), ACT.Copy)

                def step(j, k, slot_count, last=False):
                    hidden(k, slot_count)
                    if not last:
                        gathered()
                    if weighed:
                        act.wait_ge(wcol_made, j + 1)
                    bank = ringS.take(act)
                    nc.scalar.activation(c_ohi, ps[:, bank, :], ACT.Copy, **scale)
                    ringS.empty(nc.scalar.activation(flat(c_rows), ps[:, bank, :], ACT.Copy, **scale))

                gathered()
                step(0, first_slot, filled_at[first_slot])
                loops = (n_tiles - 3) // 2
                with act.Fori(0, loops, 1) as it:
                    with takes.loop(it, 0, loops, 8), relus.loop(it, 0, loops, 0 if weighed else 12):
                        for m in range(2):
                            k = first_slot + 1 + m
                            step(it * 2 + (1 + m), k, it * 32 + filled_at[k])
                for j in (n_tiles - 2, n_tiles - 1):
                    if ahead and j == n_tiles - 2:
                        ahead[0]()
                    step(j, first_slot + j, filled_at[first_slot + j], last=(j == n_tiles - 1))
                if ahead:
                    ahead[1]()

            def stage_c():
                norm()
                gate_exps()

                def hidden(k, slot_count):
                    act.wait_ge(slot_in[k % 2], slot_count)
                    for m in range(2):
                        nc.scalar.activation(flat(c_w2[0])[:, 2048 * m:2048 * (m + 1)],
                                             wbuf[:, k % 2, 4096 + 2048 * m:4096 + 2048 * (m + 1)], ACT.Copy,
                                             scale=W_UP).then_inc(w2_hi, 1)
                    for half_of in range(2):
                        bank = ringS.take(act)
                        for f in range(4):
                            o = 4 * half_of + f
                            ins = nc.scalar.activation(c_hid[:, o, :], ps[:, bank, P * f:P * (f + 1)], ACT.Relu,
                                                       bias=wbuf[:, k % 2, 8192 + o:8193 + o])
                            if f < 3:
                                ins.then_inc(relu_made, 1)
                        ringS.empty(ins)
                        relus.n += 3
                        act.wait_ge(relu_made, relus.off + relus.n)
                        act.wait_ge(ringS.emptied, takes.off + takes.n)
                        nc.scalar.activation(c_hid16[0][:, 4 * half_of:4 * half_of + 4, :],
                                             c_hid[:, 4 * half_of:4 * half_of + 4, :], ACT.Copy).then_inc(hid_hi, 1)

                def routed():
                    from_bank(c_ohT[0:EXPERTS], lambda k: ps[0:EXPERTS, k, :], ACT.Copy)
                    from_bank(flat(c_rk), lambda k: ps[:, k, 0:(NT + 1) * EXPERTS], ACT.Copy)

                for k in range(2):
                    tiles(TILES_C, hidden, 4 + TILES_C * k, {"scale": 1 / W_UP},
                          ahead=(routed, lambda: from_bank(c_bc[:, 1, :], whole, ACT.Copy)) if k == 0 else None)
                norm()

            def stage_d():
                norm()
                for dst, bias in ((d_qcT, "bq_c"), (d_kcT, "bk_c")):
                    for c in range(C):
                        from_bank(dst[:, c, :], whole, ACT.Identity, bias=col(bias)[:, c:c + 1])
                for dst in (d_qkT, d_g2T):
                    for c in range(C):
                        from_bank(dst[:, c, :], whole, ACT.Copy)
                def exps(b):
                    act.wait_ge(row_max, b + (probs0 + 1))
                    nc.scalar.activation(d_S, d_S, ACT.Exp, bias=d_nm[0:S, 0:1],
                                         accum_out=d_rs[0:S, 0:1]).then_inc(probs_made, 1)
                    act.wait_ge(s2_arg, b + 1)
                    nc.scalar.activation(d_P2, d_P2, ACT.Exp, bias=d_nm[:, 1:2],
                                         accum_out=d_rs[:, 1:2]).then_inc(s2_exp, 1)

                def turn_probs():
                    for g in (0, 2):
                        from_bank(d_PT[:, 3 * g:3 * g + 3, :],
                                  lambda k: ps[:, k, 0:3 * S].rearrange("p (j n) -> p j n", j=3), ACT.Copy)
                    from_bank(d_PT[0:LAST, KT_TILES - 1, :], lambda k: ps[0:LAST, k, 0:S], ACT.Copy)

                exps(0)
                with act.Fori(1, B, 1) as b:
                    with takes.loop(b, 1, B - 1, 3):
                        turn_probs()
                        exps(b)
                turn_probs()
                act.wait_ge(d_vectors, 1)
                for i in range(NT):
                    bank = ringS.take(act)
                    nc.scalar.activation(d_P2T[0:S, i, 0:S], ps[0:S, bank, 0:S], ACT.Copy)
                    ringS.empty(nc.scalar.activation(d_P2T[S:P, i, S:P], ps[S:P, bank, 0:S], ACT.Copy))
                for dst in (d_s2c, d_pcT):
                    for c in range(C):
                        from_bank(dst[:, c, :], whole, ACT.Copy)
                for c in range(C):
                    from_bank(d_c2s[:, c, :], whole, ACT.Identity, bias=col("bv_s")[:, c:c + 1])
                act.wait_ge(nbg_made, 1)
                for c in range(C):
                    from_bank(d_gate[:, c, :], whole, ACT.Exp, scale=-1.0, bias=d_nbg[:, c:c + 1])

            def stage_e():
                nc.scalar.activation(e_negA, col("A_log"), ACT.Exp).then_inc(neg_a, 1)
                norm()
                def silu_exp(c):
                    act.wait_ge(ringV.emptied, marks["conv"] + c + 1)
                    nc.scalar.activation(e_de[:, c, :], e_dx[:, c, :], ACT.Exp, scale=-1.0).then_inc(conv_exp, 1)

                cw, cb = col("conv_w"), col("conv_b")
                for c in range(8):
                    act.wait_ge(ringV.filled, marks["conv"] + c + 1)
                    nc.scalar.activation(e_dx[:, c, :], ps[:, ringV.banks[(marks["conv"] + c) % 4], :], ACT.Identity,
                                         scale=cw[:, TAPS * (c + 1) - 1:TAPS * (c + 1)],
                                         bias=cb[:, c:c + 1]).then_inc(conv_tap, 1)
                    if c:
                        silu_exp(c - 1)
                silu_exp(7)
                from_bank(e_ssm[0:S], lambda k: ps[0:S, k, :], ACT.Copy)
                def small_exp(c):
                    act.wait_ge(dt_arg, c + 1)
                    nc.scalar.activation(e_dx[:, c, :], flat(e_dA)[:, N * c:N * (c + 1)], ACT.Exp).then_inc(dt_exp, 1)

                for c in range(8):
                    from_bank(e_de[:, c, :], whole, ACT.Identity, bias=col("b_dt")[:, c:c + 1])
                    if c:
                        small_exp(c - 1)
                small_exp(7)
                for c in range(8):
                    act.wait_ge(dt_exp, c + 1)
                    nc.scalar.activation(flat(e_h)[:, N * c:N * (c + 1)], e_dx[:, c, :], ACT.Ln, bias=1.0).then_inc(dt_ln, 1)
                act.wait_ge(neg_a, 2)

                def decays(c, g):
                    k = c * (NS // G) + g
                    if k >= 2:
                        act.wait_ge(h_made, k - 1)
                    else:
                        act.wait_ge(dt_exp, 8)
                    if g == 0:
                        act.wait_ge(delta_made, c + 1)
                    for n in range(G):
                        a = NS * c + G * g + n
                        ins = nc.scalar.activation(e_dA[:, g % 2, N * n:N * (n + 1)], e_de[:, c, :], ACT.Exp,
                                                   scale=e_negA[:, a:a + 1])
                    ins.then_inc(da_made, 1)

                for g in range(NS // G):
                    for n in range(G * g, G * (g + 1)):
                        from_bank(e_B[:, N * n:N * (n + 1)], whole, ACT.Copy)
                    for n in range(G * g, G * (g + 1)):
                        from_bank(e_C[n // 8][:, N * (n % 8):N * (n % 8 + 1)], whole, ACT.Copy)
                    if g < 2:
                        decays(0, g)
                for c in range(8):
                    for g in range(NS // G):
                        if c or g >= 2:
                            decays(c, g)

            def stage_f():
                norm()
                gate_exps()

                def hidden(k, slot_count):
                    bank = ringS.take(act)
                    nc.scalar.activation(flat(c_h1), ps[:, bank, :], ACT.Copy)
                    ringS.empty(nc.scalar.activation(flat(c_e), ps[:, bank, :], ACT.Exp, scale=-1.0))
                    from_bank(flat(c_h2), whole, ACT.Copy)

                tiles(TILES_F, hidden, 29, {"scale": c_wcol[:, 0:1]}, weighed=True)

            for st, run in (("A", stage_a), ("B", stage_b), ("C", stage_c), ("D", stage_d), ("E", stage_e), ("F", stage_f)):
                if st in stages:
                    run()

        @block.gpsimd
        def _(pool):
            chain = Chain(pool, pool_done)
            pool.wait_ge(in_consts, 32)

            def stage_a():
                def distances(b):
                    pool.wait_ge(pos_in, b * 64 + 64)
                    held(pool)
                    nc.gpsimd.tensor_scalar(a_dist, a_dist.bitcast(I32), a_qpos.bitcast(I32), None, ALU.subtract)
                    chain.link(nc.gpsimd.tensor_scalar(a_mask, a_mask.bitcast(I32), 0.0, -1e30, ALU.is_equal, ALU.mult))
                    chain.link(nc.gpsimd.tensor_tensor(a_dist, a_dist, a_mask, ALU.add))

                def even_bias(b, p, first=False):
                    if not first:
                        pool.wait_ge(row_max, b * PAIRS + (p - 1))
                        held(pool)
                    nc.gpsimd.tensor_scalar(a_bias[:, 0, :], a_dist, col("slopes")[:, p:p + 1], None,
                                            ALU.mult).then_inc(bias_made[0], 1)

                def ctx_lower(b, c):
                    pool.wait_ge(ctx_hi, b * 4 + (c + 1))
                    held(pool)
                    nc.gpsimd.tensor_tensor(a_ctx[1][:, c, :], a_stage[c % 2], a_ctx[0][:, c, :],
                                            ALU.subtract).then_inc(ctx_split, 1)

                distances(0)
                even_bias(0, 0, first=True)
                even_bias(0, 2)
                with pool.Fori(1, B, 1) as b:
                    with chain.loop(b, 1, B - 1, 2):
                        even_bias(b - 1, 4)
                        ctx_lower(b, 0)
                        ctx_lower(b, 1)
                        even_bias(b - 1, 6)
                        ctx_lower(b, 2)
                        ctx_lower(b, 3)
                        distances(b)
                        even_bias(b, 0)
                        even_bias(b, 2)
                even_bias(B - 1, 4)
                even_bias(B - 1, 6)

            def stage_e():
                for c in range(8):
                    pool.wait_ge(conv_exp, c + 1)
                    nc.gpsimd.tensor_scalar(e_de[:, c, :], e_de[:, c, :], 1.0, None, ALU.add).then_inc(conv_sum, 1)
                    if c:
                        pool.wait_ge(conv_inv, c)
                        nc.gpsimd.tensor_tensor(e_xv[:, c - 1, :], e_dx[:, c - 1, :], e_de[:, c - 1, :],
                                                ALU.mult).then_inc(xv_made, 1)
                pool.wait_ge(conv_inv, 8)
                nc.gpsimd.tensor_tensor(e_xv[:, 7, :], e_dx[:, 7, :], e_de[:, 7, :], ALU.mult).then_inc(xv_made, 1)

            def stage_d():
                def pick(b):
                    pool.wait_ge(ctx_in, b * 32 + (ctx0 + 32))
                    held(pool)
                    rows_of = d_ctxT[:, :, 0:S * STRIDE].rearrange("p c (i r) -> p c i r", r=STRIDE)
                    for k in range(2):
                        ins = nc.gpsimd.tensor_copy(d_sel[:, :, S * k:S * (k + 1)], rows_of[:, :, :, PICK + k])
                    ins.then_inc(picked, 1)

                pick(0)
                with pool.Fori(1, B, 1) as b:
                    pool.wait_ge(s2_arg, b)
                    pick(b)

            def stage_c():
                pool.wait_ge(ln_rows, NT * (NORMS.index("C") + 1))
                for i in range(NT):
                    nc.gpsimd.tensor_tensor(x[:, i, :], x[:, i, :], row("beta"), ALU.add).then_inc(shifted, 1)

            if "A" in stages:
                stage_a()
            if "C" in stages:
                stage_c()
            if "D" in stages:
                stage_d()
            if "E" in stages:
                stage_e()

        @block.vector
        def _(dve):
            V = nc.vector
            chain = Chain(dve, dve_done)
            link = chain.link
            takes = ringV.takes
            norms = [0]
            halves_seen = [0]

            def own():
                dve.wait_ge(ringV.emptied, takes.off + takes.n)

            def add_bank(dst, i):
                bank = ringV.take(dve)
                ringV.empty(V.tensor_tensor(dst[:, i, :], dst[:, i, :], ps[:, bank, :], ALU.add))
                own()
                chain.done(V.bn_stats(ln_st[:, 6 * i:6 * i + 6], dst[:, i, :]))

            def moments(src, begun=False):
                if not begun:
                    for i in range(NT):
                        chain.done(V.bn_stats(ln_st[:, 6 * i:6 * i + 6], src[:, i, :]))
                chain.wait()
                for i in range(NT):
                    ins = V.bn_aggr(ln_mv[:, i, :], ln_st[:, 6 * i:6 * i + 6])
                ins.then_inc(ln_var, 1)
                norms[0] += 1
                dve.wait_ge(ln_std, norms[0])
                link(V.reciprocal(ln_rstd, ln_sd))

            def norm(src, dst, begun=False):
                moments(src, begun)
                for i in range(NT):
                    V.tensor_scalar(dst[:, i, :], src[:, i, :], ln_mv[:, i, 0:1], ln_rstd[:, i:i + 1],
                                    ALU.subtract, ALU.mult).then_inc(ln_rows, 1)

            def own_rows():
                dve.wait_ge(ln_rows, NT * norms[0])

            def turned(dst, gain=None):
                for i in range(NT):
                    bank = ringV.take(dve)
                    if gain is None:
                        ins = V.tensor_copy(dst[:, :, P * i:P * (i + 1)], ps[:, bank, :].rearrange("p (c n) -> p c n", c=C))
                    else:
                        for c in range(C):
                            ins = V.tensor_scalar(dst[:, c, P * i:P * (i + 1)], ps[:, bank, P * c:P * (c + 1)],
                                                  col(gain + "_g")[:, c:c + 1], col(gain + "_b")[:, c:c + 1],
                                                  ALU.mult, ALU.add)
                    ringV.empty(ins)

            link(V.memset(ln_eps, 1e-5))
            V.memset(a_Qbd_all, 0.0).then_inc(eps_made, 1)
            dve.wait_ge(eps_made, 1)
            dve.wait_ge(in_consts, 32)
            dve.wait_ge(in_x, 16)

            def stage_a():
                norm(x, h_tok)
                turned(hT)
                for k, dst in enumerate((a_wk, a_wv)):
                    dve.wait_ge(w_hi, k + 1)
                    V.scalar_tensor_tensor(out=flat(dst[1]), in0=wbuf[:, 0, 2048 * (k + 1):2048 * (k + 2)], scalar=W_UP,
                                           in1=flat(dst[0]), op0=ALU.mult, op1=ALU.subtract).then_inc(w_split, 1)
                seenS, uppers = Side(), Side()
                seenS.n = marks["q"]

                def lower(ring, side, hi, lo, part, scale):
                    dve.wait_ge(hi_made, uppers.off + (uppers.n + 1))
                    bank = ring.banks[side.n % len(ring.banks)]
                    V.scalar_tensor_tensor(out=lo, in0=part(bank), scalar=scale, in1=hi, op0=ALU.mult,
                                           op1=ALU.subtract).then_inc(ring.emptied, 1)
                    side.n += 1
                    uppers.n += 1

                def k_tiles(i0, i1):
                    for i in range(i0, i1):
                        o, (lo, hi) = i // 4, CHUNKS[i % 4]
                        lower(ringS, seenS, a_KT[0][:, o, lo:hi], a_KT[1][:, o, lo:hi], lambda k: ps[:, k, 0:hi - lo], 1 / W_UP)

                def turn_probs(p):
                    for g in range(4):
                        ring, side = ((ringS, seenS), (ringV, takes))[g % 2]
                        if g < 3:
                            lower(ring, side, *(h[:, 4 * g:4 * g + 4, :] for h in a_PT[p % 2]),
                                  lambda k: ps[:, k, :].rearrange("p (j n) -> p j n", j=4), P_UP)
                        else:
                            lower(ring, side, *(h[0:LAST, 12, :] for h in a_PT[p % 2]), lambda k: ps[0:LAST, k, 0:P], P_UP)

                def add_bias(b, p, j, first):
                    lo, hi = CHUNKS[j]
                    if j == 0:
                        if not first or p:
                            dve.wait_ge(row_max, b * PAIRS + p)
                        dve.wait_ge(bias_made[p % 2], b * 4 + (p // 2 + 1))
                    bank = ringV.take(dve)
                    held(dve)
                    ringV.empty(V.tensor_tensor_reduce(a_S[:, p % 2, lo:hi], ps[:, bank, 0:hi - lo],
                                                       a_bias[:, p % 2, lo:hi], 1.0, -3e38, ALU.add, ALU.max,
                                                       a_mx[:, j:j + 1]))
                    if j == 3:
                        own()
                        V.tensor_reduce(a_nm[:, p:p + 1], a_mx, AX_X, ALU.max, negate=True).then_inc(row_max, 1)

                def heads_out(b, p):
                    rd = a_rd[:, p:p + 1]
                    link(V.tensor_scalar(rd, a_rs[:, p:p + 1], 1.0, P_UP, ALU.add, ALU.mult))
                    link(V.reciprocal(rd, rd))
                    bank = ringV.take(dve)
                    at = 2 * HD * p
                    link(V.tensor_scalar(a_low, ps[:, bank, 2 * HD:4 * HD], rd, None, ALU.mult))
                    for h, rows_of in enumerate((slice(0, S), slice(S, P))):
                        ins = V.scalar_tensor_tensor(out=a_attn[:, b, at + HD * h:at + HD * (h + 1)],
                                                     in0=ps[rows_of, bank, HD * h:HD * (h + 1)], scalar=rd[rows_of],
                                                     in1=a_low[rows_of, HD * h:HD * (h + 1)], op0=ALU.mult, op1=ALU.add)
                    ringV.empty(ins)

                def head(b, first):
                    blocks = []
                    for r in range(4):
                        dst = [h[HD * r:HD * (r + 1), :, S * (r % 2):S * (r % 2 + 1)]
                               .rearrange("p (c k) n -> p k c n", k=2)[:, r // 2] for h in a_Qbd]
                        blocks.append((dst, a_QT[HD * r:HD * (r + 1), :, bass.ds(b * S, S)]))
                    for dst, src in blocks:
                        V.tensor_copy(dst[0], src).then_inc(qbd_made, 1)
                    dve.wait_ge(qbd_made, b * 8 + 4)
                    held(dve)
                    for dst, src in blocks:
                        V.tensor_tensor(dst[1], src, dst[0], ALU.subtract).then_inc(qbd_made, 1)
                    k_tiles(0, 4)
                    if not first:
                        turn_probs(6)
                        heads_out(b - 1, 5)
                    k_tiles(4, 8)
                    if not first:
                        turn_probs(7)
                        heads_out(b - 1, 6)
                    k_tiles(8, 12)
                    if not first:
                        heads_out(b - 1, 7)
                    k_tiles(12, 16)
                    for i in range(12):
                        lower(ringS, seenS, a_Vparts[:, i, :, 0, :], a_Vparts[:, i, :, 1, :],
                              lambda k: ps[:, k, :].rearrange("p (h n) -> p h n", h=PAIRS), 1 / W_UP)
                        if i < 8:
                            add_bias(b, i // 4, i % 4, first)
                    for q in range(4):
                        lower(ringV, takes, *(a_Vparts[0:LAST, KT_TILES - 1, 2 * q:2 * q + 2, k, :] for k in range(2)),
                              lambda k: ps[0:LAST, k, 0:P].rearrange("p (h n) -> p h n", h=2), 1 / W_UP)

                def pairs(b, first):
                    for p in range(6):
                        turn_probs(p)
                        if p:
                            heads_out(b, p - 1)
                        for j in range(4):
                            add_bias(b, p + 2, j, first)

                for c in range(C):
                    dve.wait_ge(ctx_hi, c + 1)
                    V.tensor_tensor(a_ctx[1][:, c, :], a_ctx0[:, c, :], a_ctx[0][:, c, :], ALU.subtract).then_inc(ctx_split, 1)
                dve.wait_ge(ringS.emptied, marks["q"])
                head(0, True)
                with dve.Fori(1, B, 1) as b:
                    with takes.loop(b, 1, B - 1, 60), chain.loop(b, 1, B - 1, 24), seenS.loop(b, 1, B - 1, 44), \
                            uppers.loop(b, 1, B - 1, 64):
                        pairs(b - 1, False)
                        head(b, False)
                pairs(B - 1, False)
                for p in (6, 7):
                    turn_probs(p)
                    heads_out(B - 1, p - 1)
                heads_out(B - 1, 7)
                for i in range(NT):
                    add_bank(x, i)
                chain.wait()

            def stage_b():
                norm(x, b_h1, begun="A" in stages)
                own_rows()
                norm(b_h1, h_tok)
                V.tensor_scalar(b_omk[:, 0:12], cols[:, COLS["mix_k"][0]:COLS["mix_k"][0] + 12], -1.0, 1.0, ALU.mult, ALU.add)
                link(V.tensor_scalar(b_omk[:, 12:20], cols[:, COLS["cmix_k"][0]:COLS["cmix_k"][0] + 8], -1.0, 1.0,
                                     ALU.mult, ALU.add))
                turned(b_xxT, "ln1")

                def mixes(first, dsts):
                    own()
                    for j, dst in enumerate(dsts):
                        for c in range(C):
                            halves_seen[0] += 1
                            dve.wait_ge(mix_half, halves_seen[0])
                            k = 4 * (first + j) + c
                            V.scalar_tensor_tensor(out=dst[:, c, S:], in0=b_xxT[:, c, 0:N - S], scalar=b_omk[:, k:k + 1],
                                                   in1=dst[:, c, S:], op0=ALU.mult, op1=ALU.add).then_inc(mix_made, 1)

                mixes(0, (b_mk, b_mv, b_mr))

                dve.wait_ge(wkv_exp, 1)
                link(V.tensor_scalar(b_w, b_w, -1.0, None, ALU.mult))
                first = col("first")

                def projected(name):
                    dve.wait_ge(ringS.emptied, marks["kvr"] + KVR_ORDER.index(name) + 1)

                def by_time(v):
                    return v.rearrange("p (s t) -> p s t", t=B)

                def exponents(c):
                    E1p, E2p, E1, E2, PN, PP, NUM, DEN = (b_wkv[c][:, k, :] for k in range(8))
                    k, w, u = b_k[:, c, :], b_w[:, c:c + 1], first[:, c:c + 1]
                    projected("k%d" % c)
                    if c >= 2:
                        projected(("k3", "r3")[c - 2])
                    link(V.tensor_scalar(DEN, k, 0.0, w, ALU.mult, ALU.add))
                    link(V.memset(by_time(DEN)[:, :, 0:1], -BIG))
                    chain.done(V.memset(by_time(PP)[:, :, 0:1], -BIG))
                    link(V.tensor_tensor_scan(PN, DEN, k, -BIG, ALU.add, ALU.max))
                    link(V.tensor_copy(by_time(PP)[:, :, 1:], by_time(PN)[:, :, 0:B - 1]))
                    chain.done(V.scalar_tensor_tensor(out=NUM, in0=k, scalar=u, in1=PP, op0=ALU.add, op1=ALU.max))
                    V.scalar_tensor_tensor(out=E1p, in0=PP, scalar=w, in1=PN, op0=ALU.add, op1=ALU.subtract)
                    V.tensor_tensor(E2p, k, PN, ALU.subtract)
                    chain.wait()
                    V.tensor_tensor(E1, PP, NUM, ALU.subtract)
                    V.scalar_tensor_tensor(out=E2, in0=k, scalar=u, in1=NUM, op0=ALU.add,
                                           op1=ALU.subtract).then_inc(wkv_arg, 1)

                def sums(c):
                    E1p, E2p, E1, E2, PN, PP, NUM, DEN = (b_wkv[c][:, k, :] for k in range(8))
                    v, rr = b_v[:, c, :], b_r[:, c, :]
                    dve.wait_ge(wkv_exp, c + 2)
                    projected("v%d" % c)
                    chain.done(V.tensor_tensor(PP, E2p, v, ALU.mult))
                    link(V.tensor_tensor_scan(DEN, E1p, E2p, 0.0, ALU.mult, ALU.add))
                    link(V.tensor_tensor_scan(PN, E1p, PP, 0.0, ALU.mult, ALU.add))
                    chain.done(V.tensor_tensor(NUM, E2, v, ALU.mult))
                    chain.done(V.tensor_tensor(by_time(E1p)[:, :, 1:], by_time(E1)[:, :, 1:], by_time(PN)[:, :, 0:B - 1], ALU.mult))
                    link(V.tensor_tensor(by_time(E2p)[:, :, 1:], by_time(E1)[:, :, 1:], by_time(DEN)[:, :, 0:B - 1], ALU.mult))
                    projected("r%d" % c)
                    chain.done(V.tensor_scalar(rr, rr, 1.0, None, ALU.add))
                    link(V.tensor_tensor(by_time(E2)[:, :, 1:], by_time(E2)[:, :, 1:], by_time(E2p)[:, :, 1:], ALU.add))
                    chain.done(V.tensor_tensor(by_time(NUM)[:, :, 1:], by_time(NUM)[:, :, 1:], by_time(E1p)[:, :, 1:], ALU.add))
                    link(V.tensor_tensor(E2, E2, rr, ALU.mult))
                    link(V.reciprocal(E2, E2))
                    V.tensor_tensor(b_k[:, c, :].rearrange("p (t s) -> p s t", t=B), by_time(NUM), by_time(E2),
                                    ALU.mult).then_inc(wkv_made, 1)

                for step, c in ((exponents, 0), (exponents, 1), (sums, 0), (sums, 1),
                                (exponents, 2), (exponents, 3), (sums, 2), (sums, 3)):
                    step(c)
                for i in range(NT):
                    add_bank(b_h1, i)
                norm(b_h1, h_tok, begun=True)
                turned(b_xxT, "ln2")
                mixes(3, (b_mk, b_mv))
                for f in range(16):
                    dve.wait_ge(ringS.emptied, marks["kk"] + f + 1)
                    V.tensor_tensor(b_kk[:, f, :], b_kk[:, f, :], b_kk[:, f, :], ALU.mult).then_inc(sq_made, 1)
                dve.wait_ge(ringS.emptied, marks["kk"] + 16 + NT)
                rr = b_rr
                link(V.tensor_scalar(flat(rr), flat(rr), 1.0, None, ALU.add))
                link(V.reciprocal(flat(rr), flat(rr)))
                for i in range(NT):
                    chain.done(V.tensor_tensor(x[:, i, :], x[:, i, :], b_h1[:, i, :], ALU.add))
                    bank = ringV.take(dve)
                    ringV.empty(V.tensor_tensor(rr[:, i, :], rr[:, i, :], ps[:, bank, :], ALU.mult))
                    own()
                    chain.wait()
                    link(V.tensor_tensor(x[:, i, :], x[:, i, :], rr[:, i, :], ALU.add))
                    chain.done(V.bn_stats(ln_st[:, 6 * i:6 * i + 6], x[:, i, :]))

            gates = [0]

            def route(bias):
                for i in range(NT):
                    bank = ringV.take(dve)
                    if bias:
                        ins = V.tensor_tensor(c_lg[:, i, :], ps[:, bank, 0:EXPERTS], row("gate_b", EXPERTS), ALU.add)
                    else:
                        ins = V.tensor_copy(c_lg[:, i, :], ps[:, bank, 0:EXPERTS])
                    ringV.empty(ins)
                own()
                for i in range(NT):
                    link(V.max(c_m8[:, i, :], c_lg[:, i, :]))
                    chain.done(V.max_index(c_ix[:, i, :].bitcast(U32), c_m8[:, i, :], c_lg[:, i, :]))
                chain.wait()
                V.tensor_scalar(c_nmx, c_m8[:, :, 0], -1.0, None, ALU.mult).then_inc(gate_arg, 1)
                link(V.tensor_copy(c_ixf, c_ix.bitcast(U32)))
                for k in range(2):
                    for i in range(NT):
                        ins = V.tensor_scalar(c_oh[:, k, i, :], col("iota"), c_ixf[:, i, k:k + 1], None, ALU.is_equal)
                    link(ins)
                gates[0] += 1
                dve.wait_ge(gate_exp, NT * gates[0])

            tiles_done = [0]

            def places(n_tiles, oh, which, expert_row, here=True):
                if here:
                    bank = ringV.take(dve)
                    ringV.empty(V.tensor_copy(flat(c_rk), ps[:, bank, 0:(NT + 1) * EXPERTS]))
                    own()
                count = c_rk[:, NT, :]
                link(V.tensor_scalar(c_tl, count, 0.0, None, ALU.is_gt))
                for full in range(1, NT):
                    link(V.scalar_tensor_tensor(out=c_tl, in0=count, scalar=float(P * full), in1=c_tl, op0=ALU.is_gt,
                                                op1=ALU.add))
                chain.done(V.memset(c_tst, 1.0))
                chain.wait()
                link(V.tensor_tensor_scan(c_tend, c_tst, c_tl, 0.0, ALU.mult, ALU.add))
                link(V.tensor_tensor(c_tst, c_tend, c_tl, ALU.subtract))
                link(V.tensor_scalar(c_tst, c_tst, float(P), None, ALU.mult))
                ranked = c_rk[:, 0:NT, :]
                link(V.tensor_tensor(ranked, ranked, c_tst.rearrange("p (o e) -> p o e", o=1).broadcast_to([P, NT, EXPERTS]),
                                     ALU.add))
                link(V.tensor_tensor(c_cmp[:, 0:n_tiles, :],
                                     c_tend.rearrange("p (o e) -> p o e", o=1).broadcast_to([P, n_tiles, EXPERTS]),
                                     c_j[:, 0:n_tiles].rearrange("p (j o) -> p j o", o=1).broadcast_to([P, n_tiles, EXPERTS]),
                                     ALU.is_le))
                link(V.tensor_reduce(c_te[:, expert_row, 0:n_tiles], c_cmp[:, 0:n_tiles, :], AX_X, ALU.add))
                V.tensor_scalar(c_te[:, expert_row, 0:n_tiles].bitcast(I32), c_te[:, expert_row, 0:n_tiles],
                                float(EXPERTS - 1), None, ALU.min).then_inc(tiles_known, 1)
                for k in which:
                    link(V.tensor_tensor(c_cmp[:, 0:NT, :], ranked, oh(k), ALU.mult))
                    link(V.tensor_reduce(c_slot[:, k, :], c_cmp[:, 0:NT, :], AX_X, ALU.add))
                    for i in range(NT):
                        ins = V.tensor_scalar(c_diag[:, i, :], ident, c_slot[:, k, i:i + 1], None, ALU.mult)
                    ins.then_inc(diag_made, 1)
                    if here:
                        bank = ringV.take(dve)
                        ringV.empty(V.tensor_copy(c_bc[:, k, :], ps[:, bank, :]))

            def split(src):
                link(V.tensor_copy(c_hi, src))
                V.tensor_tensor(c_lo, src, c_hi, ALU.subtract).then_inc(split_made, 1)

            def tiles(n_tiles, which, hidden, g0, weigh=None, ahead=None):
                t0 = tiles_done[0]

                def gather_matrix():
                    for i in range(NT):
                        ins = V.tensor_scalar(c_sel[:, i, :], c_iota, c_slot[:, which[0], i:i + 1], None, ALU.is_equal)
                    if len(which) == 2:
                        link(ins)
                        for i in range(NT):
                            ins = V.scalar_tensor_tensor(out=c_sel[:, i, :], in0=c_iota, scalar=c_slot[:, which[1], i:i + 1],
                                                         in1=c_sel[:, i, :], op0=ALU.is_equal, op1=ALU.add)
                    ins.then_inc(gather_made, 1)

                def step(j, parity, first=False, last=False, late=0):
                    if not last:
                        slots_now = c_slot[:, which[0]:which[-1] + 1, :]
                        dve.wait_ge(gather_made, j + (t0 + 1))
                        link(V.tensor_scalar(slots_now, slots_now, -float(P), None, ALU.add))
                        dve.wait_ge(ringS.emptied, (g0 + 1) if first else j * 4 + g0)
                        gather_matrix()
                    hidden(j, parity)
                    if not first:
                        dve.wait_ge(scattered, j + scattered0[0])
                    link(V.tensor_scalar(c_selT, c_bc[:, which[0], :], c_place, None, ALU.is_equal))
                    if len(which) == 2:
                        link(V.scalar_tensor_tensor(out=c_selT, in0=c_bc[:, 1, :], scalar=c_place, in1=c_selT,
                                                    op0=ALU.is_equal, op1=ALU.add))
                    if weigh:
                        weigh(j)
                    link(V.tensor_scalar(c_place, c_place, float(P), None, ALU.add))
                    dve.wait_ge(ringS.emptied, j * 4 + (g0 + (4 if last else 5) + late))
                    V.tensor_tensor(c_olo, flat(c_rows), c_ohi, ALU.subtract).then_inc(out_split, 1)

                link(V.tensor_copy(c_place, c_p))
                gather_matrix()
                per = chain.n
                step(0, 0, first=True)
                per = chain.n - per
                loops = (n_tiles - 3) // 2
                with dve.Fori(0, loops, 1) as it:
                    with chain.loop(it, 0, loops, 2 * per):
                        for m in range(2):
                            step(it * 2 + (1 + m), 1 - m)
                late = 2 if ahead else 0
                step(n_tiles - 2, 1, late=late)
                if ahead:
                    dve.wait_ge(ringS.emptied, (n_tiles - 2) * 4 + g0 + 3)
                    ahead()
                step(n_tiles - 1, 0, last=True, late=late)
                tiles_done[0] += n_tiles
                scattered0[0] += n_tiles - 1

            scattered0 = [0]

            def stage_c():
                norm(x, h_tok, begun="B" in stages)
                turned(hT)
                route(True)
                link(V.reciprocal(c_sum, c_sum))
                for k in range(2):
                    chain.done(V.tensor_tensor(c_w[:, 4 * k:4 * k + 4], c_e8[:, :, k], c_sum, ALU.mult))
                chain.wait()
                dve.wait_ge(stage_w_in, 16 * (2 + ("B" in stages)))
                V.drain().then_inc(oh_made, 1)
                bank = ringV.take(dve)
                ringV.empty(V.tensor_copy(c_ohT[0:EXPERTS], ps[0:EXPERTS, bank, :]))
                places(TILES_C, lambda m: c_oh[:, m], (0,), 0)
                split(h_tok)

                def lower_halves(j, parity):
                    t0 = tiles_done[0]
                    w = wbuf[:, (4 + t0 + parity) % 2, 4096:8192]
                    for m in range(2):
                        dve.wait_ge(w2_hi, j * 2 + (2 * t0 + m + 1))
                        held(dve)
                        cut = slice(2048 * m, 2048 * (m + 1))
                        V.scalar_tensor_tensor(out=flat(c_w2[1])[:, cut], in0=w[:, cut], scalar=W_UP,
                                               in1=flat(c_w2[0])[:, cut], op0=ALU.mult,
                                               op1=ALU.subtract).then_inc(w2_split, 1)
                    for m in range(2):
                        dve.wait_ge(hid_hi, j * 2 + (2 * t0 + m + 1))
                        held(dve)
                        cut = slice(4 * m, 4 * m + 4)
                        V.tensor_tensor(c_hid16[1][:, cut], c_hid[:, cut], c_hid16[0][:, cut],
                                        ALU.subtract).then_inc(hid_split, 1)

                for k in range(2):
                    tiles(TILES_C, (k,), lower_halves, marks["tiles"][k],
                          ahead=(lambda: places(TILES_C, lambda m: c_oh[:, m], (1,), 1, here=False)) if k == 0 else None)
                    prior = (h_tok, c_res)[k]
                    for i in range(NT):
                        bank = ringV.take(dve)
                        weight = c_w[:, 4 * k + i:4 * k + i + 1]
                        if k == 0:
                            V.scalar_tensor_tensor(out=c_acc[:, i, :], in0=ps[:, bank, :], scalar=0.5,
                                                   in1=h_tok[:, i, :], op0=ALU.mult, op1=ALU.add)
                        ringV.empty(V.scalar_tensor_tensor(out=c_res[:, i, :], in0=ps[:, bank, :], scalar=weight,
                                                           in1=prior[:, i, :], op0=ALU.mult, op1=ALU.add))
                    own()
                    if k == 0:
                        split(c_acc)
                moments(c_res)
                for i in range(NT):
                    V.scalar_tensor_tensor(out=c_acc[:, i, :], in0=c_res[:, i, :], scalar=ln_mv[:, i, 0:1],
                                           in1=row("gamma"), op0=ALU.subtract, op1=ALU.mult).then_inc(ln_rows, 1)
                own_rows()
                dve.wait_ge(shifted, NT)
                for i in range(NT):
                    ins = V.scalar_tensor_tensor(out=x[:, i, :], in0=c_acc[:, i, :], scalar=ln_rstd[:, i:i + 1],
                                                 in1=x[:, i, :], op0=ALU.mult, op1=ALU.add)
                link(ins)

            def stage_f():
                norm(x, h_tok, begun="E" in stages)
                turned(hT)
                route(False)
                link(V.tensor_tensor(c_sum, c_e8[:, :, 0], c_e8[:, :, 1], ALU.add))
                link(V.reciprocal(c_sum, c_sum))
                for k in range(2):
                    chain.done(V.tensor_tensor(c_w[:, 4 * k:4 * k + 4], c_e8[:, :, k], c_sum, ALU.mult))
                chain.wait()
                dve.wait_ge(stage_w_in, w_in_F)
                V.tensor_tensor(c_ohc, c_oh[:, 0], c_oh[:, 1], ALU.add).then_inc(oh_made, 1)
                places(TILES_F, lambda m: c_oh[:, m], (0, 1), 0)
                weights_of = flat(c_acc).rearrange("p (k n) -> p k n", k=4)[:, 0:2]
                picked = flat(c_res).rearrange("p (k n) -> p k n", k=4)[:, 0:2]
                for k in range(2):
                    for i in range(NT):
                        ins = V.tensor_scalar(c_diag[:, i, :], ident, c_w[:, 4 * k + i:4 * k + i + 1], None, ALU.mult)
                    ins.then_inc(diag_made, 1)
                    bank = ringV.take(dve)
                    ringV.empty(V.tensor_copy(weights_of[:, k, :], ps[:, bank, :]))
                split(h_tok)

                def hidden(j, parity):
                    dve.wait_ge(ringS.emptied, j * 4 + (marks["tiles"][-1] + 2))
                    link(V.tensor_scalar(flat(c_e), flat(c_e), 1.0, None, ALU.add))
                    link(V.reciprocal(flat(c_e), flat(c_e)))
                    link(V.tensor_tensor(flat(c_e), flat(c_e), flat(c_h1), ALU.mult))
                    dve.wait_ge(ringS.emptied, j * 4 + (marks["tiles"][-1] + 3))
                    held(dve)
                    V.tensor_tensor(c_hid[:, 0:4, :], c_e, c_h2, ALU.mult).then_inc(hid_made, 1)

                def weigh(j):
                    for k in range(2):
                        ins = V.scalar_tensor_tensor(out=picked[:, k, :], in0=c_bc[:, k, :], scalar=c_place,
                                                     in1=weights_of[:, k, :], op0=ALU.is_equal, op1=ALU.mult)
                    link(ins)
                    V.tensor_reduce(c_wcol[:, 0:1], flat(picked), AX_X, ALU.add).then_inc(wcol_made, 1)

                tiles(TILES_F, (0, 1), hidden, marks["tiles"][-1], weigh)
                for i in range(NT):
                    bank = ringV.take(dve)
                    ringV.empty(V.tensor_copy(x[:, i, :], ps[:, bank, :]))
                own()

            def stage_d():
                scale = float(D) ** -0.5
                V.tensor_scalar(d_nbg, col("bg"), -1.0, None, ALU.mult).then_inc(nbg_made, 1)
                norm(x, h_tok)
                link(V.memset(d_P2T, 0.0))
                V.memset(d_ones, 1.0).then_inc(d_vectors, 1)
                turned(hT)
                bank = ringV.take(dve)
                ringV.empty(V.tensor_copy(d_bqk, ps[0:1, bank, :]))
                for b in range(B):
                    bank = ringV.take(dve)
                    ringV.empty(V.tensor_copy(d_qbk[0:S, b:b + 1], ps[0:S, bank, 0:1]))
                for i in range(NT):
                    bank = ringV.take(dve)
                    ringV.empty(V.tensor_tensor(d_Vc[:, i, :], ps[:, bank, :], row("bv_c"), ALU.add))
                own()
                dve.wait_ge(ringS.emptied, marks["qk"])
                def latents(b):
                    V.tensor_copy(d_qk_b, d_qkT[:, :, bass.ds(b * S, S)]).then_inc(qkb_made, 1)
                    link(V.tensor_copy(d_qb1[0:S], d_qbk[0:S, bass.ds(b, 1)]))

                def scores(b):
                    for lo, hi in CHUNKS:
                        bank = ringV.take(dve)
                        ringV.empty(V.tensor_scalar(d_S[:, lo:hi], ps[0:S, bank, 0:hi - lo], d_qb1[0:S], scale,
                                                    ALU.add, ALU.mult))
                    own()
                    V.tensor_reduce(d_nm[0:S, 0:1], d_S, AX_X, ALU.max, negate=True).then_inc(row_max, 1)
                    if not isinstance(b, int):
                        dve.wait_ge(s2_made, b)
                        held(dve)
                    bank = ringV.take(dve)
                    ringV.empty(V.tensor_scalar(d_P2, ps[:, bank, 0:S], scale, None, ALU.mult))
                    own()
                    V.tensor_reduce(d_nm[:, 1:2], d_P2, AX_X, ALU.max, negate=True).then_inc(s2_arg, 1)
                    dve.wait_ge(s2_exp, b + 1)
                    link(V.reciprocal(d_rd[:, 1:2], d_rs[:, 1:2]))
                    V.tensor_scalar(d_P2_all[:, b, :], d_P2, d_rd[:, 1:2], None, ALU.mult).then_inc(s2_made, 1)

                def turn_probs():
                    for g in (1, 3):
                        bank = ringV.take(dve)
                        ringV.empty(V.tensor_copy(d_PT[:, 3 * g:3 * g + 3, :],
                                                  ps[:, bank, 0:3 * S].rearrange("p (j n) -> p j n", j=3)))

                def weighted_ctx(b):
                    bank = ringV.take(dve)
                    ringV.empty(V.tensor_scalar(d_pc[:, b, :], ps[0:S, bank, :], d_rd[0:S, 0:1], None, ALU.mult))

                latents(0)
                scores(0)
                link(V.reciprocal(d_rd[0:S, 0:1], d_rs[0:S, 0:1]))
                with dve.Fori(1, B, 1) as b:
                    with takes.loop(b, 1, B - 1, 8), chain.loop(b, 1, B - 1, 3):
                        latents(b)
                        turn_probs()
                        scores(b)
                        weighted_ctx(b - 1)
                        own()
                        link(V.reciprocal(d_rd[0:S, 0:1], d_rs[0:S, 0:1]))
                turn_probs()
                weighted_ctx(B - 1)
                def add_rows(c):
                    bank = ringV.take(dve)
                    part = x[:, :, P * c:P * (c + 1)]
                    ringV.empty(V.tensor_tensor(part, part, ps[:, bank, :].rearrange("p (t n) -> p t n", t=NT), ALU.add))

                dve.wait_ge(ringS.emptied, marks["gate"])
                diff = flat(d_ctxT)[:, 0:N]
                for c in range(C):
                    g = d_gate[:, c, :]
                    chain.done(V.tensor_tensor(diff, d_c2s[:, c, :], d_s2c[:, c, :], ALU.subtract))
                    dve.wait_ge(ringS.emptied, marks["gate"] + c + 1)
                    link(V.tensor_scalar(g, g, 1.0, None, ALU.add))
                    link(V.reciprocal(g, g))
                    link(V.tensor_tensor(g, g, diff, ALU.mult))
                    V.tensor_tensor(g, g, d_s2c[:, c, :], ALU.add).then_inc(gated_made, 1)
                    if c:
                        add_rows(c - 1)
                add_rows(C - 1)
                own()

            def stage_e():
                norm(x, h_tok)
                turned(hT)
                dve.wait_ge(neg_a, 1)
                V.tensor_scalar(e_negA, e_negA, -1.0, None, ALU.mult).then_inc(neg_a, 1)
                cw = col("conv_w")

                def inverse(c):
                    dve.wait_ge(conv_sum, c + 1)
                    V.reciprocal(e_de[:, c, :], e_de[:, c, :]).then_inc(conv_inv, 1)

                for c in range(8):
                    bank = ringV.take(dve)
                    v = ps[:, bank, :].rearrange("p (b s) -> p b s", b=B)
                    cv = e_dx[:, c, :].rearrange("p (b s) -> p b s", b=B)
                    dve.wait_ge(conv_tap, c + 1)
                    for d in (1, 2, 3):
                        w = cw[:, TAPS * (c + 1) - 1 - d:TAPS * (c + 1) - d]
                        ins = V.scalar_tensor_tensor(out=cv[:, :, d:], in0=v[:, :, 0:S - d], scalar=w, in1=cv[:, :, d:],
                                                     op0=ALU.mult, op1=ALU.add)
                        if d < 3:
                            link(ins)
                    ringV.empty(ins)
                    if c:
                        inverse(c - 1)
                inverse(7)
                dve.wait_ge(xv_made, 8)
                for c in range(8):
                    dve.wait_ge(ringS.emptied, marks["dt"] - 8 + c + 1)
                    z = e_de[:, c, :]
                    V.scalar_tensor_tensor(out=flat(e_dA)[:, N * c:N * (c + 1)], in0=z, scalar=-1.0, in1=z, op0=ALU.mult,
                                           op1=ALU.min).then_inc(dt_arg, 1)
                def softplus(c):
                    z, u = e_de[:, c, :], e_dx[:, c, :]
                    ln, q = (flat(v)[:, N * c:N * (c + 1)] for v in (e_h, e_hC))
                    dve.wait_ge(dt_exp, c + 1)
                    link(V.tensor_scalar(q, u, -0.25, 1 / 3, ALU.mult, ALU.add))
                    link(V.tensor_tensor(q, q, u, ALU.mult))
                    link(V.scalar_tensor_tensor(out=q, in0=q, scalar=-0.5, in1=u, op0=ALU.add, op1=ALU.mult))
                    link(V.scalar_tensor_tensor(out=q, in0=q, scalar=1.0, in1=u, op0=ALU.add, op1=ALU.mult))
                    chain.done(V.scalar_tensor_tensor(out=q, in0=u, scalar=1 / 64, in1=q, op0=ALU.is_lt, op1=ALU.mult))
                    dve.wait_ge(dt_ln, c + 1)
                    link(V.scalar_tensor_tensor(out=ln, in0=u, scalar=1 / 64, in1=ln, op0=ALU.is_ge, op1=ALU.mult))
                    link(V.tensor_tensor(ln, ln, q, ALU.add))
                    link(V.scalar_tensor_tensor(out=z, in0=z, scalar=0.0, in1=ln, op0=ALU.max, op1=ALU.add))
                    link(V.tensor_tensor(u, z, e_xv[:, c, :], ALU.mult))
                    V.memset(z.rearrange("p (b s) -> p b s", s=S)[:, :, 0:1], 1e28).then_inc(delta_made, 1)

                for c in range(8):
                    softplus(c)

                def y_rows(c):
                    dve.wait_ge(y_made, (NS // G) * (c + 1))
                    V.scalar_tensor_tensor(out=e_dx[:, c, :], in0=e_xv[:, c, :], scalar=col("D")[:, c:c + 1],
                                           in1=ps[:, c % 4, :], op0=ALU.mult, op1=ALU.add).then_inc(y_taken, 1)

                def weigh_states(k):
                    g = k % (NS // G)
                    dve.wait_ge(h_made, k + 1)
                    if k < NS // G:
                        dve.wait_ge(ringS.emptied, marks["dt"] + 2 * G * (k + 1))
                    if k >= 2:
                        dve.wait_ge(y_made, k - 1)
                    c_rows = e_C[g // 2][:, G * N * (g % 2):G * N * (g % 2 + 1)]
                    V.tensor_tensor(e_hC[:, g % 2, :], e_h[:, g % 2, :], c_rows, ALU.mult).then_inc(hc_made, 1)

                for c in range(8):
                    for g in range(NS // G):
                        k = c * (NS // G) + g
                        if k >= 2:
                            dve.wait_ge(hc_made, k - 1)
                        if c == 0:
                            dve.wait_ge(delta_made, 8)
                            dve.wait_ge(ringS.emptied, marks["dt"] + 2 * G * g + G)
                        h = e_h[:, g % 2, :]
                        dx = e_dx[:, c:c + 1, :].broadcast_to([P, G, N])
                        V.tensor_tensor(h.rearrange("p (n k) -> p n k", n=G), dx,
                                        e_B[:, G * N * g:G * N * (g + 1)].rearrange("p (n k) -> p n k", n=G),
                                        ALU.mult).then_inc(inputs_made, 1)
                        if k:
                            weigh_states(k - 1)
                        dve.wait_ge(inputs_made, k + 1)
                        dve.wait_ge(da_made, k + 1)
                        V.tensor_tensor_scan(h, e_dA[:, g % 2, :], h, 0.0, ALU.mult, ALU.add).then_inc(h_made, 1)
                        if g == 1 and c:
                            y_rows(c - 1)
                weigh_states(8 * NS // G - 1)
                V.drain().then_inc(brows_free, 1)
                y_rows(7)
                for i in range(NT):
                    dve.wait_ge(rows_summed, i + 1)
                    link(V.tensor_tensor(x[:, i, :], x[:, i, :], ps[:, 4 + i, :], ALU.add))
                    chain.done(V.bn_stats(ln_st[:, 6 * i:6 * i + 6], x[:, i, :]))
                chain.wait()

            for st, run in (("A", stage_a), ("B", stage_b), ("C", stage_c), ("D", stage_d), ("E", stage_e), ("F", stage_f)):
                if st in stages:
                    run()
            V.drain().then_inc(x_made, 1)

        @block.sync
        def _(sp):
            sp.dma_start(x[:], t["x"]).then_inc(in_x, 16)
            sp.dma_start(cols[:], t["cols"]).then_inc(in_consts, 16)
            sp.dma_start(rows[:], t["rows"].partition_broadcast(P)).then_inc(in_consts, 16)

            def load(n, src, per):
                for a in range(0, src.shape[1], per):
                    sp.dma_start(wbuf[:, n % 2, a:a + per], src[:, a:a + per]).then_inc(slot_in[n % 2], 16)

            def load_ctxT(dst, b):
                sp.dma_start(dst, t["ctxT"][b]).then_inc(ctx_in, 16)

            def tile_weights(n_tiles, first_slot, weights, width, row_of, g0):
                def one(j, k, free, early=True):
                    def part(a, b):
                        sp.dma_start(wbuf[:, k % 2, a:b],
                                     weights[bass.ds(e, 1), :, a:b].rearrange("o p n -> (o p) n")).then_inc(slot_in[k % 2], 16)

                    if early:
                        sp.wait_ge(ringS.filled, j * 4 + (g0 - 5))
                    else:
                        sp.wait_ge(slot_free, free)
                    e = sp.value_load(c_te[0:1, row_of, bass.ds(j, 1)].bitcast(I32), min_val=0, max_val=EXPERTS - 1)
                    part(0, 4096)
                    if early:
                        sp.wait_ge(slot_free, free)
                    part(4096, width)

                for j in range(3):
                    one(j, first_slot + j, first_slot + j - 1, early=(j == 2))
                with sp.Fori(0, (n_tiles - 3) // 2, 1) as it:
                    for m in range(2):
                        one(it * 2 + (3 + m), first_slot + 1 + m, it * 2 + (first_slot + 2 + m))

            if "A" in stages:
                def load_part(dst, k):
                    sp.dma_start(dst, t["wA"][:, 2048 * k:2048 * (k + 1)]).then_inc(slot_in[0], 16)

                load_part(flat(a_wq), 0)
                load_part(wbuf[:, 0, 2048:4096], 1)
                load_part(wbuf[:, 0, 4096:6144], 2)
                load_ctxT(a_ctx0, 0)
                def load_pos(b):
                    sp.dma_start(a_dist.bitcast(I32), t["kpos"][b].partition_broadcast(P)).then_inc(pos_in, 16)
                    for half in (0, S):
                        sp.dma_start(a_mask[half:half + S].bitcast(I32), t["mask"][b]).then_inc(pos_in, 16)
                    sp.dma_start(a_qpos.bitcast(I32), t["qpos"][b]).then_inc(pos_in, 16)

                def stage_chunk(b, c, free):
                    sp.wait_ge(ctx_split, free)
                    sp.dma_start(a_stage[c % 2], t["ctxT"][b, :, c]).then_inc(stage_in[c % 2], 16)

                load_pos(0)
                sp.wait_ge(w_split, 2)
                with sp.Fori(1, B, 1) as b:
                    for c in range(C):
                        stage_chunk(b, c, b * 4 + (c - 1))
                    for made in bias_made:
                        sp.wait_ge(made, b * 4)
                    load_pos(b)
                sp.wait_ge(kt_free, 1)
                load_part(flat(a_wo), 3)
            if "B" in stages:
                sp.wait_ge(kt_free, 1)
                load(1, t["wB1"], 2048)
                sp.wait_ge(slot_free, 1)
                load(2, t["wB2"], 2048)
                sp.wait_ge(ln_rows, NT * NORMS.index("B0") + 1)
                sp.dma_start(b_wcr, t["wcr"].rearrange("p (c n) -> p c n", c=C)).then_inc(stage_w_in, 16)
                sp.wait_ge(slot_free, 2)
                load(3, t["wB3"], 2048)
            if "C" in stages:
                sp.wait_ge(ln_rows, NT * NORMS.index("C") + 1)
                sp.dma_start(c_b2[0:EXPERTS], t["b2"]).then_inc(stage_w_in, 16)
                sp.dma_start(c_const, t["sel"]).then_inc(stage_w_in, 16)
                for k in range(2):
                    sp.wait_ge(tiles_known, k + 1)
                    tile_weights(TILES_C, 4 + TILES_C * k, t["wC"], SLOT, k, marks["tiles"][k])
            if "D" in stages:
                sp.wait_ge(slot_free, 25)
                load(26, t["wD1"], 2048)
                sp.wait_ge(slot_free, 26)
                load(27, t["wD2"], 2048)
                sp.wait_ge(ln_rows, NT * NORMS.index("D") + 1)
                v0 = marks["D loop start"]

                def load_keys(b, half_of):
                    lo, hi = CHUNKS[2 * half_of][0], CHUNKS[2 * half_of + 1][1]
                    sp.dma_start(d_ctxT[:, :, lo:hi], t["ctxT"][b, :, :, lo:hi]).then_inc(ctx_in, 16)

                def next_keys(b):
                    sp.wait_ge(picked, b)
                    for half_of in range(2):
                        sp.wait_ge(ringV.emptied, b * 8 + (v0 - 6 + 2 * half_of))
                        load_keys(b, half_of)

                def load_ctx(b):
                    full = (KT_TILES - 1) * P
                    sp.dma_start(d_ctx[:, 0:KT_TILES - 1, :],
                                 t["ctx"][b][0:full].rearrange("(k p) d -> p k d", p=P)).then_inc(ctxn_in, 16)
                    sp.dma_start(d_ctx[0:LAST, KT_TILES - 1, :], t["ctx"][b][full:S2]).then_inc(ctxn_in, 16)

                load_keys(0, 0)
                load_keys(0, 1)
                sp.wait_ge(slot_free, 27)
                load_ctx(0)
                next_keys(1)
                with sp.Fori(2, B, 1) as b:
                    next_keys(b)
                    sp.wait_ge(ringV.emptied, b * 8 + (v0 - 3))
                    load_ctx(b - 1)
                sp.wait_ge(ringV.emptied, v0 + 8 * (B - 1) + 5)
                load_ctx(B - 1)
                sp.wait_ge(ringV.emptied, marks["D loop end"])
            if "E" in stages:
                sp.wait_ge(slot_free, 27)
                load(28, t["wE"], 4096)
                sp.wait_ge(ln_rows, NT * NORMS.index("E") + 1)
                sp.dma_start(e_wx, t["wx"].rearrange("p (c n) -> p c n", c=8)).then_inc(stage_w_in, 16)
                sp.dma_start(e_wdt[0:RANK], t["wdt"]).then_inc(stage_w_in, 16)
            if "F" in stages:
                if "E" in stages:
                    sp.wait_ge(brows_free, 1)
                sp.wait_ge(ln_rows, NT * NORMS.index("F") + 1)
                sp.dma_start(c_const, t["sel"]).then_inc(stage_w_in, 16)
                sp.wait_ge(tiles_known, (2 if "C" in stages else 0) + 1)
                tile_weights(TILES_F, 29, t["wF"], 6144, 0, marks["tiles"][-1])
            sp.wait_ge(x_made, 1)
            sp.dma_start(t["out"], x[:]).then_inc(out_done, 16)
            sp.wait_ge(out_done, 16)



def by_partition(m):
    k, n = m.shape
    return np.ascontiguousarray(m.reshape(k // P, P, n).transpose(1, 0, 2).reshape(P, (k // P) * n))


def side_by_side(*parts):
    return np.concatenate(parts, axis=-1)


def layout(i):
    f = {k: np.asarray(v) for k, v in i.items()}
    L0x, L0a, L0f, L1x, L1a, L1f = "L0_xattn_", "L0_attn_", "L0_ffn_", "L1_xattn_", "L1_attn_", "L1_ffn_"
    f32 = np.float32

    def vec(v):
        return v.reshape(-1, P).T

    slopes = np.repeat(np.array([(2.0 ** (-8.0 / HEADS)) ** (h + 1) for h in range(HEADS)], f32).reshape(PAIRS, 2).T, S, axis=0)
    weight = ((1 + 2 * np.arange(S)) / 128).astype(f32)
    interp = np.concatenate([np.diag(1 - weight), np.diag(weight)]).astype(f32)
    packed = {
        "ln1_g": vec(f[L0a + "ln1_g"]), "ln1_b": vec(f[L0a + "ln1_b"]), "ln2_g": vec(f[L0a + "ln2_g"]),
        "ln2_b": vec(f[L0a + "ln2_b"]), "mix_k": vec(f[L0a + "time_mix_k"]), "mix_v": vec(f[L0a + "time_mix_v"]),
        "mix_r": vec(f[L0a + "time_mix_r"]), "decay": vec(f[L0a + "time_decay"]), "first": vec(f[L0a + "time_first"]),
        "cmix_k": vec(f[L0a + "cmix_k"]), "cmix_r": vec(f[L0a + "cmix_r"]),
        "bq_c": vec(f[L1x + "bq_c"]), "bk_s": vec(f[L1x + "bk_s"]), "bv_s": vec(f[L1x + "bv_s"]),
        "bq_s": vec(f[L1x + "bq_s"]), "bk_c": vec(f[L1x + "bk_c"]), "bg": vec(f[L1x + "bg"]),
        "conv_w": by_partition(f[L1a + "conv_w"].reshape(DI, TAPS)), "conv_b": vec(f[L1a + "conv_b"]),
        "b_dt": vec(f[L1a + "b_dt"]), "A_log": by_partition(f[L1a + "A_log"]), "D": vec(f[L1a + "D"]),
        "ident": np.eye(P, dtype=f32), "slopes": slopes, "interp": interp,
        "iota": np.tile(np.arange(EXPERTS, dtype=f32), (P, 1)),
        "gate_W": by_partition(f[L0f + "gate_W"]), "router": by_partition(f[L1f + "router_w"].T),
    }
    ctx = f["ctx_1024"]
    a, m = f["itok_BxS_8_8191"], f["itok_BxS2_1_8191"]
    experts = [side_by_side(by_partition(f[L0f + "W1"][e]), by_partition(f[L0f + "W2"][e]), vec(f[L0f + "b1"][e]))
               for e in range(EXPERTS)]
    return {
        "x": f["x"].reshape(NT, P, D).transpose(1, 0, 2),
        "cols": side_by_side(*[packed[n] for n in COLS]),
        "rows": side_by_side(f[L0f + "ln_gamma"], f[L0f + "ln_beta"], f[L1x + "bv_c"], f[L0f + "gate_b"]),
        "ctxT": ctx.transpose(0, 2, 1).reshape(B, C, P, S2).transpose(0, 2, 1, 3),
        "ctx": ctx,
        "mask": f["mask_BxSxS2_if1"],
        "qpos": np.concatenate([a, a], axis=1).reshape(B, P, 1),
        "kpos": m,
        "b2": f[L0f + "b2"],
        "sel": side_by_side(np.tile(np.arange(P), (P, 1)), np.triu(np.ones((P, P)), 1), np.ones((P, P)),
                            np.tile(np.arange(16), (P, 1)), np.arange(P)[:, None]).astype(f32),
        "wA": side_by_side(*[by_partition(f[L0x + n].T) for n in ("W_q", "W_k", "W_v", "W_o")]),
        "wB1": side_by_side(*[by_partition(f[L0a + n].T) for n in ("Wk", "Wv", "Wr", "Wo")]),
        "wB2": by_partition(f[L0a + "Wck"].T),
        "wB3": by_partition(f[L0a + "Wcv"].T),
        "wcr": by_partition(f[L0a + "Wcr"].T),
        "wC": np.stack(experts),
        "wD1": side_by_side(by_partition(f[L1x + "Wq_c"].T), by_partition(f[L1x + "Wk_s"]),
                            by_partition(f[L1x + "Wk_c"].T), by_partition(f[L1x + "Wq_s"])),
        "wD2": side_by_side(by_partition(f[L1x + "Wv_c"].T), by_partition(f[L1x + "Wv_s"].T),
                            by_partition(f[L1x + "Wg"].T)),
        "wE": side_by_side(by_partition(f[L1a + "W_in"]), by_partition(f[L1a + "W_out"])),
        "wx": by_partition(f[L1a + "W_x"]),
        "wdt": f[L1a + "W_dt"],
        "wF": np.stack([side_by_side(by_partition(f[L1f + "up_proj"][e]), by_partition(f[L1f + "down_proj"][e]))
                        for e in range(EXPERTS)]),
    }


def kernel(**inputs):
    import concourse.bacc as bacc
    from concourse.bass_utils import run_bass_kernel_spmd

    nc = bacc.Bacc("TRN2", target_bir_lowering=False, num_devices=1)
    arrays = {n: np.ascontiguousarray(v) for n, v in layout(inputs).items()}
    t = {n: nc.dram_tensor("in_" + n, v.shape, mybir.dt.from_np(v.dtype), kind="ExternalInput").ap() for n, v in arrays.items()}
    t["out"] = nc.dram_tensor("out", (P, NT, D), F32, kind="ExternalOutput").ap()
    perceiver_kernel(nc, t)
    r = run_bass_kernel_spmd(nc, [{"in_" + n: v for n, v in arrays.items()}], core_ids=[0])
    return np.asarray(r.results[0]["out"]).transpose(1, 0, 2).reshape(B, S, D)
```
